# Optimizing a Trainium2 kernel written in Bass

```python
import numpy as np
import jax
import jax.numpy as jnp

def _softmax(x, axis=-1):
    return jax.nn.softmax(x, axis=axis)

def _gelu(x):
    return jax.nn.gelu(x, approximate=True)

def _silu(x):
    return jax.nn.silu(x)

def _sigmoid(x):
    return jax.nn.sigmoid(x)

def _layernorm(x, axis=-1, eps=1e-05):
    m = jnp.mean(x, axis=axis, keepdims=True)
    v = jnp.var(x, axis=axis, keepdims=True)
    return (x - m) / jnp.sqrt(v + eps)

def _scatter_add(tgt, idx, src, axis=0):
    return tgt.at[idx].add(src)

def _segment_sum(src, seg, n):
    return jax.ops.segment_sum(src, seg, n)
kernel_name = 'mk_decoder_preln_d1_seqx_r8_183c75'

def setup_inputs(seed: int=0):
    np.random.seed(seed)
    _w = jnp.asarray

    def _rec_inputs():
        import jax
        import jax.numpy as jnp
        _rk = jax.random.key(seed)
        x = 0.0003765 + 1 * jax.random.normal(jax.random.fold_in(_rk, 1), (16, 128, 256), jnp.float32)
        _lenS = 128 - jax.random.randint(jax.random.fold_in(_rk, 7), (16,), 0, max(1, 128 // 4) + 1, jnp.int32)
        _lenS2 = 128 - jax.random.randint(jax.random.fold_in(_rk, 8), (16,), 0, max(1, 128 // 4) + 1, jnp.int32)
        _ctx_2048P = jax.random.normal(jax.random.fold_in(_rk, 11), (16, 16, 256), jnp.float32)
        _ctx_2048c = jax.random.dirichlet(jax.random.fold_in(_rk, 511), 0.3 * jnp.ones((16,), jnp.float32), (16, 128))
        _ctx_2048t = jnp.einsum('bsk,bkd->bsd', _ctx_2048c, _ctx_2048P)
        _ctx_2048t = _ctx_2048t * jax.lax.rsqrt(jnp.mean(jnp.square(_ctx_2048t)) + 1e-12) * 0.953939
        ctx_2048 = -0.000292821 + 1.00034 * (_ctx_2048t + 0.3 * jax.random.normal(jax.random.fold_in(_rk, 611), (16, 128, 256), jnp.float32))
        return (x, ctx_2048)
    x, ctx_2048 = _rec_inputs()

    def _L0_attn_setup():
        import jax, jax.numpy as jnp
        import numpy as np
        import math
        B, T, D_MODEL, N_HEADS, K_CONV = (2, 256, 256, 16, 4)
        HEAD_DIM = D_MODEL // N_HEADS
        EPS_GN = 1e-05

        def _group_norm(x2d, w, b, groups, eps):
            N, C = x2d.shape
            xg = x2d.reshape(N, groups, C // groups)
            mu = xg.mean(-1, keepdims=True)
            var = ((xg - mu) ** 2).mean(-1, keepdims=True)
            xn = ((xg - mu) * jax.lax.rsqrt(var + eps)).reshape(N, C)
            return xn * w + b

        def _causal_depthwise_conv(x, w, b):
            xt = jnp.transpose(x, (0, 2, 1))
            xp = jnp.pad(xt, ((0, 0), (0, 0), (K_CONV - 1, 0)))
            y = jax.lax.conv_general_dilated(xp, w[:, None, :], (1,), 'VALID', feature_group_count=D_MODEL, dimension_numbers=('NCH', 'OIH', 'NCH'))
            y = y + b[None, :, None]
            return jax.nn.silu(jnp.transpose(y, (0, 2, 1)))

        def _l2norm(t):
            n = jnp.sqrt(jnp.sum(t * t, axis=-1, keepdims=True))
            return t / jnp.maximum(n, 1e-12)

        def _reference_tuple_inner(x, Wq, Wk, Wv, Wo, conv_w, conv_b, Wig, b_ig, Wog, b_og, Wg, b_g, gn_w, gn_b, mn_w, mn_b):
            Bq, Tq, C = x.shape
            x_conv = _causal_depthwise_conv(x, conv_w, conv_b)
            q = _l2norm((x @ Wq.T).reshape(Bq, Tq, N_HEADS, HEAD_DIM))
            k = _l2norm((x @ Wk.T).reshape(Bq, Tq, N_HEADS, HEAD_DIM))
            v = (x @ Wv.T).reshape(Bq, Tq, N_HEADS, HEAD_DIM)
            input_gate = jax.nn.sigmoid(x_conv @ Wig.T + b_ig).reshape(Bq, Tq, N_HEADS, HEAD_DIM)
            gamma = jax.nn.sigmoid(x_conv @ Wg.T + b_g).reshape(Bq, Tq, N_HEADS, 1)
            bterm = input_gate * k * v
            aterm = jnp.broadcast_to(gamma, bterm.shape)

            def scan_op(c1, c2):
                a1, b1 = c1
                a2, b2 = c2
                return (a1 * a2, a2 * b1 + b2)
            _, mem = jax.lax.associative_scan(scan_op, (aterm, bterm), axis=1)
            next_rnn_state = mem[:, -1]
            mem_n = _group_norm(mem.reshape(Bq * Tq, D_MODEL), mn_w, mn_b, N_HEADS, EPS_GN)
            mem_n = mem_n.reshape(Bq, Tq, N_HEADS, HEAD_DIM)
            out = (mem_n * q).reshape(Bq * Tq, C)
            out = _group_norm(out, gn_w, gn_b, N_HEADS, EPS_GN).reshape(Bq, Tq, C)
            output_gate = jax.nn.sigmoid(x_conv @ Wog.T + b_og)
            out = out * output_gate @ Wo.T
            new_conv_cache = jnp.transpose(x, (0, 2, 1))[:, :, -(K_CONV - 1):]
            return (out, next_rnn_state, new_conv_cache)
        key = jax.random.key(seed)
        ks = jax.random.split(key, 16)
        s = 0.02
        min_d, max_d = (0.9, 0.9999)
        tgt = 1.0 - np.exp(np.linspace(math.log(1 - min_d), math.log(1 - max_d), N_HEADS))
        gamma_bias = np.log(tgt / (1 - tgt)).astype(np.float32)
        return {'x': jax.random.normal(ks[0], (B, T, D_MODEL), jnp.float32), 'Wq': jax.random.normal(ks[1], (D_MODEL, D_MODEL), jnp.float32) * s, 'Wk': jax.random.normal(ks[2], (D_MODEL, D_MODEL), jnp.float32) * s, 'Wv': jax.random.normal(ks[3], (D_MODEL, D_MODEL), jnp.float32) * s, 'Wo': jax.random.normal(ks[4], (D_MODEL, D_MODEL), jnp.float32) * s, 'conv_w': jax.random.normal(ks[5], (D_MODEL, K_CONV), jnp.float32) * 0.1, 'conv_b': jnp.zeros((D_MODEL,), jnp.float32), 'Wig': jax.random.normal(ks[6], (D_MODEL, D_MODEL), jnp.float32) * s, 'b_ig': jnp.zeros((D_MODEL,), jnp.float32), 'Wog': jax.random.normal(ks[7], (D_MODEL, D_MODEL), jnp.float32) * s, 'b_og': jnp.zeros((D_MODEL,), jnp.float32), 'Wg': jnp.zeros((N_HEADS, D_MODEL), jnp.float32), 'b_g': jnp.asarray(gamma_bias), 'gn_w': jnp.ones((D_MODEL,), jnp.float32), 'gn_b': jnp.zeros((D_MODEL,), jnp.float32), 'mn_w': jnp.ones((D_MODEL,), jnp.float32), 'mn_b': jnp.zeros((D_MODEL,), jnp.float32)}
    _L0_attn_all = _L0_attn_setup()
    _L0_attn_in = {k: v for k, v in _L0_attn_all.items() if k in ('Wq', 'Wk', 'Wv', 'Wo', 'conv_w', 'conv_b', 'Wig', 'b_ig', 'Wog', 'b_og', 'Wg', 'b_g', 'gn_w', 'gn_b', 'mn_w', 'mn_b')}
    del _L0_attn_all

    def _L0_xattn_setup():
        import jax, jax.numpy as jnp
        import numpy as np
        key = jax.random.key(seed)
        k1, k2, k3, k4, k5 = jax.random.split(key, 5)
        B, D_MODEL, L = (2, 128, 256)
        HEAD_DIM = 8
        H = D_MODEL // HEAD_DIM
        return {'k': jax.random.normal(k1, (B, D_MODEL, L), dtype=jnp.float32), 'v': jax.random.normal(k2, (B, D_MODEL, L), dtype=jnp.float32), 'q': jax.random.normal(k3, (B, D_MODEL, L), dtype=jnp.float32), 'ssm_kernel': jax.random.normal(k4, (H, L), dtype=jnp.float32), 'D': jax.random.normal(k5, (H,), dtype=jnp.float32), 'head_dim': HEAD_DIM}
    _L0_xattn_all = _L0_xattn_setup()
    _L0_xattn_in = {k: v for k, v in _L0_xattn_all.items() if k in ('ssm_kernel', 'D')}
    del _L0_xattn_all

    def _L0_ffn_setup():
        import jax, jax.numpy as jnp
        import numpy as np
        NUM_EXPERTS = 32
        TOP_K = 4
        key = jax.random.key(seed)
        k0, k1, k2, k3, k4 = jax.random.split(key, 5)
        B, S, H, I = (4, 256, 256, 128)
        sh = 1.0 / np.sqrt(H).astype(np.float32)
        si = 1.0 / np.sqrt(I).astype(np.float32)
        return {'hidden_states': jax.random.normal(k0, (B, S, H), jnp.float32), 'router_w': jax.random.normal(k1, (NUM_EXPERTS, H), jnp.float32) * sh, 'w_gate': jax.random.normal(k2, (NUM_EXPERTS, I, H), jnp.float32) * sh, 'w_up': jax.random.normal(k3, (NUM_EXPERTS, I, H), jnp.float32) * sh, 'w_down': jax.random.normal(k4, (NUM_EXPERTS, H, I), jnp.float32) * si}
    _L0_ffn_all = _L0_ffn_setup()
    _L0_ffn_in = {k: v for k, v in _L0_ffn_all.items() if k in ('router_w', 'w_gate', 'w_up', 'w_down')}
    del _L0_ffn_all
    return {'x': x, 'ctx_2048': ctx_2048, 'L0_attn_Wq': _L0_attn_in['Wq'], 'L0_attn_Wk': _L0_attn_in['Wk'], 'L0_attn_Wv': _L0_attn_in['Wv'], 'L0_attn_Wo': _L0_attn_in['Wo'], 'L0_attn_conv_w': _L0_attn_in['conv_w'], 'L0_attn_conv_b': _L0_attn_in['conv_b'], 'L0_attn_Wig': _L0_attn_in['Wig'], 'L0_attn_b_ig': _L0_attn_in['b_ig'], 'L0_attn_Wog': _L0_attn_in['Wog'], 'L0_attn_b_og': _L0_attn_in['b_og'], 'L0_attn_Wg': _L0_attn_in['Wg'], 'L0_attn_b_g': _L0_attn_in['b_g'], 'L0_attn_gn_w': _L0_attn_in['gn_w'], 'L0_attn_gn_b': _L0_attn_in['gn_b'], 'L0_attn_mn_w': _L0_attn_in['mn_w'], 'L0_attn_mn_b': _L0_attn_in['mn_b'], 'L0_xattn_ssm_kernel': _L0_xattn_in['ssm_kernel'], 'L0_xattn_D': _L0_xattn_in['D'], 'L0_ffn_router_w': _L0_ffn_in['router_w'], 'L0_ffn_w_gate': _L0_ffn_in['w_gate'], 'L0_ffn_w_up': _L0_ffn_in['w_up'], 'L0_ffn_w_down': _L0_ffn_in['w_down']}

def reference(x, ctx_2048, L0_attn_Wq, L0_attn_Wk, L0_attn_Wv, L0_attn_Wo, L0_attn_conv_w, L0_attn_conv_b, L0_attn_Wig, L0_attn_b_ig, L0_attn_Wog, L0_attn_b_og, L0_attn_Wg, L0_attn_b_g, L0_attn_gn_w, L0_attn_gn_b, L0_attn_mn_w, L0_attn_mn_b, L0_xattn_ssm_kernel, L0_xattn_D, L0_ffn_router_w, L0_ffn_w_gate, L0_ffn_w_up, L0_ffn_w_down):
    import jax
    import jax.numpy as jnp

    def _L0_attn_ref(x, Wq, Wk, Wv, Wo, conv_w, conv_b, Wig, b_ig, Wog, b_og, Wg, b_g, gn_w, gn_b, mn_w, mn_b):
        import jax, jax.numpy as jnp
        import numpy as np
        import math
        B, T, D_MODEL, N_HEADS, K_CONV = (2, 256, 256, 16, 4)
        HEAD_DIM = D_MODEL // N_HEADS
        EPS_GN = 1e-05

        def _group_norm(x2d, w, b, groups, eps):
            N, C = x2d.shape
            xg = x2d.reshape(N, groups, C // groups)
            mu = xg.mean(-1, keepdims=True)
            var = ((xg - mu) ** 2).mean(-1, keepdims=True)
            xn = ((xg - mu) * jax.lax.rsqrt(var + eps)).reshape(N, C)
            return xn * w + b

        def _causal_depthwise_conv(x, w, b):
            xt = jnp.transpose(x, (0, 2, 1))
            xp = jnp.pad(xt, ((0, 0), (0, 0), (K_CONV - 1, 0)))
            y = jax.lax.conv_general_dilated(xp, w[:, None, :], (1,), 'VALID', feature_group_count=D_MODEL, dimension_numbers=('NCH', 'OIH', 'NCH'))
            y = y + b[None, :, None]
            return jax.nn.silu(jnp.transpose(y, (0, 2, 1)))

        def _l2norm(t):
            n = jnp.sqrt(jnp.sum(t * t, axis=-1, keepdims=True))
            return t / jnp.maximum(n, 1e-12)

        def _reference_tuple_inner(x, Wq, Wk, Wv, Wo, conv_w, conv_b, Wig, b_ig, Wog, b_og, Wg, b_g, gn_w, gn_b, mn_w, mn_b):
            Bq, Tq, C = x.shape
            x_conv = _causal_depthwise_conv(x, conv_w, conv_b)
            q = _l2norm((x @ Wq.T).reshape(Bq, Tq, N_HEADS, HEAD_DIM))
            k = _l2norm((x @ Wk.T).reshape(Bq, Tq, N_HEADS, HEAD_DIM))
            v = (x @ Wv.T).reshape(Bq, Tq, N_HEADS, HEAD_DIM)
            input_gate = jax.nn.sigmoid(x_conv @ Wig.T + b_ig).reshape(Bq, Tq, N_HEADS, HEAD_DIM)
            gamma = jax.nn.sigmoid(x_conv @ Wg.T + b_g).reshape(Bq, Tq, N_HEADS, 1)
            bterm = input_gate * k * v
            aterm = jnp.broadcast_to(gamma, bterm.shape)

            def scan_op(c1, c2):
                a1, b1 = c1
                a2, b2 = c2
                return (a1 * a2, a2 * b1 + b2)
            _, mem = jax.lax.associative_scan(scan_op, (aterm, bterm), axis=1)
            next_rnn_state = mem[:, -1]
            mem_n = _group_norm(mem.reshape(Bq * Tq, D_MODEL), mn_w, mn_b, N_HEADS, EPS_GN)
            mem_n = mem_n.reshape(Bq, Tq, N_HEADS, HEAD_DIM)
            out = (mem_n * q).reshape(Bq * Tq, C)
            out = _group_norm(out, gn_w, gn_b, N_HEADS, EPS_GN).reshape(Bq, Tq, C)
            output_gate = jax.nn.sigmoid(x_conv @ Wog.T + b_og)
            out = out * output_gate @ Wo.T
            new_conv_cache = jnp.transpose(x, (0, 2, 1))[:, :, -(K_CONV - 1):]
            return (out, next_rnn_state, new_conv_cache)
        return _reference_tuple_inner(x, Wq, Wk, Wv, Wo, conv_w, conv_b, Wig, b_ig, Wog, b_og, Wg, b_g, gn_w, gn_b, mn_w, mn_b)[0]

    def _L0_xattn_ref(k, v, q, ssm_kernel, D, head_dim):
        import jax, jax.numpy as jnp
        import numpy as np
        B, HD, L = k.shape
        H = HD // head_dim
        fft_size = 2 * L
        k_ = k.reshape(B, H, head_dim, L)
        v_ = v.reshape(B, H, head_dim, L)
        q_ = q.reshape(B, H, head_dim, L)
        kv = jnp.einsum('bhil,bhjl->bijhl', k_, v_)
        kv_f = jnp.fft.rfft(kv, n=fft_size)
        kernel_f = jnp.fft.rfft(ssm_kernel, n=fft_size)
        y = jnp.fft.irfft(kv_f * kernel_f, n=fft_size)[..., :L]
        out = y + kv * D[None, None, None, :, None]
        out = jnp.einsum('bijhl,bhil->bjhl', out, q_)
        out = jnp.transpose(out, (0, 2, 1, 3)).reshape(B, H * head_dim, L)
        return out.astype(k.dtype)

    def _L0_ffn_ref(hidden_states, router_w, w_gate, w_up, w_down):
        import jax, jax.numpy as jnp
        import numpy as np
        NUM_EXPERTS = 32
        TOP_K = 4
        B, S, H = hidden_states.shape
        x = hidden_states.reshape(-1, H)
        T = x.shape[0]
        logits = x @ router_w.T
        probs = jax.nn.softmax(logits.astype(jnp.float32), axis=-1)
        top_w, top_i = jax.lax.top_k(probs, TOP_K)
        top_w = top_w / jnp.sum(top_w, axis=-1, keepdims=True)
        top_w = top_w.astype(x.dtype)
        comb = jnp.zeros((T, NUM_EXPERTS), x.dtype).at[jnp.arange(T)[:, None], top_i].add(top_w)

        def body(acc, ws):
            wg, wu, wd, c = ws
            h = jax.nn.silu(x @ wg.T) * (x @ wu.T) @ wd.T
            return (acc + h * c[:, None], None)
        out, _ = jax.lax.scan(body, jnp.zeros_like(x), (w_gate, w_up, w_down, comb.T))
        return out.reshape(B, S, H)
    x = x + _L0_attn_ref(_layernorm(x, axis=-1), L0_attn_Wq, L0_attn_Wk, L0_attn_Wv, L0_attn_Wo, L0_attn_conv_w, L0_attn_conv_b, L0_attn_Wig, L0_attn_b_ig, L0_attn_Wog, L0_attn_b_og, L0_attn_Wg, L0_attn_b_g, L0_attn_gn_w, L0_attn_gn_b, L0_attn_mn_w, L0_attn_mn_b)
    x = x + _L0_xattn_ref(ctx_2048, ctx_2048, _layernorm(x, axis=-1), L0_xattn_ssm_kernel, L0_xattn_D, 8)
    x = x + _L0_ffn_ref(_layernorm(x, axis=-1), L0_ffn_router_w, L0_ffn_w_gate, L0_ffn_w_up, L0_ffn_w_down)
    return x

_drawn_inputs = setup_inputs


def setup_inputs(seed=0):
    import zlib

    import numpy as np

    out = dict(_drawn_inputs(seed))
    spreads = {'L0_attn_conv_b': (0.0, 0.8),
     'L0_attn_b_ig': (0.0, 0.8),
     'L0_attn_b_og': (0.0, 0.8),
     'L0_attn_Wg': (0.0, 0.8),
     'L0_attn_gn_w': (1.0, 0.2),
     'L0_attn_gn_b': (0.0, 0.306),
     'L0_attn_mn_w': (1.0, 0.6),
     'L0_attn_mn_b': (0.0, 0.481)}
    factors = {'L0_attn_conv_w': 8.0,
     'L0_attn_Wig': 8.0,
     'L0_attn_Wog': 8.0,
     'L0_ffn_router_w': 6.945,
     'L0_ffn_w_gate': 6.96,
     'L0_ffn_w_up': 6.533,
     'L0_ffn_w_down': 6.529}
    for name, (base, spread) in spreads.items():
        noise = np.random.default_rng([zlib.crc32(name.encode()), seed]).standard_normal(out[name].shape)
        drawn = base * np.exp(spread * noise) if base else spread * noise
        out[name] = jnp.asarray(drawn.astype(out[name].dtype))
    for name, factor in factors.items():
        out[name] = (out[name] * factor).astype(out[name].dtype)
    return out
```

```python
from contextlib import ExitStack

import concourse.bass as bass
from concourse import mybir

ALU = mybir.AluOpType
ACT = mybir.ActivationFunctionType
AX = mybir.AxisListType
F32 = mybir.dt.float32
BF16 = mybir.dt.bfloat16
I32 = mybir.dt.int32
U32 = mybir.dt.uint32

B, T, C = 16, 128, 256
P = 128
NC = C // P
NTOK = B * T
HEADS, HD = 16, 16
KC = 4
XH, XD = 16, 8
NPAIR = XD * (XD + 1) // 2
G = 4
NG = B // G
GT = G * T
E, TOPK, INNER = 32, 4, 128
NSLOT = NTOK * TOPK
NTILE = (NSLOT + E * (P - 1)) // P + 1
NTILE += -NTILE % 4
ELOW = 2
GUW = NC * 2 * INNER
LN_EPS = 1e-5
NHOT = 8
AHEAD = 2
NZ = 4
RT_SEL, RT_STEPS = 20, 29
PLAN_DONE = 21
FAR = 1 << 14


class Signal:

    def __init__(self, sem, per):
        self.sem, self.per = sem, per

    def now(self, g, k=None):
        return (g + 1) * self.per + (self.per if k is None else k)

    def before(self, g, k=None):
        return g * self.per + (self.per if k is None else k)


def pair_offset(s):
    return s * XD - s * (s - 1) // 2


def program(nc, x, ctx_t, w_qk, w_v, w_ig, w_g, w_og, w_o, w_rt, cols, rows, toep, dskip,
            w_gu, w_dn, consts, iotas, out):
    with ExitStack() as stack:
        def sb(name, shape, dt=F32):
            return stack.enter_context(nc.sbuf_tensor(name, shape, dt))

        def sem(name):
            return stack.enter_context(nc.semaphore(name))

        def signal(name, per):
            return Signal(sem(name), per)

        hn_dram = nc.dram_tensor("hn_scratch", [NTOK, C], F32, kind="Internal").ap()
        z_dram = nc.dram_tensor("z_scratch", [NSLOT, C], F32, kind="Internal").ap()

        X2 = sb("X2", [P, B, C])
        WQK = sb("WQK", [P, NC, 2 * C])
        WV = sb("WV", [P, NC, C])
        WIG = sb("WIG", [P, NC, C])
        WG = sb("WG", [P, NC, C])
        WOG = sb("WOG", [P, NC, C])
        WO = sb("WO", [P, NC, C])
        WRT = sb("WRT", [P, NC, E])
        COLS = sb("COLS", [P, NC, 10])
        ROWS = sb("ROWS", [P, 2, C])
        TOEP = sb("TOEP", [P, XH, C])
        DSK = sb("DSK", [P, XH])
        CST = sb("CST", [P, 3, P])
        IOT = sb("IOT", [P, 4, P])
        TRI = sb("TRI", [P, 2, P], BF16)
        WDN = sb("WDN", [P, E, C])
        WGU = sb("WGU", [P, E * GUW])
        at = [ELOW * GUW]

        def high(*shape):
            n = 1
            for s in shape:
                n *= s
            v = WGU[:, at[0]:at[0] + n]
            at[0] += n
            return v

        prod_f = high(G * XH * XD * XD)
        prod = prod_f.rearrange("p (q n) -> p q n", n=XD * XD)
        kvp_f = high(NC * G * XH * NPAIR)
        kvp = kvp_f.rearrange("p (q n) -> p q n", n=NPAIR)
        kvp_h = kvp_f.rearrange("p (c b h n) -> p c b h n", c=NC, b=G, h=XH)
        xnT = high(NC * G * (T + KC - 1)).rearrange("p (c b t) -> p c b t", c=NC, b=G)
        ig = high(NC * GT).rearrange("p (c t) -> p c t", c=NC)
        gam = high(NC * GT).rearrange("p (c t) -> p c t", c=NC)
        ctx_f = sb("ctx_f", [P, NC * G * XH * XD])
        ctxm = ctx_f[:, :].rearrange("p (q i) -> p q i", i=XD)
        YB = sb("YB", [P, NC * G * XH * NPAIR])
        yq = YB[:, :].rearrange("p (q n) -> p q n", n=NPAIR)
        yh = YB[:, :].rearrange("p (c b h n) -> p c b h n", c=NC, b=G, h=XH)

        def buf(name, shared=False):
            t = high(G * C) if shared else sb(name, [P, G * C])
            return t, t[:, :].rearrange("p (b c) -> p b c", b=G), t[:, :].rearrange("p (c t) -> p c t", c=NC)

        xn_f, xn, _ = buf("xn")
        y_f, _, y = buf("y")
        s_f, _, s_ = buf("sg", True)
        v_f, v, vC = buf("v")
        kv_f, kv, kvC = buf("kv", True)
        qn_f, qn, _ = buf("qn")
        bt_f, bt, btC = buf("bt", True)
        o_f, o, oC = buf("o")

        def per_head(f):
            return f.rearrange("p (r d) -> p r d", d=HD)

        st = sb("st", [P, G, 6])
        mv = sb("mv", [P, G, 2])
        rs = sb("rs", [P, G])
        rstd = sb("rstd", [P, G])
        nmean = sb("nmean", [P, G])
        nmr = sb("nmr", [P, G])
        half = sb("half", [P, P])
        ss = sb("ss", [P, 2 * G * HEADS])
        rqk = sb("rqk", [P, 2 * G * HEADS])
        s2 = sb("s2", [P, G * HEADS])
        r2 = sb("r2", [P, G * HEADS])
        mu = sb("mu", [P, G * HEADS])
        s3 = sb("s3", [P, G * HEADS])
        r3 = sb("r3", [P, G * HEADS])
        lmax = sb("lmax", [P, G])
        lg = sb("lg", [P, G, E])
        pe_ = sb("pe_", [P, G, E])
        psm = sb("psm", [P, 2, G])
        pr = sb("pr", [P, G, E])
        m8 = sb("m8", [P, G, 8])
        ix = sb("ix", [P, G, 8], U32)
        ixf = sb("ixf", [P, G, TOPK])
        wsum = sb("wsum", [P, 2, G])
        WT = sb("WT", [P, B, TOPK])
        OH = sb("OH", [P, B, TOPK * E], BF16)
        sel = sb("sel", [P, G, E], BF16)
        cum = sb("cum", [P, G + 1, E], BF16)
        posr = sb("posr", [P, B, TOPK])
        tmp_oh = sb("tmp_oh", [P, G * TOPK * E])
        big = TOEP[:, :, :].rearrange("p h l -> p (h l)")
        oh_prod = big[:, 0:B * TOPK * E].rearrange("p (q e) -> p q e", e=E)
        lo_hot = [big[:, 2048 + i * P:2048 + (i + 1) * P] for i in range(NHOT)]
        hi_hot = [big[:, 3072 + i * NTILE:3072 + (i + 1) * NTILE] for i in range(NHOT)]
        posf = sb("posf", [P, B * TOPK])
        posi = sb("posi", [P, 3, B * TOPK], I32)
        pos2 = sb("pos2", [P, 2, B * TOPK])
        ntf = sb("ntf", [E, 1])
        nti = sb("nti", [E, 2], I32)
        ntb = sb("ntb", [E, P])
        endt = sb("endt", [E, 1])
        over = sb("over", [E, NTILE])
        etile = sb("etile", [1, NTILE], I32)
        start = sb("start", [P, E])
        idx_t = sb("idx_t", [P, 3, NTILE])
        SIDX = sb("SIDX", [P, NTILE], I32)
        GIDX = sb("GIDX", [P, 2, NTILE], I32)
        NB = 4
        gcol = sb("gcol", [P, NB], U32)
        scol = sb("scol", [P, NB], U32)

        def ybuf(k):
            return YB[:, k * C:(k + 1) * C]

        xg = [ybuf(i) for i in range(NB)]
        xgT = [ybuf(NB + i) for i in range(2)]
        res = [ybuf(NB + 2 + i) for i in range(NB)]
        act_g = [ybuf(2 * NB + 2)[:, i * P:(i + 1) * P] for i in range(2)]
        hid = [ybuf(2 * NB + 3)[:, i * P:(i + 1) * P] for i in range(2)]
        hidT = [ybuf(2 * NB + 4)[:, i * P:(i + 1) * P] for i in range(2)]

        pA, pB, pC = (stack.enter_context(nc.psum_tensor(n, [P, 1024], F32)) for n in ("pA", "pB", "pC"))
        pY = stack.enter_context(nc.psum_tensor("pY", [P, 2, 512], F32))

        WGU_E = WGU[:, :].rearrange("p (q n) -> p q n", n=2 * INNER)
        z_buf = [prod_f[:, i * TOPK * C:(i + 1) * TOPK * C] for i in range(NZ)]

        def tok(p):
            return p[:, :].rearrange("p (b c) -> p b c", b=G)

        def chan(p):
            return p[:, :].rearrange("p (c t) -> p c t", c=NC)

        ident = CST[:, 0, :]
        center = CST[:, 1, :]
        onesf = CST[:, 2, :]
        iota = IOT[:, 0, :]
        rownum = IOT[:, 1, 0:B * TOPK]
        tri_lt = IOT[0:E, 2, 0:E]
        tri_le = IOT[0:E, 2, E:2 * E]
        CONVB, BIG, BG, BOG, GNW, GNB = range(KC, KC + 6)

        consts_in = sem("consts_in")
        half_set = sem("half_set")
        toep_ready = sem("toep_ready")
        x_in = signal("x_in", 16)
        ctx_in = signal("ctx_in", 16)
        stats = signal("stats", 3 * G)
        aggr1 = signal("aggr1", G)
        aggr2 = signal("aggr2", G)
        aggr3 = signal("aggr3", G)
        rstd_step = signal("rstd_step", 12)
        xn_ready = signal("xn_ready", 1)
        xn_tr = signal("xn_tr", 1)
        xnT_ready = signal("xnT_ready", 2)
        tap0 = signal("tap0", 2)
        conv = signal("conv", 6)
        sig_y = signal("sig_y", 1)
        xc_ready = signal("xc_ready", 1)
        v_mm = signal("v_mm", 1)
        k_mm = signal("k_mm", 1)
        q_mm = signal("q_mm", 1)
        v_out = signal("v_out", 1)
        ksq = signal("ksq", 1)
        qsq = signal("qsq", 1)
        ssum = signal("ssum", 2)
        ssmax = signal("ssmax", 1)
        rqk_ready = signal("rqk_ready", 1)
        kv_step = signal("kv_step", 1)
        kv_ready = signal("kv_ready", 1)
        qn_ready = signal("qn_ready", 1)
        qw_ready = signal("qw_ready", 1)
        qb_ready = signal("qb_ready", 1)
        ig_mm = signal("ig_mm", 1)
        gam_mm = signal("gam_mm", 1)
        ig_ready = signal("ig_ready", 2)
        gam_out = signal("gam_out", 2)
        gam_ready = signal("gam_ready", 1)
        kv_tr = signal("kv_tr", 1)
        bt_ready = signal("bt_ready", 1)
        mem_ready = signal("mem_ready", 2)
        og_mm = signal("og_mm", 1)
        og_ready = signal("og_ready", 2)
        mem_tr = signal("mem_tr", 1)
        memsq = signal("memsq", 1)
        memvar = signal("memvar", 1)
        r2_step = signal("r2_step", 2)
        o_step = signal("o_step", 7)
        osq = signal("osq", 1)
        ovar = signal("ovar", 1)
        r3_step = signal("r3_step", 2)
        o_tr = signal("o_tr", 1)
        oT_out = signal("oT_out", 2)
        oT_ready = signal("oT_ready", 1)
        wo_mm = signal("wo_mm", 1)
        x1_ready = signal("x1_ready", 1)
        q2_ready = signal("q2_ready", 1)
        q2_tr = signal("q2_tr", 1)
        q2T_ready = signal("q2T_ready", 1)
        pairs = signal("pairs", XD)
        y_mm = signal("y_mm", XH)
        y_out = signal("y_out", XH)
        prods = signal("prods", 2 * 15)
        redd = signal("redd", 2)
        y2_tr = signal("y2_tr", 1)
        x2_ready = signal("x2_ready", 1)
        h_ready = signal("h_ready", 1)
        hn_stored = signal("hn_stored", 16)
        h_tr = signal("h_tr", 1)
        hT_ready = signal("hT_ready", 1)
        lg_mm = signal("lg_mm", 1)
        rt = signal("rt", RT_STEPS)
        ex_ready = signal("ex_ready", 1)
        rank_mm = signal("rank_mm", 1)
        gu_in = sem("gu_in")
        high_in = sem("high_in")
        cnt_mm = sem("cnt_mm")
        plan = sem("plan")
        start_mm = sem("start_mm")
        etile_mm = sem("etile_mm")
        lo_ready = sem("lo_ready")
        hi_ready = sem("hi_ready")
        id_mm = sem("id_mm")
        gcol_ready = sem("gcol_ready")
        scol_ready = sem("scol_ready")
        pos_ready = sem("pos_ready")
        gathered = [sem(f"gathered{i}") for i in range(NB)]
        scattered = [sem(f"scattered{i}") for i in range(NB)]
        xg_tr = sem("xg_tr")
        xgT_ready = sem("xgT_ready")
        gu_mm = sem("gu_mm")
        silu_ready = sem("silu_ready")
        hid_ready = sem("hid_ready")
        hid_tr = sem("hid_tr")
        hidT_ready = sem("hidT_ready")
        dn_mm = sem("dn_mm")
        res_ready = sem("res_ready")
        z_in = [sem(f"z_in{i}") for i in range(NZ)]
        comb = sem("comb")
        out_stored = sem("out_stored")

        NLOAD = 17
        block = stack.enter_context(nc.Block())

        @block.sync
        def _(sp):
            sp.sem_inc(x_in.sem, 16)
            sp.sem_inc(ctx_in.sem, 16)
            sp.sem_inc(hn_stored.sem, 16)
            sp.dma_start(X2[:, 0:G, :], x[0:G].rearrange("b t c -> t b c")).then_inc(x_in.sem, 16)
            sp.dma_start(CST[:], consts[:, 0:3, :]).then_inc(consts_in, 16)
            sp.dma_start(COLS[:], cols).then_inc(consts_in, 16)
            sp.dma_start(ctx_f[:], ctx_t[0]).then_inc(ctx_in.sem, 16)
            for dst, src in ((WV, w_v), (WQK, w_qk), (WIG, w_ig), (WG, w_g), (WOG, w_og), (WO, w_o),
                             (WRT, w_rt), (ROWS, rows), (DSK, dskip), (IOT, iotas), (TOEP, toep)):
                sp.dma_start(dst[:], src).then_inc(consts_in, 16)
            with sp.Fori(0, NG - 1) as g:
                sp.wait_ge(x_in.sem, x_in.now(g))
                sp.nop(nofuse=True)
                sp.dma_start(X2[:, bass.ds(G * g + G, G), :],
                             x[bass.ds(G * g + G, G)].rearrange("b t c -> t b c")).then_inc(x_in.sem, 16)
                sp.wait_ge(ctx_in.sem, ctx_in.now(g))
                sp.wait_ge(pairs.sem, pairs.now(g))
                sp.nop(nofuse=True)
                sp.dma_start(ctx_f[:], ctx_t[bass.ds(g + 1, 1)].rearrange("g p n -> (g p) n"))\
                    .then_inc(ctx_in.sem, 16)
                sp.wait_ge(h_ready.sem, h_ready.now(g))
                sp.nop(nofuse=True)
                sp.dma_start(hn_dram[bass.ds(GT * g, GT), :].rearrange("(b t) c -> t b c", t=T), xn)\
                    .then_inc(hn_stored.sem, 16)
                sp.wait_ge(hn_stored.sem, hn_stored.now(g))
                sp.nop(nofuse=True)
            last = NG - 1
            sp.wait_ge(redd.sem, redd.now(last))
            sp.wait_ge(y_mm.sem, y_mm.now(last))
            sp.wait_ge(q_mm.sem, q_mm.now(last))
            sp.wait_ge(conv.sem, conv.now(last))
            sp.wait_ge(mem_ready.sem, mem_ready.now(last))
            sp.wait_ge(y2_tr.sem, y2_tr.now(last))
            sp.wait_ge(oT_ready.sem, oT_ready.now(last))
            sp.nop(nofuse=True)
            sp.dma_start(WGU[:, ELOW * GUW:], w_gu[:, ELOW * GUW:]).then_inc(high_in, 16)
            sp.wait_ge(h_ready.sem, h_ready.now(last))
            sp.nop(nofuse=True)
            sp.dma_start(hn_dram[last * GT:, :].rearrange("(b t) c -> t b c", t=T), xn)\
                .then_inc(hn_stored.sem, 16)
            for i in range(NB):
                sp.wait_ge(scattered[i], 16 * (NTILE // NB))
                sp.nop(nofuse=True)
            z_v = z_dram.rearrange("(n p k) c -> n p (k c)", p=P, k=TOPK)
            for n in range(B):
                if n >= NZ:
                    sp.wait_ge(comb, TOPK * (n - NZ + 1))
                    sp.nop(nofuse=True)
                    sp.dma_start(out[n - NZ], X2[:, n - NZ, :]).then_inc(out_stored, 16)
                sp.dma_start(z_buf[n % NZ], z_v[n]).then_inc(z_in[n % NZ], 16)
            for n in range(B - NZ, B):
                sp.wait_ge(comb, TOPK * (n + 1))
                sp.nop(nofuse=True)
                sp.dma_start(out[n], X2[:, n, :]).then_inc(out_stored, 16)
            sp.wait_ge(out_stored, 16 * B)
            sp.nop(nofuse=True)

        @block.gpsimd
        def _(pool):
            for s in (rstd_step, rqk_ready, qw_ready, qb_ready, gam_ready,
                      r2_step, r3_step, pairs):
                pool.sem_inc(s.sem, s.per)
            pool.dma_start(WGU[:, 0:ELOW * GUW], w_gu[:, 0:ELOW * GUW])\
                .then_inc(gu_in, 16)
            pool.dma_start(WDN[:], w_dn).then_inc(gu_in, 16)
            pool.memset(half[:], -0.5).then_inc(half_set, 1)
            pool.memset(xnT[:, :, :, 0:KC - 1], 0.0).then_inc(half_set, 1)
            pool.wait_ge(half_set, 2)
            pool.wait_ge(consts_in, 16 * 13)
            pool.nop(nofuse=True)

            def norm_factors(g, aggr, k):
                pool.wait_ge(aggr.sem, aggr.now(g))
                pool.nop(nofuse=True)
                nc.gpsimd.tensor_scalar(rs[:], mv[:, :, 1], LN_EPS, None, ALU.add).then_inc(rstd_step.sem, 1)
                nc.gpsimd.tensor_scalar(nmean[:], mv[:, :, 0], -1.0, None, ALU.mult).then_inc(rstd_step.sem, 1)
                pool.wait_ge(rstd_step.sem, rstd_step.now(g, k + 2))
                pool.nop(nofuse=True)
                nc.gpsimd.tensor_tensor(rstd[:], rs[:], half[:, 0:G], ALU.pow).then_inc(rstd_step.sem, 1)
                pool.wait_ge(rstd_step.sem, rstd_step.now(g, k + 3))
                pool.nop(nofuse=True)
                nc.gpsimd.tensor_tensor(nmr[:], nmean[:], rstd[:], ALU.mult).then_inc(rstd_step.sem, 1)

            with pool.Fori(0, NG) as g:
                norm_factors(g, aggr1, 0)
                pool.wait_ge(ctx_in.sem, ctx_in.now(g))
                pool.wait_ge(y_mm.sem, y_mm.before(g))
                pool.nop(nofuse=True)
                for s in range(XD):
                    n, off = XD - s, pair_offset(s)
                    nc.gpsimd.tensor_tensor(kvp[:, :, off:off + n], ctxm[:, :, 0:n], ctxm[:, :, s:XD],
                                            ALU.mult).then_inc(pairs.sem, 1)
                pool.wait_ge(ssmax.sem, ssmax.now(g))
                pool.nop(nofuse=True)
                nc.gpsimd.tensor_tensor(rqk[:], ss[:], half[:], ALU.pow).then_inc(rqk_ready.sem, 1)
                pool.wait_ge(gam_out.sem, gam_out.now(g))
                pool.nop(nofuse=True)
                pool.memset(gam[:, :, :].rearrange("p c (b t) -> p (c b) t", t=T)[:, :, 0:1], 0.0)\
                    .then_inc(gam_ready.sem, 1)
                pool.wait_ge(qn_ready.sem, qn_ready.now(g))
                pool.wait_ge(kv_step.sem, kv_step.now(g))
                pool.nop(nofuse=True)
                nc.gpsimd.tensor_tensor(v, qn, ROWS[:, 0:1, :].to_broadcast([P, G, C]), ALU.mult)\
                    .then_inc(qw_ready.sem, 1)
                nc.gpsimd.tensor_tensor(qn, qn, ROWS[:, 1:2, :].to_broadcast([P, G, C]), ALU.mult)\
                    .then_inc(qb_ready.sem, 1)
                pool.wait_ge(memvar.sem, memvar.now(g))
                pool.nop(nofuse=True)
                nc.gpsimd.tensor_scalar(s2[:], s2[:], 1.0 / HD, LN_EPS, ALU.mult, ALU.add).then_inc(r2_step.sem, 1)
                pool.wait_ge(r2_step.sem, r2_step.now(g, 1))
                pool.nop(nofuse=True)
                nc.gpsimd.tensor_tensor(r2[:], s2[:], half[:, 0:G * HEADS], ALU.pow).then_inc(r2_step.sem, 1)
                pool.wait_ge(ovar.sem, ovar.now(g))
                pool.nop(nofuse=True)
                nc.gpsimd.tensor_scalar(s3[:], s3[:], 1.0 / HD, LN_EPS, ALU.mult, ALU.add).then_inc(r3_step.sem, 1)
                pool.wait_ge(r3_step.sem, r3_step.now(g, 1))
                pool.nop(nofuse=True)
                nc.gpsimd.tensor_tensor(r3[:], s3[:], half[:, 0:G * HEADS], ALU.pow).then_inc(r3_step.sem, 1)
                norm_factors(g, aggr2, 4)
                norm_factors(g, aggr3, 8)

            def gather(t, u):
                pool.indirect_dma_start(out=xg[u], out_offset=None, in_=hn_dram,
                                        in_offset=bass.IndirectOffsetOnAxis(gcol[:, u:u + 1], 0))\
                    .then_inc(gathered[u], 16)

            def scatter(t, u):
                pool.wait_ge(scol_ready, t + 1)
                pool.wait_ge(res_ready, t + 1 + AHEAD)
                pool.nop(nofuse=True)
                pool.indirect_dma_start(out=z_dram, out_offset=bass.IndirectOffsetOnAxis(scol[:, u:u + 1], 0),
                                        in_=res[u], in_offset=None, bounds_check=NSLOT - 1,
                                        oob_is_err=False).then_inc(scattered[u], 16)

            pool.wait_ge(hn_stored.sem, hn_stored.now(NG - 1))
            pool.nop(nofuse=True)
            for u in range(NB):
                pool.wait_ge(gcol_ready, u + 1)
                pool.nop(nofuse=True)
                gather(u, u)
            with pool.Fori(0, NTILE // NB - 1) as i:
                for u in range(NB):
                    t = NB * i + u
                    pool.wait_ge(gcol_ready, t + NB + 1)
                    pool.wait_ge(xg_tr, t + 1)
                    pool.nop(nofuse=True)
                    gather(t + NB, u)
                    scatter(t, u)
            for u in range(NB):
                scatter(NTILE - NB + u, u)

        @block.tensor
        def _(pe):
            for s in (xn_tr, v_mm, k_mm, q_mm, ig_mm, gam_mm, kv_tr, og_mm, mem_tr, o_tr, wo_mm, q2_tr,
                      y_mm, y2_tr, h_tr, lg_mm, rank_mm):
                pe.sem_inc(s.sem, s.per)
            pe.sem_inc(id_mm, NHOT)
            for s in (hid_tr, gu_mm, dn_mm):
                pe.sem_inc(s, AHEAD)
            pe.wait_ge(consts_in, 16 * 13)
            pe.wait_ge(half_set, 2)

            def transposed(src, dst, signal_):
                for c in range(NC):
                    for b in range(G):
                        last = nc.tensor.transpose(chan(dst)[:, c, b * T:(b + 1) * T],
                                                   src[:, b, c * P:(c + 1) * P], ident)
                last.then_inc(signal_.sem, 1)

            def by_channel(dst, w, rhs, signal_):
                for c in range(NC):
                    for k in range(NC):
                        last = nc.tensor.matmul(chan(dst)[:, c, :], w[:, k, c * P:(c + 1) * P], rhs[:, k, :],
                                                start=(k == 0), stop=(k == NC - 1))
                last.then_inc(signal_.sem, 1)

            def by_token(dst, lhs, w, signal_):
                for b in range(G):
                    for k in range(NC):
                        last = nc.tensor.matmul(tok(dst)[:, b, :], lhs(k, b), w[:, k, :],
                                                start=(k == 0), stop=(k == NC - 1))
                last.then_inc(signal_.sem, 1)

            def toeplitz(g, h):
                pe.wait_ge(y_out.sem, y_out.now(g, h - 1))
                for lc in range(NC):
                    for mc in range(lc + 1):
                        last = nc.tensor.matmul(
                            pY[:, h % 2, lc * G * NPAIR:(lc + 1) * G * NPAIR]
                            .rearrange("p (b n) -> p b n", n=NPAIR),
                            TOEP[:, h, (lc - mc) * P:(lc - mc + 1) * P], kvp_h[:, mc, :, h, :],
                            start=(mc == 0), stop=(mc == lc))
                last.then_inc(y_mm.sem, 1)

            with pe.Fori(0, NG) as g:
                def feature(k, b):
                    return xnT[:, k, b, KC - 1:]

                pe.wait_ge(xn_ready.sem, xn_ready.now(g))
                pe.wait_ge(hT_ready.sem, hT_ready.before(g))
                transposed(xn, pA, xn_tr)
                pe.wait_ge(xnT_ready.sem, xnT_ready.now(g))
                pe.wait_ge(rt.sem, rt.before(g, 2))
                by_token(pB, feature, WV[:, :, :], v_mm)
                pe.wait_ge(rt.sem, rt.before(g))
                by_token(pC, feature, WQK[:, :, C:2 * C], k_mm)
                by_token(pA, feature, WQK[:, :, 0:C], q_mm)
                pe.wait_ge(xc_ready.sem, xc_ready.now(g))
                pe.wait_ge(v_out.sem, v_out.now(g))
                by_channel(pB, WIG, y, ig_mm)
                pe.wait_ge(kv_step.sem, kv_step.now(g))
                pe.wait_ge(ksq.sem, ksq.now(g))
                by_channel(pC, WG, y, gam_mm)
                pe.wait_ge(kv_ready.sem, kv_ready.now(g))
                pe.wait_ge(qn_ready.sem, qn_ready.now(g))
                pe.wait_ge(qsq.sem, qsq.now(g))
                transposed(kv, pA, kv_tr)
                pe.wait_ge(ig_ready.sem, ig_ready.now(g))
                by_channel(pB, WOG, y, og_mm)
                pe.wait_ge(toep_ready, 1)
                pe.wait_ge(pairs.sem, pairs.now(g))
                pe.wait_ge(prods.sem, prods.before(g))
                for h in range(XH // 2):
                    toeplitz(g, h)
                pe.wait_ge(mem_ready.sem, mem_ready.now(g))
                pe.wait_ge(gam_out.sem, gam_out.now(g))
                for b in range(G):
                    for c in range(NC):
                        last = nc.tensor.matmul(tok(pC)[:, b, c * P:(c + 1) * P], s_[:, c, b * T:(b + 1) * T],
                                                center, start=True, stop=True)
                last.then_inc(mem_tr.sem, 1)
                for h in range(XH // 2, XH):
                    toeplitz(g, h)
                pe.wait_ge(o_step.sem, o_step.now(g))
                pe.wait_ge(bt_ready.sem, bt_ready.now(g))
                transposed(o, pA, o_tr)
                pe.wait_ge(oT_ready.sem, oT_ready.now(g))
                pe.wait_ge(og_ready.sem, og_ready.now(g))
                by_token(pB, lambda k, b: y[:, k, b * T:(b + 1) * T], WO, wo_mm)
                pe.wait_ge(q2_ready.sem, q2_ready.now(g))
                pe.wait_ge(oT_out.sem, oT_out.now(g))
                transposed(xn, pA, q2_tr)
                pe.wait_ge(redd.sem, redd.now(g))
                pe.wait_ge(memsq.sem, memsq.now(g))
                pe.wait_ge(o_step.sem, o_step.now(g, 1))
                for b in range(G):
                    for c in range(NC):
                        last = nc.tensor.transpose(tok(pC)[:, b, c * P:(c + 1) * P],
                                                   kv_f[:, (c * G + b) * P:(c * G + b + 1) * P], ident)
                last.then_inc(y2_tr.sem, 1)
                pe.wait_ge(h_ready.sem, h_ready.now(g))
                pe.wait_ge(q2T_ready.sem, q2T_ready.now(g))
                transposed(xn, pA, h_tr)
                pe.wait_ge(hT_ready.sem, hT_ready.now(g))
                pe.wait_ge(x1_ready.sem, x1_ready.now(g))
                for b in range(G):
                    for k in range(NC):
                        last = nc.tensor.matmul(pB[:, b * E:(b + 1) * E], y[:, k, b * T:(b + 1) * T],
                                                WRT[:, k, :], start=(k == 0), stop=(k == NC - 1))
                last.then_inc(lg_mm.sem, 1)
                pe.wait_ge(x2_ready.sem, x2_ready.now(g))
                pe.wait_ge(rt.sem, rt.now(g, RT_SEL))
                for b in range(G):
                    nc.tensor.matmul(pC[:, b * E:(b + 1) * E], TRI[:, 0, :], sel[:, b, :], start=True, stop=False)
                    last = nc.tensor.matmul(pC[:, b * E:(b + 1) * E], TRI[:, 1, :], cum[:, b, :],
                                            start=False, stop=True)
                last.then_inc(rank_mm.sem, 1)

            pe.wait_ge(rt.sem, rt.now(NG - 1))
            nc.tensor.matmul(pB[0:E, 0:1], cum[:, 0, :], TRI[:, 1, 0:1], start=True, stop=True).then_inc(cnt_mm, 1)
            pe.wait_ge(plan, 6)
            nc.tensor.matmul(pA[:, 0:E], ntb[:, :], tri_lt, start=True, stop=True)
            nc.tensor.matmul(pA[0:E, 512:513], tri_le, ntf[:, :], start=True, stop=True).then_inc(start_mm, 1)
            pe.wait_ge(plan, 7)
            nc.tensor.matmul(pC[0:1, 0:NTILE], onesf[0:E, 0:1], over[:, :], start=True, stop=True).then_inc(etile_mm, 1)
            def number_rows(r, first=False, last=False):
                for u in range(NHOT):
                    pe.wait_ge(lo_ready, NHOT * r + u + 1)
                    pe.wait_ge(hi_ready, NHOT * r + u + 1)
                    nc.tensor.matmul(pA[:, 0:NTILE], lo_hot[u], hi_hot[u], start=(first and u == 0),
                                     stop=(last and u == NHOT - 1)).then_inc(id_mm, 1)

            rounds = B * TOPK // NHOT
            pe.wait_ge(plan, 8)
            number_rows(0, first=True)
            with pe.Fori(1, rounds - 1) as r:
                number_rows(r)
            number_rows(rounds - 1, last=True)

            def rows_T(t, u):
                pe.wait_ge(gathered[u % NB], 16 * (t // NB + 1))
                pe.wait_ge(xgT_ready, t + 1)
                for k in range(NC):
                    last = nc.tensor.transpose(pA[:, (u % 2) * 512 + k * P:(u % 2) * 512 + (k + 1) * P],
                                               xg[u % NB][:, k * P:(k + 1) * P], ident)
                last.then_inc(xg_tr, 1)

            def gate_up(t, u):
                e = pe.value_load(etile[0:1, bass.ds(t, 1)], min_val=0, max_val=E - 1)
                pe.wait_ge(xgT_ready, t + 1 + AHEAD)
                pe.wait_ge(hid_ready, t + 1)
                for k in range(NC):
                    last = nc.tensor.matmul(pB[:, (u % 2) * 512:(u % 2) * 512 + 2 * INNER],
                                            xgT[u % 2][:, k * P:(k + 1) * P], WGU_E[:, bass.ds(e * NC + k, 1), :],
                                            start=(k == 0), stop=(k == NC - 1))
                last.then_inc(gu_mm, 1)

            def hidden_T(t, u):
                pe.wait_ge(hid_ready, t + 1 + AHEAD)
                pe.wait_ge(hidT_ready, t + 1)
                nc.tensor.transpose(pY[:, u % 2, 0:P], hid[u % 2], ident).then_inc(hid_tr, 1)

            def down(t, u):
                e = pe.value_load(etile[0:1, bass.ds(t, 1)], min_val=0, max_val=E - 1)
                pe.wait_ge(hidT_ready, t + 1 + AHEAD)
                pe.wait_ge(res_ready, t + 1)
                nc.tensor.matmul(pC[:, (u % 2) * 512:(u % 2) * 512 + C], hidT[u % 2],
                                 WDN[:, bass.ds(e, 1), :], start=True, stop=True).then_inc(dn_mm, 1)

            pe.wait_ge(plan, PLAN_DONE)
            pe.wait_ge(gu_in, 32)
            pe.wait_ge(high_in, 16)
            rows_T(0, 0)
            gate_up(0, 0)
            with pe.Fori(0, NTILE // NB - 1) as i:
                for u in range(NB):
                    t = NB * i + u
                    pe.wait_ge(gathered[(u + 1) % NB], 16 * i + 16 * (1 + (u + 1) // NB))
                    pe.wait_ge(xgT_ready, t + 2)
                    for k in range(NC):
                        last = nc.tensor.transpose(pA[:, ((u + 1) % 2) * 512 + k * P:((u + 1) % 2) * 512 + (k + 1) * P],
                                                   xg[(u + 1) % NB][:, k * P:(k + 1) * P], ident)
                    last.then_inc(xg_tr, 1)
                    hidden_T(t, u)
                    gate_up(t + 1, u + 1)
                    down(t, u)
            for u in range(NB):
                t = NTILE - NB + u
                if u < NB - 1:
                    rows_T(t + 1, u + 1)
                hidden_T(t, u)
                if u < NB - 1:
                    gate_up(t + 1, u + 1)
                down(t, u)

        @block.scalar
        def _(act):
            for s in (xn_ready, q2_ready, h_ready, xnT_ready, tap0, sig_y, v_out, ksq, qsq, ig_ready, gam_out, og_ready, memsq, osq,
                      oT_out, q2T_ready, y_out, hT_ready, ex_ready):
                act.sem_inc(s.sem, s.per)
            for s in (xgT_ready, silu_ready):
                act.sem_inc(s, AHEAD)
            act.wait_ge(consts_in, 16 * 13)

            def evict_y(g, h):
                act.wait_ge(y_mm.sem, y_mm.now(g, h + 1))
                nc.scalar.activation(yh[:, :, :, h, :],
                                     pY[:, h % 2, 0:NC * G * NPAIR].rearrange("p (c b n) -> p c b n", c=NC, b=G),
                                     ACT.Copy).then_inc(y_out.sem, 1)

            def normalize(g, ready, k):
                act.wait_ge(rstd_step.sem, rstd_step.now(g, k))
                act.nop(nofuse=True)
                for b in range(G):
                    last = nc.scalar.activation(xn[:, b, :], X2[:, bass.ds(G * g + b, 1), :]
                                                .rearrange("p b c -> p (b c)"), ACT.Identity,
                                                scale=rstd[:, b:b + 1], bias=nmr[:, b:b + 1])
                last.then_inc(ready.sem, 1)

            with act.Fori(0, NG) as g:
                act.wait_ge(hn_stored.sem, hn_stored.before(g))
                normalize(g, xn_ready, 4)
                act.wait_ge(xn_tr.sem, xn_tr.now(g))
                for c in range(NC):
                    nc.scalar.activation(xnT[:, c, :, KC - 1:], chan(pA)[:, c, :].rearrange("p (b t) -> p b t", b=G),
                                         ACT.Copy).then_inc(xnT_ready.sem, 1)
                for c in range(NC):
                    act.wait_ge(xnT_ready.sem, xnT_ready.now(g, c + 1))
                    nc.scalar.activation(y[:, c, :].rearrange("p (b t) -> p b t", b=G), xnT[:, c, :, KC - 1:],
                                         ACT.Identity, scale=COLS[:, c, KC - 1:KC],
                                         bias=COLS[:, c, CONVB:CONVB + 1]).then_inc(tap0.sem, 1)
                act.wait_ge(v_mm.sem, v_mm.now(g))
                nc.scalar.activation(v_f[:, :], pB[:, :], ACT.Copy).then_inc(v_out.sem, 1)
                act.wait_ge(k_mm.sem, k_mm.now(g))
                nc.scalar.activation(o_f[:, :], pC[:, :], ACT.Square).then_inc(ksq.sem, 1)
                act.wait_ge(q_mm.sem, q_mm.now(g))
                nc.scalar.activation(bt_f[:, :], pA[:, :], ACT.Square).then_inc(qsq.sem, 1)
                act.wait_ge(conv.sem, conv.now(g))
                nc.scalar.activation(s_f[:, :], y_f[:, :], ACT.Sigmoid).then_inc(sig_y.sem, 1)
                act.wait_ge(ig_mm.sem, ig_mm.now(g))
                for c in range(NC):
                    nc.scalar.activation(ig[:, c, :], chan(pB)[:, c, :], ACT.Sigmoid,
                                         bias=COLS[:, c, BIG:BIG + 1]).then_inc(ig_ready.sem, 1)
                act.wait_ge(gam_mm.sem, gam_mm.now(g))
                for c in range(NC):
                    nc.scalar.activation(gam[:, c, :], chan(pC)[:, c, :], ACT.Sigmoid,
                                         bias=COLS[:, c, BG:BG + 1]).then_inc(gam_out.sem, 1)
                act.wait_ge(prods.sem, prods.before(g))
                for h in range(XH // 2):
                    evict_y(g, h)
                act.wait_ge(og_mm.sem, og_mm.now(g))
                act.wait_ge(mem_ready.sem, mem_ready.now(g))
                for c in range(NC):
                    nc.scalar.activation(btC[:, c, :], chan(pB)[:, c, :], ACT.Sigmoid,
                                         bias=COLS[:, c, BOG:BOG + 1]).then_inc(og_ready.sem, 1)
                act.wait_ge(mem_tr.sem, mem_tr.now(g))
                nc.scalar.activation(kv_f[:, :], pC[:, :], ACT.Square).then_inc(memsq.sem, 1)
                for h in range(XH // 2, XH):
                    evict_y(g, h)
                act.wait_ge(o_step.sem, o_step.now(g, 6))
                nc.scalar.activation(kv_f[:, :], o_f[:, :], ACT.Square).then_inc(osq.sem, 1)
                act.wait_ge(o_tr.sem, o_tr.now(g))
                for c in range(NC):
                    nc.scalar.activation(y[:, c, :], chan(pA)[:, c, :], ACT.Identity,
                                         scale=COLS[:, c, GNW:GNW + 1],
                                         bias=COLS[:, c, GNB:GNB + 1]).then_inc(oT_out.sem, 1)
                normalize(g, q2_ready, 8)
                act.wait_ge(q2_tr.sem, q2_tr.now(g))
                nc.scalar.activation(v_f[:, :], pA[:, :], ACT.Copy).then_inc(q2T_ready.sem, 1)
                normalize(g, h_ready, 12)
                act.wait_ge(h_tr.sem, h_tr.now(g))
                nc.scalar.activation(y_f[:, :], pA[:, :], ACT.Copy).then_inc(hT_ready.sem, 1)
                act.wait_ge(rt.sem, rt.now(g, 2))
                nc.scalar.activation(pe_[:], lg[:], ACT.Exp).then_inc(ex_ready.sem, 1)

            def tile(t, u):
                act.wait_ge(xg_tr, t + 1)
                act.wait_ge(gu_mm, t + 1)
                nc.scalar.activation(xgT[u % 2], pA[:, (u % 2) * 512:(u % 2) * 512 + C], ACT.Copy)\
                    .then_inc(xgT_ready, 1)
                act.wait_ge(gu_mm, t + 1 + AHEAD)
                act.wait_ge(hid_ready, t + 1)
                nc.scalar.activation(act_g[u % 2], pB[:, (u % 2) * 512:(u % 2) * 512 + INNER], ACT.Silu)\
                    .then_inc(silu_ready, 1)

            with act.Fori(0, NTILE // NB) as i:
                for u in range(NB):
                    tile(NB * i + u, u)

        @block.vector
        def _(dve):
            for s in (stats, aggr1, aggr2, aggr3, conv, xc_ready, ssum, ssmax, kv_step, kv_ready, qn_ready,
                      bt_ready, mem_ready, memvar, o_step, ovar, oT_ready, x1_ready, prods, redd, x2_ready, rt):
                dve.sem_inc(s.sem, s.per)
            for s in (hid_ready, hidT_ready, res_ready):
                dve.sem_inc(s, AHEAD)
            nc.vector.memset(cum[:], 0.0)
            nc.vector.memset(TRI[:, 1, :], 1.0).then_inc(plan, 1)
            dve.wait_ge(consts_in, 16 * 13)
            nc.vector.tensor_copy(TRI[:, 0, :], IOT[:, 3, :]).then_inc(plan, 1)
            for h in range(XH):
                last = nc.vector.scalar_tensor_tensor(TOEP[:, h, 0:P], ident, DSK[:, h:h + 1], TOEP[:, h, 0:P],
                                                      ALU.mult, ALU.add)
            last.then_inc(toep_ready, 1)

            def x2_of(g, b=None):
                return X2[:, bass.ds(G * g, G), :] if b is None else \
                    X2[:, bass.ds(G * g + b, 1), :].rearrange("p b c -> p (b c)")

            def statistics(g, aggr, k):
                for b in range(G):
                    nc.vector.bn_stats(st[:, b, :], x2_of(g, b)).then_inc(stats.sem, 1)
                for b in range(G):
                    dve.wait_ge(stats.sem, stats.now(g, k + b + 1))
                    dve.nop(nofuse=True)
                    nc.vector.bn_aggr(mv[:, b, :], st[:, b, :]).then_inc(aggr.sem, 1)

            with dve.Fori(0, NG) as g:
                dve.wait_ge(x_in.sem, x_in.now(g))
                dve.nop(nofuse=True)
                statistics(g, aggr1, 0)
                for j in range(1, KC):
                    for c in range(NC):
                        if j == 1:
                            dve.wait_ge(tap0.sem, tap0.now(g, c + 1))
                        else:
                            dve.wait_ge(conv.sem, conv.now(g, 2 * (j - 1) - 1 + c))
                        yc = y[:, c, :].rearrange("p (b t) -> p b t", b=G)
                        nc.vector.scalar_tensor_tensor(yc, xnT[:, c, :, KC - 1 - j:KC - 1 - j + T],
                                                       COLS[:, c, KC - 1 - j:KC - j], yc, ALU.mult, ALU.add)\
                            .then_inc(conv.sem, 1)
                dve.wait_ge(ksq.sem, ksq.now(g))
                nc.vector.tensor_reduce(ss[:, G * HEADS:], per_head(o_f[:, :]), AX.X, ALU.add).then_inc(ssum.sem, 1)
                dve.wait_ge(qsq.sem, qsq.now(g))
                nc.vector.tensor_reduce(ss[:, 0:G * HEADS], per_head(bt_f[:, :]), AX.X, ALU.add).then_inc(ssum.sem, 1)
                dve.wait_ge(ssum.sem, ssum.now(g))
                nc.vector.tensor_scalar(ss[:], ss[:], 1e-24, None, ALU.max).then_inc(ssmax.sem, 1)
                dve.wait_ge(v_out.sem, v_out.now(g))
                nc.vector.tensor_tensor(kv_f[:, :], pC[:, :], v_f[:, :], ALU.mult).then_inc(kv_step.sem, 1)
                dve.wait_ge(sig_y.sem, sig_y.now(g))
                nc.vector.tensor_tensor(y_f[:, :], y_f[:, :], s_f[:, :], ALU.mult).then_inc(xc_ready.sem, 1)
                dve.wait_ge(kv_step.sem, kv_step.now(g))
                dve.wait_ge(rqk_ready.sem, rqk_ready.now(g))
                nrm = rqk[:, :].rearrange("p (r o) -> p r o", o=1)
                nc.vector.tensor_tensor(per_head(kv_f[:, :]), per_head(kv_f[:, :]),
                                        nrm[:, G * HEADS:, :].to_broadcast([P, G * HEADS, HD]), ALU.mult)\
                    .then_inc(kv_ready.sem, 1)
                nc.vector.tensor_tensor(per_head(qn_f[:, :]), per_head(pA[:, :]),
                                        nrm[:, 0:G * HEADS, :].to_broadcast([P, G * HEADS, HD]), ALU.mult)\
                    .then_inc(qn_ready.sem, 1)
                dve.wait_ge(kv_tr.sem, kv_tr.now(g))
                dve.wait_ge(ig_ready.sem, ig_ready.now(g))
                nc.vector.tensor_tensor(bt_f[:, :], pA[:, :], ig.rearrange("p c t -> p (c t)"), ALU.mult)\
                    .then_inc(bt_ready.sem, 1)
                dve.wait_ge(gam_ready.sem, gam_ready.now(g))
                dve.wait_ge(bt_ready.sem, bt_ready.now(g))
                for c in range(NC):
                    nc.vector.tensor_tensor_scan(s_[:, c, :], gam[:, c, :], btC[:, c, :], 0.0, ALU.mult, ALU.add)\
                        .then_inc(mem_ready.sem, 1)
                dve.wait_ge(memsq.sem, memsq.now(g))
                nc.vector.tensor_reduce(s2[:], per_head(kv_f[:, :]), AX.X, ALU.add).then_inc(memvar.sem, 1)
                dve.wait_ge(r2_step.sem, r2_step.now(g))

                def small(f):
                    return f[:, :].rearrange("p (r o) -> p r o", o=1).to_broadcast([P, G * HEADS, HD])

                nc.vector.tensor_tensor(per_head(o_f[:, :]), per_head(pC[:, :]), small(r2), ALU.mult)\
                    .then_inc(o_step.sem, 1)
                dve.wait_ge(qw_ready.sem, qw_ready.now(g))
                dve.wait_ge(o_step.sem, o_step.now(g, 1))
                nc.vector.tensor_tensor(o_f[:, :], o_f[:, :], v_f[:, :], ALU.mult).then_inc(o_step.sem, 1)
                dve.wait_ge(qb_ready.sem, qb_ready.now(g))
                dve.wait_ge(o_step.sem, o_step.now(g, 2))
                nc.vector.tensor_tensor(o_f[:, :], o_f[:, :], qn_f[:, :], ALU.add).then_inc(o_step.sem, 1)
                dve.wait_ge(o_step.sem, o_step.now(g, 3))
                nc.vector.tensor_reduce(mu[:], per_head(o_f[:, :]), AX.X, ALU.add).then_inc(o_step.sem, 1)
                dve.wait_ge(o_step.sem, o_step.now(g, 4))
                nc.vector.tensor_scalar(mu[:], mu[:], 1.0 / HD, None, ALU.mult).then_inc(o_step.sem, 1)
                dve.wait_ge(o_step.sem, o_step.now(g, 5))
                nc.vector.tensor_tensor(per_head(o_f[:, :]), per_head(o_f[:, :]), small(mu), ALU.subtract)\
                    .then_inc(o_step.sem, 1)
                dve.wait_ge(osq.sem, osq.now(g))
                nc.vector.tensor_reduce(s3[:], per_head(kv_f[:, :]), AX.X, ALU.add).then_inc(ovar.sem, 1)
                dve.wait_ge(r3_step.sem, r3_step.now(g))
                nc.vector.tensor_tensor(per_head(o_f[:, :]), per_head(o_f[:, :]), small(r3), ALU.mult)\
                    .then_inc(o_step.sem, 1)
                dve.wait_ge(oT_out.sem, oT_out.now(g))
                dve.wait_ge(og_ready.sem, og_ready.now(g))
                nc.vector.tensor_tensor(y_f[:, :], y_f[:, :], bt_f[:, :], ALU.mult).then_inc(oT_ready.sem, 1)
                dve.wait_ge(wo_mm.sem, wo_mm.now(g))
                nc.vector.tensor_tensor(x2_of(g), tok(pB), x2_of(g), ALU.add).then_inc(x1_ready.sem, 1)
                dve.wait_ge(x1_ready.sem, x1_ready.now(g))
                dve.nop(nofuse=True)
                statistics(g, aggr2, G)
                dve.wait_ge(q2T_ready.sem, q2T_ready.now(g))
                dve.wait_ge(y_out.sem, y_out.now(g))
                nq = G * XH
                qT = v_f[:, :].rearrange("p (q i) -> p q i", i=XD)
                for lc in range(NC):
                    if lc:
                        dve.wait_ge(redd.sem, redd.now(g, lc))
                    rows_ = slice(lc * nq, (lc + 1) * nq)
                    for s in range(XD):
                        n, off = XD - s, pair_offset(s)
                        conv_pairs = yq[:, rows_, off:off + n]
                        nc.vector.tensor_tensor(prod[:, :, s * XD:s * XD + n * (XD + 1) - XD:XD + 1], conv_pairs,
                                                qT[:, rows_, 0:n], ALU.mult).then_inc(prods.sem, 1)
                        if s:
                            nc.vector.tensor_tensor(prod[:, :, s:s + n * (XD + 1) - XD:XD + 1], conv_pairs,
                                                    qT[:, rows_, s:XD], ALU.mult).then_inc(prods.sem, 1)
                    dve.wait_ge(prods.sem, prods.now(g, 15 * (lc + 1)))
                    nc.vector.tensor_reduce(kv_f[:, lc * nq * XD:(lc + 1) * nq * XD],
                                            prod_f.rearrange("p (r i) -> p r i", i=XD), AX.X, ALU.add)\
                        .then_inc(redd.sem, 1)
                dve.wait_ge(y2_tr.sem, y2_tr.now(g))
                nc.vector.tensor_tensor(x2_of(g), tok(pC), x2_of(g), ALU.add).then_inc(x2_ready.sem, 1)
                dve.wait_ge(x2_ready.sem, x2_ready.now(g))
                dve.nop(nofuse=True)
                statistics(g, aggr3, 2 * G)

                done = [0]

                def link(ins):
                    done[0] += 1
                    ins.then_inc(rt.sem, 1)
                    dve.wait_ge(rt.sem, rt.now(g, done[0]))
                    dve.nop(nofuse=True)

                def bc(f, n):
                    return f.rearrange("p (b o) -> p b o", o=1).to_broadcast([P, G, n])

                logits = pB[:, 0:G * E].rearrange("p (b e) -> p b e", b=G)
                dve.wait_ge(lg_mm.sem, lg_mm.now(g))
                link(nc.vector.tensor_reduce(lmax[:], logits, AX.X, ALU.max))
                link(nc.vector.tensor_tensor(lg[:], logits, bc(lmax[:, :], E), ALU.subtract))
                dve.wait_ge(ex_ready.sem, ex_ready.now(g))
                link(nc.vector.tensor_reduce(psm[:, 0, :], pe_[:], AX.X, ALU.add))
                link(nc.vector.reciprocal(psm[:, 1, :], psm[:, 0, :]))
                link(nc.vector.tensor_tensor(pr[:], pe_[:], bc(psm[:, 1, :], E), ALU.mult))
                for b in range(G):
                    link(nc.vector.max(m8[:, b, :], pr[:, b, :]))
                for b in range(G):
                    link(nc.vector.max_index(ix[:, b, :], m8[:, b, :], pr[:, b, :]))
                link(nc.vector.tensor_copy(ixf[:], ix[:, :, 0:TOPK]))
                oh_g = OH[:, bass.ds(G * g, G), :]
                link(nc.vector.tensor_tensor(
                    oh_g.rearrange("p b (k e) -> p (b k) e", k=TOPK),
                    IOT[:, 0:1, 0:E].to_broadcast([P, G * TOPK, E]),
                    ixf[:, :, :].rearrange("p b (k o) -> p (b k) o", o=1).to_broadcast([P, G * TOPK, E]),
                    ALU.is_equal))
                with nc.allow_low_precision("zeros and ones"):
                    link(nc.vector.tensor_reduce(sel[:], oh_g.rearrange("p b (k e) -> p b e k", k=TOPK),
                                                 AX.X, ALU.add))
                for b in range(G):
                    link(nc.vector.tensor_tensor(cum[:, b + 1, :], cum[:, b, :], sel[:, b, :], ALU.add))
                assert done[0] == RT_SEL
                link(nc.vector.tensor_reduce(wsum[:, 0, :], m8[:, :, 0:TOPK], AX.X, ALU.add))
                link(nc.vector.reciprocal(wsum[:, 1, :], wsum[:, 0, :]))
                link(nc.vector.tensor_tensor(WT[:, bass.ds(G * g, G), :], m8[:, :, 0:TOPK],
                                             bc(wsum[:, 1, :], TOPK), ALU.mult))
                dve.wait_ge(rank_mm.sem, rank_mm.now(g))
                for b in range(G):
                    t4 = tmp_oh[:, b * TOPK * E:(b + 1) * TOPK * E].rearrange("p (k e) -> p k e", k=TOPK)
                    link(nc.vector.tensor_tensor(
                        t4, pC[:, b * E:(b + 1) * E].rearrange("p (o e) -> p o e", o=1).to_broadcast([P, TOPK, E]),
                        OH[:, bass.ds(G * g + b, 1), :].rearrange("p b (k e) -> p (b k) e", k=TOPK), ALU.mult))
                link(nc.vector.tensor_reduce(posr[:, bass.ds(G * g, G), :],
                                             tmp_oh[:, :].rearrange("p (b k e) -> p b k e", b=G, k=TOPK),
                                             AX.X, ALU.add))
                link(nc.vector.tensor_copy(cum[:, 0, :], cum[:, G, :]))
                assert done[0] == RT_STEPS

            def step(ins, value):
                ins.then_inc(plan, 1)
                dve.wait_ge(plan, value)

            dve.wait_ge(cnt_mm, 1)
            step(nc.vector.tensor_scalar(nti[:, 0:1], pB[0:E, 0:1], float(P - 1), None, ALU.add), 3)
            step(nc.vector.tensor_scalar(nti[:, 1:2], nti[:, 0:1], 7, None, ALU.arith_shift_right), 4)
            step(nc.vector.tensor_copy(ntf[:], nti[:, 1:2]), 5)
            step(nc.vector.tensor_copy(ntb[:], ntf[:, 0:1].to_broadcast([E, P])), 6)
            dve.wait_ge(start_mm, 1)
            step(nc.vector.tensor_scalar(over[:], IOT[0:E, 0, 0:NTILE], pA[0:E, 512:513], None, ALU.is_ge), 7)
            step(nc.vector.tensor_copy(start[:], pA[:, 0:E]), 8)
            step(nc.vector.tensor_tensor(oh_prod, OH[:, :, :].rearrange("p b (k e) -> p (b k) e", k=TOPK),
                                         start[:, :].rearrange("p (o e) -> p o e", o=1)
                                         .to_broadcast([P, B * TOPK, E]), ALU.mult), 9)
            step(nc.vector.tensor_reduce(posf[:], oh_prod, AX.X, ALU.add), 10)
            step(nc.vector.tensor_tensor(posf[:], posf[:], posr[:, :, :].rearrange("p b k -> p (b k)"), ALU.add), 11)
            step(nc.vector.tensor_copy(posi[:, 0, :], posf[:]), 12)
            step(nc.vector.tensor_scalar(posi[:, 1, :], posi[:, 0, :], 7, None, ALU.arith_shift_right), 13)
            step(nc.vector.tensor_scalar(posi[:, 2, :], posi[:, 0, :], P - 1, None, ALU.bitwise_and), 14)
            nc.vector.tensor_copy(pos2[:, :, :], posi[:, 1:3, :]).then_inc(pos_ready, 1)
            dve.wait_ge(pos_ready, 1)
            with dve.Fori(0, B * TOPK // NHOT) as r:
                for u in range(NHOT):
                    dve.wait_ge(id_mm, NHOT * r + u + 1)
                    nc.vector.tensor_scalar(lo_hot[u], iota, pos2[:, 1, bass.ds(NHOT * r + u, 1)], None,
                                            ALU.is_equal).then_inc(lo_ready, 1)
                    nc.vector.tensor_scalar(hi_hot[u], IOT[:, 0, 0:NTILE], pos2[:, 0, bass.ds(NHOT * r + u, 1)],
                                            IOT[:, 1, bass.ds(NHOT * r + u, 1)], ALU.is_equal, ALU.mult)\
                        .then_inc(hi_ready, 1)
            dve.wait_ge(etile_mm, 1)
            step(nc.vector.tensor_scalar(etile[:], pC[0:1, 0:NTILE], float(E - 1), None, ALU.min), 15)
            dve.wait_ge(id_mm, NHOT + B * TOPK)
            step(nc.vector.tensor_scalar(idx_t[:, 0, :], pA[:, 0:NTILE], 0.0, float(FAR), ALU.is_equal, ALU.mult), 16)
            step(nc.vector.scalar_tensor_tensor(idx_t[:, 1, :], pA[:, 0:NTILE], -1.0, idx_t[:, 0, :],
                                                ALU.add, ALU.add), 17)
            step(nc.vector.tensor_scalar(idx_t[:, 2, :], pA[:, 0:NTILE], -1.0, 0.0, ALU.add, ALU.max), 18)
            step(nc.vector.tensor_copy(SIDX[:], idx_t[:, 1, :]), 19)
            step(nc.vector.tensor_copy(GIDX[:, 0, :], idx_t[:, 2, :]), 20)
            step(nc.vector.tensor_scalar(GIDX[:, 1, :], GIDX[:, 0, :], 2, None, ALU.arith_shift_right), PLAN_DONE)

            def gather_column(t, u):
                nc.vector.tensor_copy(gcol[:, u:u + 1], GIDX[:, 1, bass.ds(t, 1)].bitcast(U32)).then_inc(gcol_ready, 1)

            def tile(t, u, i):
                dve.wait_ge(silu_ready, t + 1 + AHEAD)
                dve.wait_ge(hid_tr, t + 1)
                nc.vector.tensor_tensor(hid[u % 2], act_g[u % 2],
                                        pB[:, (u % 2) * 512 + INNER:(u % 2) * 512 + 2 * INNER], ALU.mult)\
                    .then_inc(hid_ready, 1)
                if i is not None:
                    dve.wait_ge(scattered[u], 16 * i)
                nc.vector.tensor_copy(scol[:, u:u + 1], SIDX[:, bass.ds(t, 1)].bitcast(U32)).then_inc(scol_ready, 1)
                dve.wait_ge(hid_tr, t + 1 + AHEAD)
                dve.wait_ge(dn_mm, t + 1)
                nc.vector.tensor_copy(hidT[u % 2], pY[:, u % 2, 0:P]).then_inc(hidT_ready, 1)
                dve.wait_ge(dn_mm, t + 1 + AHEAD)
                nc.vector.tensor_copy(res[u], pC[:, (u % 2) * 512:(u % 2) * 512 + C]).then_inc(res_ready, 1)

            for u in range(NB):
                gather_column(u, u)
            for u in range(NB):
                tile(u, u, None)
                dve.wait_ge(gathered[u], 16)
                gather_column(u + NB, u)
            with dve.Fori(1, NTILE // NB - 1) as i:
                for u in range(NB):
                    tile(NB * i + u, u, i)
                    dve.wait_ge(gathered[u], 16 * i + 16)
                    gather_column(NB * i + u + NB, u)
            for u in range(NB):
                tile(NTILE - NB + u, u, NTILE // NB - 1)

            for n in range(B):
                dve.wait_ge(z_in[n % NZ], 16 * (n // NZ + 1))
                for k in range(TOPK):
                    if k:
                        dve.wait_ge(comb, TOPK * n + k)
                    nc.vector.scalar_tensor_tensor(X2[:, n, :], z_buf[n % NZ][:, k * C:(k + 1) * C],
                                                   WT[:, n, k:k + 1], X2[:, n, :], ALU.mult, ALU.add)\
                        .then_inc(comb, 1)


_OUTS = [((B, T, C), "float32")]


def kernel(**inputs):
    import numpy as np
    import concourse.bacc as bacc
    from concourse import mybir as mb
    from concourse.bass_utils import run_bass_kernel_spmd

    a = {k: np.asarray(v) for k, v in inputs.items()}
    f32 = np.float32

    def chunked(w):
        return np.ascontiguousarray(w.reshape(NC, P, -1).transpose(1, 0, 2))

    wq, wk, wv, wo, wig, wog = (a[f"L0_attn_{n}"].T for n in ("Wq", "Wk", "Wv", "Wo", "Wig", "Wog"))
    wg = np.repeat(a["L0_attn_Wg"], HD, axis=0).T
    cols = np.stack([*a["L0_attn_conv_w"].T, a["L0_attn_conv_b"], a["L0_attn_b_ig"],
                     np.repeat(a["L0_attn_b_g"], HD), a["L0_attn_b_og"], a["L0_attn_gn_w"],
                     a["L0_attn_gn_b"]], axis=1)
    rows = np.broadcast_to(np.stack([a["L0_attn_mn_w"], a["L0_attn_mn_b"]]), (P, 2, C))
    padded = np.zeros((XH, P + C), f32)
    padded[:, P:] = a["L0_xattn_ssm_kernel"]
    toep = padded[:, P + np.arange(C)[None, :] - np.arange(P)[:, None]].transpose(1, 0, 2)
    ctx_t = a["ctx_2048"].reshape(NG, G, T, NC, P).transpose(0, 4, 3, 1, 2).reshape(NG, P, NC * G * T)
    w_gu = np.concatenate([a["L0_ffn_w_gate"], a["L0_ffn_w_up"]], axis=1)
    w_gu = w_gu.reshape(E, 2 * INNER, NC, P).transpose(3, 0, 2, 1).reshape(P, E * GUW)
    w_dn = a["L0_ffn_w_down"].transpose(2, 0, 1)
    eye = np.eye(P, dtype=f32)
    head = np.kron(np.eye(P // HD), np.ones((HD, HD))).astype(f32)
    consts = np.stack([eye, eye - head / f32(HD), np.ones((P, P), f32)], axis=1)
    iotas = np.zeros((P, 4, P), f32)
    iotas[:, 0] = np.arange(P)
    n, k = np.divmod(np.arange(B * TOPK), TOPK)
    iotas[:, 1, :B * TOPK] = (n * P)[None] * TOPK + np.arange(P)[:, None] * TOPK + k[None] + 1
    before = np.arange(E)[:, None] < np.arange(E)[None, :]
    iotas[:E, 2, :E] = before * P
    iotas[:E, 2, E:2 * E] = before | np.eye(E, dtype=bool)
    iotas[:, 3] = np.arange(P)[:, None] < np.arange(P)[None, :]

    data = {
        "x": a["x"], "ctx_t": ctx_t, "w_qk": chunked(np.concatenate([wq, wk], axis=1)), "w_v": chunked(wv),
        "w_ig": chunked(wig), "w_g": chunked(wg), "w_og": chunked(wog), "w_o": chunked(wo),
        "w_rt": chunked(a["L0_ffn_router_w"].T), "cols": chunked(cols), "rows": rows, "toep": toep,
        "dskip": np.broadcast_to(a["L0_xattn_D"], (P, XH)), "w_gu": w_gu, "w_dn": w_dn,
        "consts": consts, "iotas": iotas,
    }
    nc = bacc.Bacc("TRN2", target_bir_lowering=False, num_devices=1)
    arrays, args = {}, []
    for name, v in data.items():
        v = np.ascontiguousarray(v)
        arrays[f"in_{name}"] = v
        args.append(nc.dram_tensor(f"in_{name}", v.shape, mb.dt.from_np(v.dtype), kind="ExternalInput").ap())
    args.append(nc.dram_tensor("out_0", _OUTS[0][0], mb.dt.from_np(np.dtype("float32")), kind="ExternalOutput").ap())
    program(nc, *args)
    r = run_bass_kernel_spmd(nc, [arrays], core_ids=[0])
    return r.results[0]["out_0"]
```

```python
from contextlib import ExitStack

import concourse.bass as bass
from concourse import mybir

ALU = mybir.AluOpType
ACT = mybir.ActivationFunctionType
AX = mybir.AxisListType
F32 = mybir.dt.float32
BF16 = mybir.dt.bfloat16
I32 = mybir.dt.int32
U32 = mybir.dt.uint32

B, T, C = 16, 128, 256
P = 128
NC = C // P
NTOK = B * T
HEADS, HD = 16, 16
KC = 4
XH, XD = 16, 8
NPAIR = XD * (XD + 1) // 2
G = 4
NG = B // G
GT = G * T
E, TOPK, INNER = 32, 4, 128
NSLOT = NTOK * TOPK
NTILE = (NSLOT + E * (P - 1)) // P + 1
NTILE += -NTILE % 8
DLOW = 8
ELOW = 2
GUW = NC * 2 * INNER
LN_EPS = 1e-5
NB = 8
NR = 4
NHOT = 8
AHEAD = 2
NZ = 4
RT_SEL, RT_CUM, RT_STEPS = 10, 13, 15
PLAN_DONE = 20
FAR = 1 << 14


class Signal:

    def __init__(self, sem, per):
        self.sem, self.per = sem, per

    def now(self, g, k=None):
        return (g + 1) * self.per + (self.per if k is None else k)

    def before(self, g, k=None):
        return g * self.per + (self.per if k is None else k)


def pair_offset(s):
    return s * XD - s * (s - 1) // 2


def program(nc, x, ctx_t, w_qk, w_v, w_ig, w_g, w_og, w_o, w_rt, cols, rows, toep, dskip,
            w_gu, w_dn, consts, iotas, out):
    with ExitStack() as stack:
        def sb(name, shape, dt=F32):
            return stack.enter_context(nc.sbuf_tensor(name, shape, dt))

        def sem(name):
            return stack.enter_context(nc.semaphore(name))

        def signal(name, per):
            return Signal(sem(name), per)

        hn_dram = nc.dram_tensor("hn_scratch", [NTOK, C], F32, kind="Internal").ap()
        z_dram = nc.dram_tensor("z_scratch", [NSLOT, C], F32, kind="Internal").ap()

        X2 = sb("X2", [P, B, C])
        WQK = sb("WQK", [P, NC, 2 * C])
        WV = sb("WV", [P, NC, C])
        WIG = sb("WIG", [P, NC, C])
        WG = sb("WG", [P, NC, C])
        WOG = sb("WOG", [P, NC, C])
        WO = sb("WO", [P, NC, C])
        WRT = sb("WRT", [P, NC, E])
        COLS = sb("COLS", [P, NC, 10])
        ROWS = sb("ROWS", [P, 2, C])
        TOEP = sb("TOEP", [P, XH, C])
        DSK = sb("DSK", [P, XH])
        CST = sb("CST", [P, 3, P])
        IOT = sb("IOT", [P, 4, P])
        TRI = sb("TRI", [P, 2, P], BF16)
        WDN = sb("WDN", [P, E * C])
        WGU = sb("WGU", [P, E * GUW])
        taken = {"gu": ELOW * GUW, "dn": DLOW * C}

        def high(n, where="gu"):
            first = taken[where]
            taken[where] += n
            return (WGU if where == "gu" else WDN)[:, first:first + n]

        prod_f = high(G * XH * XD * XD)
        prod = prod_f.rearrange("p (q n) -> p q n", n=XD * XD)
        kvp_f = high(NC * G * XH * NPAIR)
        kvp = kvp_f.rearrange("p (q n) -> p q n", n=NPAIR)
        kvp_h = kvp_f.rearrange("p (c b h n) -> p c b h n", c=NC, b=G, h=XH)
        xnT = high(NC * G * (T + KC - 1)).rearrange("p (c b t) -> p c b t", c=NC, b=G)
        ig = high(NC * GT).rearrange("p (c t) -> p c t", c=NC)
        gam = high(NC * GT).rearrange("p (c t) -> p c t", c=NC)
        ctx_f = sb("ctx_f", [P, NC * G * XH * XD])
        ctxm = ctx_f[:, :].rearrange("p (q i) -> p q i", i=XD)
        YB = sb("YB", [P, NC * G * XH * NPAIR])
        yq = YB[:, :].rearrange("p (q n) -> p q n", n=NPAIR)
        yh = YB[:, :].rearrange("p (c b h n) -> p c b h n", c=NC, b=G, h=XH)

        def buf(name, where=None):
            t = high(G * C, where) if where else sb(name, [P, G * C])
            return t, t[:, :].rearrange("p (b c) -> p b c", b=G), t[:, :].rearrange("p (c t) -> p c t", c=NC)

        xn_f, xn, _ = buf("xn")
        y_f, _, y = buf("y")
        s_f, _, s_ = buf("sg", "gu")
        v_f, v, vC = buf("v")
        kv_f, kv, kvC = buf("kv", "gu")
        qn_f, qn, _ = buf("qn")
        bt_f, bt, btC = buf("bt", "gu")
        o_f, o, oC = buf("o")
        og_f, _, og = buf("og", "dn")
        qT_f, _, _ = buf("qT", "dn")
        cv_f, _, _ = buf("cv", "dn")
        hn_f, hn, _ = buf("hn", "dn")
        hT_f, _, hT = buf("hT", "dn")

        def per_head(f):
            return f.rearrange("p (r d) -> p r d", d=HD)

        st = sb("st", [P, 3, G, 6])
        mv = sb("mv", [P, 3, G, 2])
        rs = sb("rs", [P, 3, G])
        rstd = sb("rstd", [P, 3, G])
        nmean = sb("nmean", [P, 3, G])
        nmr = sb("nmr", [P, 3, G])
        half = sb("half", [P, G])
        ss = sb("ss", [P, 2 * G * HEADS])
        nqk = sb("nqk", [P, 2 * G * HEADS])
        rqk = sb("rqk", [P, 2 * G * HEADS])
        s2 = sb("s2", [P, G * HEADS])
        d2 = sb("d2", [P, G * HEADS])
        d3 = sb("d3", [P, G * HEADS])
        r2 = sb("r2", [P, G * HEADS])
        mu = sb("mu", [P, G * HEADS])
        s3 = sb("s3", [P, G * HEADS])
        r3 = sb("r3", [P, G * HEADS])
        lmax = sb("lmax", [P, G])
        lg = sb("lg", [P, G, E])
        pe_ = sb("pe_", [P, G, E])
        psm = sb("psm", [P, 2, G])
        pr = sb("pr", [P, G, E])
        m8 = sb("m8", [P, G, 8])
        ix = sb("ix", [P, G, 8], U32)
        ixf = sb("ixf", [P, G, TOPK])
        wsum = sb("wsum", [P, 2, G])
        WT = sb("WT", [P, B, TOPK])
        OH = sb("OH", [P, B, TOPK * E], BF16)
        sel = sb("sel", [P, G, E], BF16)
        selg = sb("selg", [P, E], BF16)
        cum = sb("cum", [P, E], BF16)
        posr = sb("posr", [P, B, TOPK])
        tmp_oh = sb("tmp_oh", [P, G * TOPK * E])
        big = TOEP[:, :, :].rearrange("p h l -> p (h l)")
        oh_prod = big[:, 0:B * TOPK * E].rearrange("p (q e) -> p q e", e=E)
        lo_hot = [big[:, 2048 + i * P:2048 + (i + 1) * P] for i in range(NHOT)]
        hi_hot = [big[:, 3072 + i * NTILE:3072 + (i + 1) * NTILE] for i in range(NHOT)]
        starts = sb("starts", [P, B * TOPK])
        qcol = sb("qcol", [P, 3, NHOT])
        posi = sb("posi", [P, 3, B * TOPK], I32)
        pos2 = sb("pos2", [P, 2, B * TOPK])
        ntf = sb("ntf", [E, 1])
        nti = sb("nti", [E, 2], I32)
        ntb = sb("ntb", [E, P])
        endt = sb("endt", [E, 1])
        over = xn_f[0:E, 6 * NTILE:7 * NTILE]
        etile = sb("etile", [1, NTILE + NB], I32)
        start = sb("start", [P, E])
        idx_t = xn_f[:, 0:3 * NTILE].rearrange("p (n t) -> p n t", n=3)
        GIDX = xn_f[:, 3 * NTILE:5 * NTILE].rearrange("p (n t) -> p n t", n=2).bitcast(I32)
        SIDX = xn_f[:, 5 * NTILE:6 * NTILE].bitcast(I32)
        gcol = sb("gcol", [P, NB], U32)
        scol = sb("scol", [P, NR], U32)

        def ybuf(k):
            return YB[:, k * C:(k + 1) * C]

        xg = [ybuf(i) for i in range(NB)]
        xgT = [ybuf(NB + i) for i in range(2)]
        res = [ybuf(NB + 2 + i) for i in range(NR)]
        act_g = [ybuf(NB + NR + 2)[:, i * P:(i + 1) * P] for i in range(2)]
        hid = [ybuf(NB + NR + 3)[:, i * P:(i + 1) * P] for i in range(2)]
        hidT = [ybuf(NB + NR + 4)[:, i * P:(i + 1) * P] for i in range(2)]

        pA, pB, pC = (stack.enter_context(nc.psum_tensor(n, [P, 1024], F32)) for n in ("pA", "pB", "pC"))
        pY = stack.enter_context(nc.psum_tensor("pY", [P, 2, 512], F32))

        WDN_E = WDN[:, :].rearrange("p (e n) -> p e n", n=C)
        WGU_E = WGU[:, :].rearrange("p (q n) -> p q n", n=2 * INNER)
        z_buf = [prod_f[:, i * TOPK * C:(i + 1) * TOPK * C] for i in range(NZ)]

        def tok(p):
            return p[:, :].rearrange("p (b c) -> p b c", b=G)

        def chan(p):
            return p[:, :].rearrange("p (c t) -> p c t", c=NC)

        ident = CST[:, 0, :]
        center = CST[:, 1, :]
        onesf = CST[:, 2, :]
        iota = IOT[:, 0, :]
        rownum = IOT[:, 1, 0:B * TOPK]
        tri_lt = IOT[0:E, 2, 0:E]
        tri_le = IOT[0:E, 2, E:2 * E]
        CONVB, BIG, BG, BOG, GNW, GNB = range(KC, KC + 6)

        const_in = [sem(f"const_in{i}") for i in range(6)]
        half_set = sem("half_set")
        toep_ready = sem("toep_ready")
        x_in = signal("x_in", 16)
        ctx_in = signal("ctx_in", 16)
        stats = [signal(f"stats{i}", G) for i in range(3)]
        aggr = [signal(f"aggr{i}", G) for i in range(3)]
        factor = [signal(f"factor{i}", 4) for i in range(3)]
        xn_ready = signal("xn_ready", 1)
        xn_tr = signal("xn_tr", 1)
        xnT_ready = signal("xnT_ready", 2)
        tap0 = signal("tap0", 2)
        conv = signal("conv", 6)
        sig_y = signal("sig_y", 1)
        xc_ready = signal("xc_ready", 1)
        v_mm = signal("v_mm", 1)
        k_mm = signal("k_mm", 1)
        q_mm = signal("q_mm", 1)
        v_out = signal("v_out", 1)
        ksq = signal("ksq", 1)
        qsq = signal("qsq", 1)
        ssum = signal("ssum", 2)
        ssmax = signal("ssmax", 1)
        nqk_ready = signal("nqk_ready", 1)
        rqk_ready = signal("rqk_ready", 1)
        kv_step = signal("kv_step", 1)
        kv_ready = signal("kv_ready", 1)
        qn_ready = signal("qn_ready", 1)
        qw_ready = signal("qw_ready", 1)
        qb_ready = signal("qb_ready", 1)
        ig_mm = signal("ig_mm", 1)
        gam_mm = signal("gam_mm", 1)
        ig_ready = signal("ig_ready", 2)
        gam_out = signal("gam_out", 2)
        gam_ready = signal("gam_ready", 1)
        kv_tr = signal("kv_tr", 1)
        bt_ready = signal("bt_ready", 1)
        mem_ready = signal("mem_ready", 2)
        og_mm = signal("og_mm", 1)
        og_ready = signal("og_ready", 2)
        mem_tr = signal("mem_tr", 1)
        memsq = signal("memsq", 1)
        memvar = signal("memvar", 2)
        d2_ready = signal("d2_ready", 1)
        r2_ready = signal("r2_ready", 1)
        o_step = signal("o_step", 7)
        osq = signal("osq", 1)
        ovar = signal("ovar", 2)
        d3_ready = signal("d3_ready", 1)
        r3_ready = signal("r3_ready", 1)
        o_tr = signal("o_tr", 1)
        oT_out = signal("oT_out", 2)
        oT_ready = signal("oT_ready", 1)
        wo_mm = signal("wo_mm", 1)
        x1_ready = signal("x1_ready", 1)
        q2_ready = signal("q2_ready", 1)
        q2_tr = signal("q2_tr", 1)
        q2T_ready = signal("q2T_ready", 1)
        pairs = signal("pairs", XD)
        y_mm = signal("y_mm", XH)
        y_out = signal("y_out", XH)
        prods = signal("prods", 2 * 15)
        redd = signal("redd", 2)
        y2_tr = signal("y2_tr", 1)
        x2_ready = signal("x2_ready", 1)
        h_ready = signal("h_ready", 1)
        normed = (xn_ready, q2_ready, h_ready)
        hn_stored = signal("hn_stored", 16)
        h_tr = signal("h_tr", 1)
        hT_ready = signal("hT_ready", 1)
        lg_mm = signal("lg_mm", 1)
        rt = signal("rt", RT_STEPS)
        ex_ready = signal("ex_ready", 1)
        rank_mm = signal("rank_mm", 1)
        gu_in = sem("gu_in")
        high_in = sem("high_in")
        cnt_mm = sem("cnt_mm")
        plan = sem("plan")
        start_mm = sem("start_mm")
        etile_mm = sem("etile_mm")
        lo_ready = sem("lo_ready")
        hi_even = sem("hi_even")
        hi_odd = sem("hi_odd")
        qcol_ready = sem("qcol_ready")
        id_mm = sem("id_mm")
        gcol_ready = sem("gcol_ready")
        scol_ready = sem("scol_ready")
        gathered = [sem(f"gathered{i}") for i in range(NB)]
        scattered = [sem(f"scattered{i}") for i in range(NR)]
        xg_tr = sem("xg_tr")
        xgT_ready = sem("xgT_ready")
        gu_mm = sem("gu_mm")
        silu_ready = sem("silu_ready")
        hid_ready = sem("hid_ready")
        hid_tr = sem("hid_tr")
        hidT_ready = sem("hidT_ready")
        dn_mm = sem("dn_mm")
        res_ready = sem("res_ready")
        z_in = [sem(f"z_in{i}") for i in range(NZ)]
        comb = sem("comb")
        out_stored = sem("out_stored")

        block = stack.enter_context(nc.Block())

        @block.sync
        def _(sp):
            sp.sem_inc(x_in.sem, 16)
            sp.sem_inc(ctx_in.sem, 16)
            sp.sem_inc(hn_stored.sem, 16)
            sp.dma_start(X2[:, 0:G, :], x[0:G].rearrange("b t c -> t b c")).then_inc(x_in.sem, 16)
            for n, loads in enumerate((((CST, consts), (COLS, cols)), ((WV, w_v), (WQK, w_qk)),
                                       ((WIG, w_ig), (WG, w_g), (WOG, w_og)), ((ROWS, rows), (IOT, iotas), (DSK, dskip)),
                                       ((TOEP, toep),), ((WO, w_o), (WRT, w_rt)))):
                if n == 2:
                    sp.dma_start(ctx_f[:], ctx_t[0]).then_inc(ctx_in.sem, 16)
                for dst, src in loads:
                    sp.dma_start(dst[:], src).then_inc(const_in[n], 16)

            def load_group(g):
                sp.wait_ge(x_in.sem, x_in.now(g - 1))
                sp.nop(nofuse=True)
                sp.dma_start(X2[:, bass.ds(G * g, G), :],
                             x[bass.ds(G * g, G)].rearrange("b t c -> t b c")).then_inc(x_in.sem, 16)
                sp.wait_ge(ctx_in.sem, ctx_in.now(g - 1))
                sp.wait_ge(pairs.sem, pairs.now(g - 1))
                sp.nop(nofuse=True)
                sp.dma_start(ctx_f[:], ctx_t[bass.ds(g, 1)].rearrange("g p n -> (g p) n"))\
                    .then_inc(ctx_in.sem, 16)

            def store_hn(g):
                sp.wait_ge(h_ready.sem, h_ready.now(g))
                sp.wait_ge(hn_stored.sem, hn_stored.before(g))
                sp.nop(nofuse=True)
                sp.dma_start(hn_dram[bass.ds(GT * g, GT), :].rearrange("(b t) c -> t b c", t=T), hn)\
                    .then_inc(hn_stored.sem, 16)

            load_group(1)
            with sp.Fori(2, NG) as g:
                load_group(g)
                store_hn(g - 2)
            store_hn(NG - 2)
            last = NG - 1
            sp.wait_ge(redd.sem, redd.now(last))
            sp.wait_ge(y_mm.sem, y_mm.now(last))
            sp.wait_ge(o_tr.sem, o_tr.now(last))
            sp.wait_ge(oT_ready.sem, oT_ready.now(last))
            sp.dma_start(WGU[:, ELOW * GUW:], w_gu[:, ELOW * GUW:]).then_inc(high_in, 16)
            store_hn(last)
            sp.wait_ge(y2_tr.sem, y2_tr.now(last))
            sp.wait_ge(lg_mm.sem, lg_mm.now(last))
            sp.wait_ge(hn_stored.sem, hn_stored.now(last))
            sp.dma_start(WDN[:, DLOW * C:], w_dn[:, DLOW * C:]).then_inc(high_in, 16)
            for i in range(NR):
                sp.wait_ge(scattered[i], 16 * (NTILE // NR))
            z_v = z_dram.rearrange("(n p k) c -> n p (k c)", p=P, k=TOPK)
            for n in range(B):
                if n >= NZ:
                    sp.wait_ge(comb, TOPK * (n - NZ + 1))
                    sp.dma_start(out[n - NZ], X2[:, n - NZ, :]).then_inc(out_stored, 16)
                sp.dma_start(z_buf[n % NZ], z_v[n]).then_inc(z_in[n % NZ], 16)
            for n in range(B - NZ, B):
                sp.wait_ge(comb, TOPK * (n + 1))
                sp.dma_start(out[n], X2[:, n, :]).then_inc(out_stored, 16)
            sp.wait_ge(out_stored, 16 * B)

        @block.gpsimd
        def _(pool):
            for s in (*factor, qw_ready, qb_ready, gam_ready, pairs):
                pool.sem_inc(s.sem, s.per)
            pool.memset(half[:], -0.5).then_inc(half_set, 1)
            pool.memset(xnT[:, :, :, 0:KC - 1], 0.0).then_inc(half_set, 1)
            pool.wait_ge(half_set, 2)

            def norm_factors(g, i):
                f = factor[i]
                pool.wait_ge(aggr[i].sem, aggr[i].now(g))
                pool.wait_ge(normed[i].sem, normed[i].before(g))
                pool.nop(nofuse=True)
                nc.gpsimd.tensor_scalar(rs[:, i, :], mv[:, i, :, 1], LN_EPS, None, ALU.add).then_inc(f.sem, 1)
                nc.gpsimd.tensor_scalar(nmean[:, i, :], mv[:, i, :, 0], -1.0, None, ALU.mult).then_inc(f.sem, 1)
                pool.wait_ge(f.sem, f.now(g, 2))
                pool.nop(nofuse=True)
                nc.gpsimd.tensor_tensor(rstd[:, i, :], rs[:, i, :], half[:, 0:G], ALU.pow).then_inc(f.sem, 1)
                pool.wait_ge(f.sem, f.now(g, 3))
                pool.nop(nofuse=True)
                nc.gpsimd.tensor_tensor(nmr[:, i, :], nmean[:, i, :], rstd[:, i, :], ALU.mult).then_inc(f.sem, 1)

            def body(g, a, b):
                if a:
                    norm_factors(g, 0)
                    pool.wait_ge(ctx_in.sem, ctx_in.now(g))
                    pool.wait_ge(y_mm.sem, y_mm.before(g))
                    pool.nop(nofuse=True)
                    for s in range(XD):
                        n, off = XD - s, pair_offset(s)
                        nc.gpsimd.tensor_tensor(kvp[:, :, off:off + n], ctxm[:, :, 0:n], ctxm[:, :, s:XD],
                                                ALU.mult).then_inc(pairs.sem, 1)
                    pool.wait_ge(gam_out.sem, gam_out.now(g))
                    pool.nop(nofuse=True)
                    pool.memset(gam[:, :, :].rearrange("p c (b t) -> p (c b) t", t=T)[:, :, 0:1], 0.0)\
                        .then_inc(gam_ready.sem, 1)
                    pool.wait_ge(const_in[3], 16 * 3)
                    pool.wait_ge(qn_ready.sem, qn_ready.now(g))
                    pool.wait_ge(kv_step.sem, kv_step.now(g))
                    pool.nop(nofuse=True)
                    nc.gpsimd.tensor_tensor(v, qn, ROWS[:, 0:1, :].to_broadcast([P, G, C]), ALU.mult)\
                        .then_inc(qw_ready.sem, 1)
                    nc.gpsimd.tensor_tensor(qn, qn, ROWS[:, 1:2, :].to_broadcast([P, G, C]), ALU.mult)\
                        .then_inc(qb_ready.sem, 1)
                if b:
                    norm_factors(g - 1, 2)
                if a:
                    norm_factors(g, 1)

            body(0, True, False)
            pool.dma_start(WGU[:, 0:ELOW * GUW], w_gu[:, 0:ELOW * GUW]).then_inc(gu_in, 16)
            pool.dma_start(WDN[:, 0:DLOW * C], w_dn[:, 0:DLOW * C]).then_inc(gu_in, 16)
            with pool.Fori(1, NG) as g:
                body(g, True, True)
            body(NG, False, True)

            with pool.Fori(0, B * TOPK // NHOT) as r:
                pool.wait_ge(qcol_ready, 3 * r + 3)
                pool.wait_ge(id_mm, NHOT * r + NHOT)
                pool.nop(nofuse=True)
                for u in range(1, NHOT, 2):
                    nc.gpsimd.tensor_scalar(hi_hot[u], IOT[:, 0, 0:NTILE], qcol[:, 0, u:u + 1],
                                            qcol[:, 2, u:u + 1], ALU.is_equal, ALU.mult).then_inc(hi_odd, 1)

            def gather(t, u):
                pool.wait_ge(gcol_ready, t + 1)
                pool.nop(nofuse=True)
                pool.indirect_dma_start(out=xg[u], out_offset=None, in_=hn_dram,
                                        in_offset=bass.IndirectOffsetOnAxis(gcol[:, u:u + 1], 0))\
                    .then_inc(gathered[u], 16)

            def scatter(t, u):
                pool.wait_ge(scol_ready, t + 1)
                pool.wait_ge(res_ready, t + 1 + AHEAD)
                pool.nop(nofuse=True)
                pool.indirect_dma_start(out=z_dram, out_offset=bass.IndirectOffsetOnAxis(scol[:, u:u + 1], 0),
                                        in_=res[u], in_offset=None, bounds_check=NSLOT - 1,
                                        oob_is_err=False).then_inc(scattered[u], 16)

            pool.wait_ge(hn_stored.sem, hn_stored.now(NG - 1))
            for u in range(NB):
                gather(u, u)
            with pool.Fori(0, NTILE // NB - 1) as i:
                for u in range(NB):
                    pool.wait_ge(xg_tr, NB * i + u + 1)
                    gather(NB * i + u + NB, u)
                    scatter(NB * i + u, u % NR)
            for u in range(NB):
                scatter(NTILE - NB + u, u % NR)

        @block.tensor
        def _(pe):
            for s in (xn_tr, v_mm, k_mm, q_mm, ig_mm, gam_mm, kv_tr, og_mm, mem_tr, o_tr, wo_mm, q2_tr,
                      y_mm, y2_tr, h_tr, lg_mm, rank_mm):
                pe.sem_inc(s.sem, s.per)
            pe.sem_inc(id_mm, NHOT)
            for s in (gu_mm, hid_tr, dn_mm):
                pe.sem_inc(s, AHEAD)

            def transposed(src, dst, signal_):
                for c in range(NC):
                    for b in range(G):
                        last = nc.tensor.transpose(chan(dst)[:, c, b * T:(b + 1) * T],
                                                   src[:, b, c * P:(c + 1) * P], ident)
                last.then_inc(signal_.sem, 1)

            def by_channel(dst, w, rhs, signal_):
                for c in range(NC):
                    for k in range(NC):
                        last = nc.tensor.matmul(chan(dst)[:, c, :], w[:, k, c * P:(c + 1) * P], rhs[:, k, :],
                                                start=(k == 0), stop=(k == NC - 1))
                last.then_inc(signal_.sem, 1)

            def by_token(dst, lhs, w, signal_):
                for b in range(G):
                    for k in range(NC):
                        last = nc.tensor.matmul(tok(dst)[:, b, :], lhs(k, b), w[:, k, :],
                                                start=(k == 0), stop=(k == NC - 1))
                last.then_inc(signal_.sem, 1)

            def toeplitz(g, heads):
                for h in heads:
                    pe.wait_ge(y_out.sem, y_out.now(g, h - 1))
                    for lc in range(NC):
                        for mc in range(lc + 1):
                            last = nc.tensor.matmul(
                                pY[:, h % 2, lc * G * NPAIR:(lc + 1) * G * NPAIR]
                                .rearrange("p (b n) -> p b n", n=NPAIR),
                                TOEP[:, h, (lc - mc) * P:(lc - mc + 1) * P], kvp_h[:, mc, :, h, :],
                                start=(mc == 0), stop=(mc == lc))
                    last.then_inc(y_mm.sem, 1)

            def body(g, a, b):
                def feature(k, b):
                    return xnT[:, k, b, KC - 1:]

                if a:
                    pe.wait_ge(const_in[0], 16 * 2)
                    pe.wait_ge(xn_ready.sem, xn_ready.now(g))
                    pe.wait_ge(q2T_ready.sem, q2T_ready.before(g))
                    transposed(xn, pA, xn_tr)
                    pe.wait_ge(const_in[1], 16 * 2)
                    pe.wait_ge(half_set, 2)
                    pe.wait_ge(xnT_ready.sem, xnT_ready.now(g))
                    pe.wait_ge(x1_ready.sem, x1_ready.before(g))
                    by_token(pB, feature, WV[:, :, :], v_mm)
                    pe.wait_ge(rt.sem, rt.before(g - 1))
                    by_token(pC, feature, WQK[:, :, C:2 * C], k_mm)
                    by_token(pA, feature, WQK[:, :, 0:C], q_mm)
                    pe.wait_ge(const_in[2], 16 * 3)
                    pe.wait_ge(xc_ready.sem, xc_ready.now(g))
                    pe.wait_ge(v_out.sem, v_out.now(g))
                    by_channel(pB, WIG, y, ig_mm)
                    pe.wait_ge(kv_step.sem, kv_step.now(g))
                    pe.wait_ge(ksq.sem, ksq.now(g))
                    by_channel(pC, WG, y, gam_mm)
                    pe.wait_ge(kv_ready.sem, kv_ready.now(g))
                    pe.wait_ge(qn_ready.sem, qn_ready.now(g))
                    transposed(kv, pA, kv_tr)
                    pe.wait_ge(ig_ready.sem, ig_ready.now(g))
                    by_channel(pB, WOG, y, og_mm)
                    pe.wait_ge(mem_ready.sem, mem_ready.now(g))
                    pe.wait_ge(gam_out.sem, gam_out.now(g))
                    for b_ in range(G):
                        for c in range(NC):
                            last = nc.tensor.matmul(tok(pC)[:, b_, c * P:(c + 1) * P],
                                                    s_[:, c, b_ * T:(b_ + 1) * T], center, start=True, stop=True)
                    last.then_inc(mem_tr.sem, 1)
                if b:
                    pe.wait_ge(redd.sem, redd.now(g - 1))
                    for b_ in range(G):
                        for c in range(NC):
                            last = nc.tensor.transpose(tok(pA)[:, b_, c * P:(c + 1) * P],
                                                       cv_f[:, (c * G + b_) * P:(c * G + b_ + 1) * P], ident)
                    last.then_inc(y2_tr.sem, 1)
                if a:
                    pe.wait_ge(toep_ready, 1)
                    pe.wait_ge(pairs.sem, pairs.now(g))
                    toeplitz(g, range(XH // 2))
                    pe.wait_ge(o_step.sem, o_step.now(g))
                    if b:
                        pe.wait_ge(x2_ready.sem, x2_ready.now(g - 1))
                    transposed(o, pA, o_tr)
                    pe.wait_ge(const_in[5], 16 * 2)
                    pe.wait_ge(oT_ready.sem, oT_ready.now(g))
                    by_token(pB, lambda k, b: y[:, k, b * T:(b + 1) * T], WO, wo_mm)
                if b:
                    pe.wait_ge(h_ready.sem, h_ready.now(g - 1))
                    if not a:
                        pe.wait_ge(x2_ready.sem, x2_ready.now(g - 1))
                    transposed(hn, pA, h_tr)
                    pe.wait_ge(hT_ready.sem, hT_ready.now(g - 1))
                    for b_ in range(G):
                        for k in range(NC):
                            last = nc.tensor.matmul(pC[:, b_ * E:(b_ + 1) * E], hT[:, k, b_ * T:(b_ + 1) * T],
                                                    WRT[:, k, :], start=(k == 0), stop=(k == NC - 1))
                    last.then_inc(lg_mm.sem, 1)
                if a:
                    pe.wait_ge(q2_ready.sem, q2_ready.now(g))
                    if not b:
                        pe.wait_ge(oT_out.sem, oT_out.now(g))
                    transposed(xn, pA, q2_tr)
                    toeplitz(g, range(XH // 2, XH))
                if b:
                    pe.wait_ge(rt.sem, rt.now(g - 1, RT_SEL))
                    for b_ in range(G):
                        bank = pC[:, 512 + b_ * E:512 + (b_ + 1) * E]
                        nc.tensor.matmul(bank, TRI[:, 0, :], sel[:, b_, :], start=True, stop=False)
                        for e_ in range(b_):
                            nc.tensor.matmul(bank, TRI[:, 1, :], sel[:, e_, :], start=False, stop=False)
                        last = nc.tensor.matmul(bank, TRI[:, 1, :], cum[:, :], start=False, stop=True)
                    last.then_inc(rank_mm.sem, 1)

            body(0, True, False)
            with pe.Fori(1, NG) as g:
                body(g, True, True)
            body(NG, False, True)

            pe.wait_ge(rt.sem, rt.now(NG - 1, RT_CUM))
            nc.tensor.matmul(pB[0:E, 0:1], cum[:, :], TRI[:, 1, 0:1], start=True, stop=True).then_inc(cnt_mm, 1)
            pe.wait_ge(plan, 6)
            nc.tensor.matmul(pA[:, 0:E], ntb[:, :], tri_lt, start=True, stop=True)
            nc.tensor.matmul(pA[0:E, 512:513], tri_le, ntf[:, :], start=True, stop=True).then_inc(start_mm, 1)
            pe.wait_ge(plan, 10)
            nc.tensor.matmul(pB[0:1, 0:NTILE], onesf[0:E, 0:1], over, start=True, stop=True).then_inc(etile_mm, 1)

            def number_rows(r, first=False, last=False):
                for u in range(NHOT):
                    pe.wait_ge(lo_ready, NHOT * r + u + 1)
                    if u % 2 == 0:
                        pe.wait_ge(hi_even, NHOT // 2 * r + u // 2 + 1)
                    else:
                        pe.wait_ge(hi_odd, NHOT // 2 * r + u // 2 + 1)
                    nc.tensor.matmul(pA[:, 0:NTILE], lo_hot[u], hi_hot[u], start=(first and u == 0),
                                     stop=(last and u == NHOT - 1)).then_inc(id_mm, 1)

            rounds = B * TOPK // NHOT
            pe.wait_ge(plan, 11)
            number_rows(0, first=True)
            with pe.Fori(1, rounds - 1) as r:
                number_rows(r)
            number_rows(rounds - 1, last=True)

            def rows_T(u):
                for k in range(NC):
                    last = nc.tensor.transpose(pA[:, (u % 2) * 512 + k * P:(u % 2) * 512 + (k + 1) * P],
                                               xg[u % NB][:, k * P:(k + 1) * P], ident)
                last.then_inc(xg_tr, 1)

            def gate_up(t, u, e):
                pe.wait_ge(xgT_ready, t + 1 + AHEAD)
                pe.wait_ge(hid_ready, t + 1)
                for k in range(NC):
                    last = nc.tensor.matmul(pB[:, (u % 2) * 512:(u % 2) * 512 + 2 * INNER],
                                            xgT[u % 2][:, k * P:(k + 1) * P], WGU_E[:, bass.ds(e * NC + k, 1), :],
                                            start=(k == 0), stop=(k == NC - 1))
                last.then_inc(gu_mm, 1)

            def hidden_T(t, u):
                pe.wait_ge(hid_ready, t + 1 + AHEAD)
                nc.tensor.transpose(pY[:, u % 2, 0:P], hid[u % 2], ident).then_inc(hid_tr, 1)

            def down(t, u, e):
                pe.wait_ge(hidT_ready, t + 1 + AHEAD)
                pe.wait_ge(res_ready, t + 1)
                nc.tensor.matmul(pC[:, (u % 2) * 512:(u % 2) * 512 + C], hidT[u % 2],
                                 WDN_E[:, bass.ds(e, 1), :], start=True, stop=True).then_inc(dn_mm, 1)

            def experts_of(t, n):
                _, e = nc.values_load_multi_w_load_instructions(
                    etile[0:1, bass.ds(t, n)], engines=(mybir.EngineType.PE,), min_val=0, max_val=E - 1,
                    skip_runtime_bounds_check_because="the plan clamps them")
                return e

            pe.wait_ge(plan, PLAN_DONE)
            pe.wait_ge(gu_in, 32)
            pe.wait_ge(high_in, 32)
            pe.wait_ge(gathered[0], 16)
            rows_T(0)
            e = experts_of(0, 1)
            gate_up(0, 0, e[0])
            pe.wait_ge(gathered[1], 16)
            rows_T(1)

            def round_(i, t0, last):
                e = experts_of(t0, NB if last else NB + 1)
                for u in range(NB):
                    t = t0 + u
                    if not (last and u >= NB - 1):
                        gate_up(t + 1, u + 1, e[u + 1])
                    hidden_T(t, u)
                    if not (last and u >= NB - 2):
                        pe.wait_ge(gathered[(u + 2) % NB], 16 * i + 16 * (1 + (u + 2) // NB))
                        rows_T(u + 2)
                    down(t, u, e[u])

            with pe.Fori(0, NTILE // NB - 1) as i:
                round_(i, NB * i, False)
            round_(NTILE // NB - 1, NTILE - NB, True)

        @block.scalar
        def _(act):
            for s in (xn_ready, q2_ready, h_ready, xnT_ready, tap0, sig_y, v_out, ksq, qsq, nqk_ready, ig_ready,
                      gam_out, og_ready, memsq, d2_ready, osq, d3_ready, oT_out, q2T_ready, y_out, hT_ready,
                      ex_ready):
                act.sem_inc(s.sem, s.per)
            act.sem_inc(xgT_ready, AHEAD)
            act.sem_inc(silu_ready, AHEAD)

            def evict_y(g, heads):
                for h in heads:
                    act.wait_ge(y_mm.sem, y_mm.now(g, h + 1))
                    nc.scalar.activation(yh[:, :, :, h, :],
                                         pY[:, h % 2, 0:NC * G * NPAIR].rearrange("p (c b n) -> p c b n", c=NC, b=G),
                                         ACT.Copy).then_inc(y_out.sem, 1)

            def normalize(g, dst, i):
                act.wait_ge(factor[i].sem, factor[i].now(g))
                act.nop(nofuse=True)
                for b in range(G):
                    last = nc.scalar.activation(dst[:, b, :], X2[:, bass.ds(G * g + b, 1), :]
                                                .rearrange("p b c -> p (b c)"), ACT.Identity,
                                                scale=rstd[:, i, b:b + 1], bias=nmr[:, i, b:b + 1])
                last.then_inc(normed[i].sem, 1)

            def body(g, a, b):
                if a:
                    normalize(g, xn, 0)
                    act.wait_ge(const_in[0], 16 * 2)
                    act.wait_ge(xn_tr.sem, xn_tr.now(g))
                    for c in range(NC):
                        nc.scalar.activation(xnT[:, c, :, KC - 1:],
                                             chan(pA)[:, c, :].rearrange("p (b t) -> p b t", b=G),
                                             ACT.Copy).then_inc(xnT_ready.sem, 1)
                    for c in range(NC):
                        act.wait_ge(xnT_ready.sem, xnT_ready.now(g, c + 1))
                        nc.scalar.activation(y[:, c, :].rearrange("p (b t) -> p b t", b=G), xnT[:, c, :, KC - 1:],
                                             ACT.Identity, scale=COLS[:, c, KC - 1:KC],
                                             bias=COLS[:, c, CONVB:CONVB + 1]).then_inc(tap0.sem, 1)
                    act.wait_ge(v_mm.sem, v_mm.now(g))
                    nc.scalar.activation(v_f[:, :], pB[:, :], ACT.Copy).then_inc(v_out.sem, 1)
                    act.wait_ge(k_mm.sem, k_mm.now(g))
                    nc.scalar.activation(o_f[:, :], pC[:, :], ACT.Square).then_inc(ksq.sem, 1)
                    act.wait_ge(q_mm.sem, q_mm.now(g))
                    nc.scalar.activation(bt_f[:, :], pA[:, :], ACT.Square).then_inc(qsq.sem, 1)
                    act.wait_ge(ssmax.sem, ssmax.now(g))
                    nc.scalar.activation(nqk[:], ss[:], ACT.Sqrt).then_inc(nqk_ready.sem, 1)
                    act.wait_ge(conv.sem, conv.now(g))
                    nc.scalar.activation(s_f[:, :], y_f[:, :], ACT.Sigmoid).then_inc(sig_y.sem, 1)
                    for mm, src, dst, bias, ready in ((ig_mm, pB, ig, BIG, ig_ready), (gam_mm, pC, gam, BG, gam_out),
                                                      (og_mm, pB, og, BOG, og_ready)):
                        act.wait_ge(mm.sem, mm.now(g))
                        for c in range(NC):
                            nc.scalar.activation(dst[:, c, :], chan(src)[:, c, :], ACT.Sigmoid,
                                                 bias=COLS[:, c, bias:bias + 1]).then_inc(ready.sem, 1)
                    act.wait_ge(mem_tr.sem, mem_tr.now(g))
                    nc.scalar.activation(kv_f[:, :], pC[:, :], ACT.Square).then_inc(memsq.sem, 1)
                    act.wait_ge(memvar.sem, memvar.now(g))
                    nc.scalar.activation(d2[:], s2[:], ACT.Sqrt).then_inc(d2_ready.sem, 1)
                    act.wait_ge(prods.sem, prods.before(g))
                    evict_y(g, range(XH // 2))
                    act.wait_ge(o_step.sem, o_step.now(g, 6))
                    nc.scalar.activation(kv_f[:, :], o_f[:, :], ACT.Square).then_inc(osq.sem, 1)
                    act.wait_ge(ovar.sem, ovar.now(g))
                    nc.scalar.activation(d3[:], s3[:], ACT.Sqrt).then_inc(d3_ready.sem, 1)
                    act.wait_ge(o_tr.sem, o_tr.now(g))
                    for c in range(NC):
                        nc.scalar.activation(y[:, c, :], chan(pA)[:, c, :], ACT.Identity,
                                             scale=COLS[:, c, GNW:GNW + 1],
                                             bias=COLS[:, c, GNB:GNB + 1]).then_inc(oT_out.sem, 1)
                if b:
                    act.wait_ge(hn_stored.sem, hn_stored.before(g - 1))
                    normalize(g - 1, hn, 2)
                    act.wait_ge(h_tr.sem, h_tr.now(g - 1))
                    nc.scalar.activation(hT_f[:, :], pA[:, :], ACT.Copy).then_inc(hT_ready.sem, 1)
                if a:
                    normalize(g, xn, 1)
                    act.wait_ge(q2_tr.sem, q2_tr.now(g))
                    nc.scalar.activation(qT_f[:, :], pA[:, :], ACT.Copy).then_inc(q2T_ready.sem, 1)
                if b:
                    act.wait_ge(rt.sem, rt.now(g - 1, 2))
                    nc.scalar.activation(pe_[:], lg[:], ACT.Exp).then_inc(ex_ready.sem, 1)
                if a:
                    evict_y(g, range(XH // 2, XH))

            body(0, True, False)
            with act.Fori(1, NG) as g:
                body(g, True, True)
            body(NG, False, True)

            def rows_out(t, u):
                act.wait_ge(xg_tr, t + 1)
                act.wait_ge(gu_mm, t + 1)
                nc.scalar.activation(xgT[u % 2], pA[:, (u % 2) * 512:(u % 2) * 512 + C], ACT.Copy)\
                    .then_inc(xgT_ready, 1)

            def gate(t, u):
                act.wait_ge(gu_mm, t + 1 + AHEAD)
                act.wait_ge(hid_ready, t + 1)
                nc.scalar.activation(act_g[u % 2], pB[:, (u % 2) * 512:(u % 2) * 512 + INNER], ACT.Silu)\
                    .then_inc(silu_ready, 1)

            with act.Fori(0, NTILE // NB) as i:
                for u in range(NB):
                    rows_out(NB * i + u, u)
                    gate(NB * i + u, u)

        @block.vector
        def _(dve):
            for s in (*stats, *aggr, conv, xc_ready, ssum, ssmax, rqk_ready, kv_step, kv_ready,
                      qn_ready, bt_ready, mem_ready, memvar, r2_ready, o_step, ovar, r3_ready, oT_ready, x1_ready,
                      prods, redd, x2_ready, rt):
                dve.sem_inc(s.sem, s.per)
            for s in (hid_ready, hidT_ready, res_ready):
                dve.sem_inc(s, AHEAD)
            nc.vector.memset(cum[:], 0.0).then_inc(plan, 1)
            nc.vector.memset(TRI[:, 1, :], 1.0).then_inc(plan, 1)

            def x2_of(g, b=None):
                return X2[:, bass.ds(G * g, G), :] if b is None else \
                    X2[:, bass.ds(G * g + b, 1), :].rearrange("p b c -> p (b c)")

            def statistics(g, i):
                dve.wait_ge(factor[i].sem, factor[i].before(g))
                dve.nop(nofuse=True)
                for b in range(G):
                    nc.vector.bn_stats(st[:, i, b, :], x2_of(g, b)).then_inc(stats[i].sem, 1)
                dve.wait_ge(stats[i].sem, stats[i].now(g))
                dve.nop(nofuse=True)
                for b in range(G):
                    nc.vector.bn_aggr(mv[:, i, b, :], st[:, i, b, :]).then_inc(aggr[i].sem, 1)

            nq = G * XH
            qT = qT_f[:, :].rearrange("p (q i) -> p q i", i=XD)

            def products(g, lc, first, last):
                rows_ = slice(lc * nq, (lc + 1) * nq)
                for s in range(first, last):
                    n, off = XD - s, pair_offset(s)
                    conv_pairs = yq[:, rows_, off:off + n]
                    nc.vector.tensor_tensor(prod[:, :, s * XD:s * XD + n * (XD + 1) - XD:XD + 1], conv_pairs,
                                            qT[:, rows_, 0:n], ALU.mult).then_inc(prods.sem, 1)
                    if s:
                        nc.vector.tensor_tensor(prod[:, :, s:s + n * (XD + 1) - XD:XD + 1], conv_pairs,
                                                qT[:, rows_, s:XD], ALU.mult).then_inc(prods.sem, 1)

            def sum_products(g, lc):
                dve.wait_ge(prods.sem, prods.now(g, 15 * (lc + 1)))
                nc.vector.tensor_reduce(cv_f[:, lc * nq * XD:(lc + 1) * nq * XD],
                                        prod_f.rearrange("p (r i) -> p r i", i=XD), AX.X, ALU.add)\
                    .then_inc(redd.sem, 1)

            def bc(f, n):
                return f.rearrange("p (b o) -> p b o", o=1).to_broadcast([P, G, n])

            def small(f):
                return f[:, :].rearrange("p (r o) -> p r o", o=1).to_broadcast([P, G * HEADS, HD])

            def body(g, a, b):
                done = [0]

                def link(ins, n=1):
                    done[0] += n
                    ins.then_inc(rt.sem, n)
                    dve.wait_ge(rt.sem, rt.now(g - 1, done[0]))
                    dve.nop(nofuse=True)

                if a:
                    dve.wait_ge(x_in.sem, x_in.now(g))
                    statistics(g, 0)
                if b:
                    dve.wait_ge(q2T_ready.sem, q2T_ready.now(g - 1))
                    dve.wait_ge(y_out.sem, y_out.now(g - 1))
                    products(g - 1, 0, 0, XD)
                if a:
                    for j in range(1, KC):
                        for c in range(NC):
                            if j == 1:
                                dve.wait_ge(tap0.sem, tap0.now(g, c + 1))
                            else:
                                dve.wait_ge(conv.sem, conv.now(g, 2 * (j - 1) - 1 + c))
                            yc = y[:, c, :].rearrange("p (b t) -> p b t", b=G)
                            nc.vector.scalar_tensor_tensor(yc, xnT[:, c, :, KC - 1 - j:KC - 1 - j + T],
                                                           COLS[:, c, KC - 1 - j:KC - j], yc, ALU.mult, ALU.add)\
                                .then_inc(conv.sem, 1)
                    if not b:
                        dve.wait_ge(const_in[3], 16 * 3)
                        dve.wait_ge(const_in[4], 16)
                        for h in range(XH):
                            last = nc.vector.scalar_tensor_tensor(TOEP[:, h, 0:P], ident, DSK[:, h:h + 1],
                                                                  TOEP[:, h, 0:P], ALU.mult, ALU.add)
                        last.then_inc(toep_ready, 1)
                        nc.vector.tensor_copy(TRI[:, 0, :], IOT[:, 3, :]).then_inc(toep_ready, 1)
                    dve.wait_ge(ksq.sem, ksq.now(g))
                    nc.vector.tensor_reduce(ss[:, G * HEADS:], per_head(o_f[:, :]), AX.X, ALU.add)\
                        .then_inc(ssum.sem, 1)
                    dve.wait_ge(qsq.sem, qsq.now(g))
                    nc.vector.tensor_reduce(ss[:, 0:G * HEADS], per_head(bt_f[:, :]), AX.X, ALU.add)\
                        .then_inc(ssum.sem, 1)
                    dve.wait_ge(ssum.sem, ssum.now(g))
                    nc.vector.tensor_scalar(ss[:], ss[:], 1e-24, None, ALU.max).then_inc(ssmax.sem, 1)
                    dve.wait_ge(v_out.sem, v_out.now(g))
                    nc.vector.tensor_tensor(kv_f[:, :], pC[:, :], v_f[:, :], ALU.mult).then_inc(kv_step.sem, 1)
                    dve.wait_ge(nqk_ready.sem, nqk_ready.now(g))
                    nc.vector.reciprocal(rqk[:], nqk[:]).then_inc(rqk_ready.sem, 1)
                    dve.wait_ge(sig_y.sem, sig_y.now(g))
                    nc.vector.tensor_tensor(y_f[:, :], y_f[:, :], s_f[:, :], ALU.mult).then_inc(xc_ready.sem, 1)
                    dve.wait_ge(kv_step.sem, kv_step.now(g))
                    dve.wait_ge(rqk_ready.sem, rqk_ready.now(g))
                    nrm = rqk[:, :].rearrange("p (r o) -> p r o", o=1)
                    nc.vector.tensor_tensor(per_head(kv_f[:, :]), per_head(kv_f[:, :]),
                                            nrm[:, G * HEADS:, :].to_broadcast([P, G * HEADS, HD]), ALU.mult)\
                        .then_inc(kv_ready.sem, 1)
                    nc.vector.tensor_tensor(per_head(qn_f[:, :]), per_head(pA[:, :]),
                                            nrm[:, 0:G * HEADS, :].to_broadcast([P, G * HEADS, HD]), ALU.mult)\
                        .then_inc(qn_ready.sem, 1)
                if b:
                    sum_products(g - 1, 0)
                    dve.wait_ge(redd.sem, redd.now(g - 1, 1))
                    products(g - 1, 1, 0, XD // 2)
                if a:
                    dve.wait_ge(kv_tr.sem, kv_tr.now(g))
                    dve.wait_ge(ig_ready.sem, ig_ready.now(g))
                    nc.vector.tensor_tensor(bt_f[:, :], pA[:, :], ig.rearrange("p c t -> p (c t)"), ALU.mult)\
                        .then_inc(bt_ready.sem, 1)
                    dve.wait_ge(gam_ready.sem, gam_ready.now(g))
                    dve.wait_ge(bt_ready.sem, bt_ready.now(g))
                    for c in range(NC):
                        nc.vector.tensor_tensor_scan(s_[:, c, :], gam[:, c, :], btC[:, c, :], 0.0, ALU.mult, ALU.add)\
                            .then_inc(mem_ready.sem, 1)
                if b:
                    products(g - 1, 1, XD // 2, XD)
                    sum_products(g - 1, 1)
                if a:
                    dve.wait_ge(memsq.sem, memsq.now(g))
                    nc.vector.tensor_reduce(s2[:], per_head(kv_f[:, :]), AX.X, ALU.add).then_inc(memvar.sem, 1)
                    dve.wait_ge(memvar.sem, memvar.now(g, 1))
                    nc.vector.tensor_scalar(s2[:], s2[:], 1.0 / HD, LN_EPS, ALU.mult, ALU.add)\
                        .then_inc(memvar.sem, 1)
                if b:
                    dve.wait_ge(y2_tr.sem, y2_tr.now(g - 1))
                    nc.vector.tensor_tensor(x2_of(g - 1), tok(pA), x2_of(g - 1), ALU.add).then_inc(x2_ready.sem, 1)
                if a:
                    dve.wait_ge(d2_ready.sem, d2_ready.now(g))
                    nc.vector.reciprocal(r2[:], d2[:]).then_inc(r2_ready.sem, 1)
                    dve.wait_ge(r2_ready.sem, r2_ready.now(g))
                    nc.vector.tensor_tensor(per_head(o_f[:, :]), per_head(pC[:, :]), small(r2), ALU.mult)\
                        .then_inc(o_step.sem, 1)
                    dve.wait_ge(qw_ready.sem, qw_ready.now(g))
                    dve.wait_ge(o_step.sem, o_step.now(g, 1))
                    nc.vector.tensor_tensor(o_f[:, :], o_f[:, :], v_f[:, :], ALU.mult).then_inc(o_step.sem, 1)
                    dve.wait_ge(qb_ready.sem, qb_ready.now(g))
                    dve.wait_ge(o_step.sem, o_step.now(g, 2))
                    nc.vector.tensor_tensor(o_f[:, :], o_f[:, :], qn_f[:, :], ALU.add).then_inc(o_step.sem, 1)
                    dve.wait_ge(o_step.sem, o_step.now(g, 3))
                    nc.vector.tensor_reduce(mu[:], per_head(o_f[:, :]), AX.X, ALU.add).then_inc(o_step.sem, 1)
                    dve.wait_ge(o_step.sem, o_step.now(g, 4))
                    nc.vector.tensor_scalar(mu[:], mu[:], 1.0 / HD, None, ALU.mult).then_inc(o_step.sem, 1)
                    dve.wait_ge(o_step.sem, o_step.now(g, 5))
                    nc.vector.tensor_tensor(per_head(o_f[:, :]), per_head(o_f[:, :]), small(mu), ALU.subtract)\
                        .then_inc(o_step.sem, 1)
                if b:
                    dve.wait_ge(x2_ready.sem, x2_ready.now(g - 1))
                    statistics(g - 1, 2)
                if a:
                    dve.wait_ge(osq.sem, osq.now(g))
                    nc.vector.tensor_reduce(s3[:], per_head(kv_f[:, :]), AX.X, ALU.add).then_inc(ovar.sem, 1)
                    dve.wait_ge(ovar.sem, ovar.now(g, 1))
                    nc.vector.tensor_scalar(s3[:], s3[:], 1.0 / HD, LN_EPS, ALU.mult, ALU.add)\
                        .then_inc(ovar.sem, 1)
                    dve.wait_ge(d3_ready.sem, d3_ready.now(g))
                    nc.vector.reciprocal(r3[:], d3[:]).then_inc(r3_ready.sem, 1)
                    dve.wait_ge(r3_ready.sem, r3_ready.now(g))
                    nc.vector.tensor_tensor(per_head(o_f[:, :]), per_head(o_f[:, :]), small(r3), ALU.mult)\
                        .then_inc(o_step.sem, 1)
                    dve.wait_ge(oT_out.sem, oT_out.now(g))
                    dve.wait_ge(og_ready.sem, og_ready.now(g))
                    nc.vector.tensor_tensor(y_f[:, :], y_f[:, :], og_f[:, :], ALU.mult).then_inc(oT_ready.sem, 1)
                    dve.wait_ge(wo_mm.sem, wo_mm.now(g))
                    nc.vector.tensor_tensor(x2_of(g), tok(pB), x2_of(g), ALU.add).then_inc(x1_ready.sem, 1)
                    dve.wait_ge(x1_ready.sem, x1_ready.now(g))
                    statistics(g, 1)
                if b:
                    logits = pC[:, 0:G * E].rearrange("p (b e) -> p b e", b=G)
                    dve.wait_ge(lg_mm.sem, lg_mm.now(g - 1))
                    link(nc.vector.tensor_reduce(lmax[:], logits, AX.X, ALU.max))
                    link(nc.vector.tensor_tensor(lg[:], logits, bc(lmax[:, :], E), ALU.subtract))
                    dve.wait_ge(ex_ready.sem, ex_ready.now(g - 1))
                    link(nc.vector.tensor_reduce(psm[:, 0, :], pe_[:], AX.X, ALU.add))
                    link(nc.vector.reciprocal(psm[:, 1, :], psm[:, 0, :]))
                    link(nc.vector.tensor_tensor(pr[:], pe_[:], bc(psm[:, 1, :], E), ALU.mult))
                    for b_ in range(G - 1):
                        nc.vector.max(m8[:, b_, :], pr[:, b_, :])
                    link(nc.vector.max(m8[:, G - 1, :], pr[:, G - 1, :]))
                    for b_ in range(G - 1):
                        nc.vector.max_index(ix[:, b_, :], m8[:, b_, :], pr[:, b_, :])
                    link(nc.vector.max_index(ix[:, G - 1, :], m8[:, G - 1, :], pr[:, G - 1, :]))
                    link(nc.vector.tensor_copy(ixf[:], ix[:, :, 0:TOPK]))
                    oh_g = OH[:, bass.ds(G * (g - 1), G), :]
                    link(nc.vector.tensor_tensor(
                        oh_g.rearrange("p b (k e) -> p (b k) e", k=TOPK),
                        IOT[:, 0:1, 0:E].to_broadcast([P, G * TOPK, E]),
                        ixf[:, :, :].rearrange("p b (k o) -> p (b k) o", o=1).to_broadcast([P, G * TOPK, E]),
                        ALU.is_equal))
                    with nc.allow_low_precision("zeros and ones"):
                        link(nc.vector.tensor_reduce(sel[:], oh_g.rearrange("p b (k e) -> p b e k", k=TOPK),
                                                     AX.X, ALU.add))
                    assert done[0] == RT_SEL
                    with nc.allow_low_precision("counts up to 16"):
                        nc.vector.tensor_reduce(selg[:], sel[:, :, :].rearrange("p b e -> p e b"), AX.X, ALU.add)
                    link(nc.vector.tensor_reduce(wsum[:, 0, :], m8[:, :, 0:TOPK], AX.X, ALU.add))
                    link(nc.vector.reciprocal(wsum[:, 1, :], wsum[:, 0, :]))
                    nc.vector.tensor_tensor(WT[:, bass.ds(G * (g - 1), G), :], m8[:, :, 0:TOPK],
                                            bc(wsum[:, 1, :], TOPK), ALU.mult)
                    dve.wait_ge(rank_mm.sem, rank_mm.now(g - 1))
                    link(nc.vector.tensor_tensor(cum[:, :], cum[:, :], selg[:, :], ALU.add))
                    assert done[0] == RT_CUM
                    link(nc.vector.tensor_tensor(
                        tmp_oh[:, :].rearrange("p (b k e) -> p b k e", b=G, k=TOPK),
                        pC[:, 512:512 + G * E].rearrange("p (b o e) -> p b o e", b=G, o=1)
                        .to_broadcast([P, G, TOPK, E]),
                        oh_g.rearrange("p b (k e) -> p b k e", k=TOPK), ALU.mult))
                    link(nc.vector.tensor_reduce(posr[:, bass.ds(G * (g - 1), G), :],
                                                 tmp_oh[:, :].rearrange("p (b k e) -> p b k e", b=G, k=TOPK),
                                                 AX.X, ALU.add))
                    assert done[0] == RT_STEPS

            body(0, True, False)
            with dve.Fori(1, NG) as g:
                body(g, True, True)
            body(NG, False, True)

            def step(ins, value):
                ins.then_inc(plan, 1)
                dve.wait_ge(plan, value)

            dve.wait_ge(cnt_mm, 1)
            step(nc.vector.tensor_scalar(nti[:, 0:1], pB[0:E, 0:1], float(P - 1), None, ALU.add), 3)
            step(nc.vector.tensor_scalar(nti[:, 1:2], nti[:, 0:1], 7, None, ALU.arith_shift_right), 4)
            step(nc.vector.tensor_copy(ntf[:], nti[:, 1:2]), 5)
            step(nc.vector.tensor_copy(ntb[:], ntf[:, 0:1].to_broadcast([E, P])), 6)
            posf = posr[:, :, :].rearrange("p b k -> p (b k)")
            step(nc.vector.tensor_copy(posi[:, 0, :], posf), 7)
            nc.vector.tensor_scalar(posi[:, 1, :], posi[:, 0, :], 7, None, ALU.arith_shift_right)
            step(nc.vector.tensor_scalar(posi[:, 2, :], posi[:, 0, :], P - 1, None, ALU.bitwise_and), 8)
            step(nc.vector.tensor_copy(pos2[:, :, :], posi[:, 1:3, :]), 9)
            dve.wait_ge(start_mm, 1)
            step(nc.vector.tensor_scalar(over, IOT[0:E, 0, 0:NTILE], pA[0:E, 512:513], None, ALU.is_ge), 10)
            step(nc.vector.tensor_copy(start[:], pA[:, 0:E]), 11)
            step(nc.vector.tensor_tensor(oh_prod, OH[:, :, :].rearrange("p b (k e) -> p (b k) e", k=TOPK),
                                         start[:, :].rearrange("p (o e) -> p o e", o=1)
                                         .to_broadcast([P, B * TOPK, E]), ALU.mult), 12)
            step(nc.vector.tensor_reduce(starts[:], oh_prod, AX.X, ALU.add), 13)
            step(nc.vector.tensor_tensor(pos2[:, 0, :], pos2[:, 0, :], starts[:], ALU.add), 14)
            with dve.Fori(0, B * TOPK // NHOT) as r:
                dve.wait_ge(id_mm, NHOT * r + NHOT)
                dve.nop(nofuse=True)
                nc.vector.tensor_copy(qcol[:, 0, :], pos2[:, 0, bass.ds(NHOT * r, NHOT)]).then_inc(qcol_ready, 1)
                nc.vector.tensor_copy(qcol[:, 1, :], pos2[:, 1, bass.ds(NHOT * r, NHOT)]).then_inc(qcol_ready, 1)
                nc.vector.tensor_copy(qcol[:, 2, :], IOT[:, 1, bass.ds(NHOT * r, NHOT)]).then_inc(qcol_ready, 1)
                dve.wait_ge(qcol_ready, 3 * r + 3)
                for u in range(NHOT):
                    nc.vector.tensor_scalar(lo_hot[u], iota, qcol[:, 1, u:u + 1], None,
                                            ALU.is_equal).then_inc(lo_ready, 1)
                    if u % 2 == 0:
                        nc.vector.tensor_scalar(hi_hot[u], IOT[:, 0, 0:NTILE], qcol[:, 0, u:u + 1],
                                                qcol[:, 2, u:u + 1], ALU.is_equal, ALU.mult).then_inc(hi_even, 1)
            dve.wait_ge(etile_mm, 1)
            step(nc.vector.tensor_scalar(etile[:, 0:NTILE], pB[0:1, 0:NTILE], float(E - 1), None, ALU.min), 15)
            dve.wait_ge(id_mm, NHOT + B * TOPK)
            nc.vector.tensor_scalar(idx_t[:, 2, :], pA[:, 0:NTILE], -1.0, 0.0, ALU.add, ALU.max)
            step(nc.vector.tensor_scalar(idx_t[:, 0, :], pA[:, 0:NTILE], 0.0, float(FAR), ALU.is_equal, ALU.mult), 16)
            step(nc.vector.tensor_copy(GIDX[:, 0, :], idx_t[:, 2, :]), 17)
            step(nc.vector.tensor_scalar(GIDX[:, 1, :], GIDX[:, 0, :], 2, None, ALU.arith_shift_right), 18)

            def gather_column(t, u):
                nc.vector.tensor_copy(gcol[:, u:u + 1], GIDX[:, 1, bass.ds(t, 1)].bitcast(U32)).then_inc(gcol_ready, 1)

            for u in range(NB):
                gather_column(u, u)
            step(nc.vector.scalar_tensor_tensor(idx_t[:, 1, :], pA[:, 0:NTILE], -1.0, idx_t[:, 0, :],
                                                ALU.add, ALU.add), 19)
            step(nc.vector.tensor_copy(SIDX, idx_t[:, 1, :]), PLAN_DONE)

            def tile(t, u, i):
                dve.wait_ge(silu_ready, t + 1 + AHEAD)
                dve.wait_ge(hid_tr, t + 1)
                nc.vector.tensor_tensor(hid[u % 2], act_g[u % 2],
                                        pB[:, (u % 2) * 512 + INNER:(u % 2) * 512 + 2 * INNER], ALU.mult)\
                    .then_inc(hid_ready, 1)
                dve.wait_ge(hid_tr, t + 1 + AHEAD)
                dve.wait_ge(dn_mm, t + 1)
                nc.vector.tensor_copy(hidT[u % 2], pY[:, u % 2, 0:P]).then_inc(hidT_ready, 1)
                if i is not None:
                    dve.wait_ge(scattered[u % NR], 16 * (NB // NR) * i + 16 * (u // NR))
                nc.vector.tensor_copy(scol[:, u % NR:u % NR + 1], SIDX[:, bass.ds(t, 1)].bitcast(U32))\
                    .then_inc(scol_ready, 1)
                dve.wait_ge(dn_mm, t + 1 + AHEAD)
                nc.vector.tensor_copy(res[u % NR], pC[:, (u % 2) * 512:(u % 2) * 512 + C]).then_inc(res_ready, 1)

            for u in range(NB):
                tile(u, u, 0 if u >= NR else None)
                dve.wait_ge(gathered[u], 16)
                gather_column(u + NB, u)
            with dve.Fori(1, NTILE // NB - 1) as i:
                for u in range(NB):
                    tile(NB * i + u, u, i)
                    dve.wait_ge(gathered[u], 16 * i + 16)
                    gather_column(NB * i + u + NB, u)
            for u in range(NB):
                tile(NTILE - NB + u, u, NTILE // NB - 1)

            for n in range(B):
                dve.wait_ge(z_in[n % NZ], 16 * (n // NZ + 1))
                for k in range(TOPK):
                    if k:
                        dve.wait_ge(comb, TOPK * n + k)
                    nc.vector.scalar_tensor_tensor(X2[:, n, :], z_buf[n % NZ][:, k * C:(k + 1) * C],
                                                   WT[:, n, k:k + 1], X2[:, n, :], ALU.mult, ALU.add)\
                        .then_inc(comb, 1)


_OUTS = [((B, T, C), "float32")]


def kernel(**inputs):
    import numpy as np
    import concourse.bacc as bacc
    from concourse import mybir as mb
    from concourse.bass_utils import run_bass_kernel_spmd

    a = {k: np.asarray(v) for k, v in inputs.items()}
    f32 = np.float32

    def chunked(w):
        return np.ascontiguousarray(w.reshape(NC, P, -1).transpose(1, 0, 2))

    wq, wk, wv, wo, wig, wog = (a[f"L0_attn_{n}"].T for n in ("Wq", "Wk", "Wv", "Wo", "Wig", "Wog"))
    wg = np.repeat(a["L0_attn_Wg"], HD, axis=0).T
    cols = np.stack([*a["L0_attn_conv_w"].T, a["L0_attn_conv_b"], a["L0_attn_b_ig"],
                     np.repeat(a["L0_attn_b_g"], HD), a["L0_attn_b_og"], a["L0_attn_gn_w"],
                     a["L0_attn_gn_b"]], axis=1)
    rows = np.broadcast_to(np.stack([a["L0_attn_mn_w"], a["L0_attn_mn_b"]]), (P, 2, C))
    padded = np.zeros((XH, P + C), f32)
    padded[:, P:] = a["L0_xattn_ssm_kernel"]
    toep = padded[:, P + np.arange(C)[None, :] - np.arange(P)[:, None]].transpose(1, 0, 2)
    ctx_t = a["ctx_2048"].reshape(NG, G, T, NC, P).transpose(0, 4, 3, 1, 2).reshape(NG, P, NC * G * T)
    w_gu = np.concatenate([a["L0_ffn_w_gate"], a["L0_ffn_w_up"]], axis=1)
    w_gu = w_gu.reshape(E, 2 * INNER, NC, P).transpose(3, 0, 2, 1).reshape(P, E * GUW)
    w_dn = a["L0_ffn_w_down"].transpose(2, 0, 1).reshape(P, E * C)
    eye = np.eye(P, dtype=f32)
    head = np.kron(np.eye(P // HD), np.ones((HD, HD))).astype(f32)
    consts = np.stack([eye, eye - head / f32(HD), np.ones((P, P), f32)], axis=1)
    iotas = np.zeros((P, 4, P), f32)
    iotas[:, 0] = np.arange(P)
    n, k = np.divmod(np.arange(B * TOPK), TOPK)
    iotas[:, 1, :B * TOPK] = (n * P)[None] * TOPK + np.arange(P)[:, None] * TOPK + k[None] + 1
    before = np.arange(E)[:, None] < np.arange(E)[None, :]
    iotas[:E, 2, :E] = before
    iotas[:E, 2, E:2 * E] = before | np.eye(E, dtype=bool)
    iotas[:, 3] = np.arange(P)[:, None] < np.arange(P)[None, :]

    data = {
        "x": a["x"], "ctx_t": ctx_t, "w_qk": chunked(np.concatenate([wq, wk], axis=1)), "w_v": chunked(wv),
        "w_ig": chunked(wig), "w_g": chunked(wg), "w_og": chunked(wog), "w_o": chunked(wo),
        "w_rt": chunked(a["L0_ffn_router_w"].T), "cols": chunked(cols), "rows": rows, "toep": toep,
        "dskip": np.broadcast_to(a["L0_xattn_D"], (P, XH)), "w_gu": w_gu, "w_dn": w_dn,
        "consts": consts, "iotas": iotas,
    }
    nc = bacc.Bacc("TRN2", target_bir_lowering=False, num_devices=1)
    arrays, args = {}, []
    for name, v in data.items():
        v = np.ascontiguousarray(v)
        arrays[f"in_{name}"] = v
        args.append(nc.dram_tensor(f"in_{name}", v.shape, mb.dt.from_np(v.dtype), kind="ExternalInput").ap())
    args.append(nc.dram_tensor("out_0", _OUTS[0][0], mb.dt.from_np(np.dtype("float32")), kind="ExternalOutput").ap())
    program(nc, *args)
    r = run_bass_kernel_spmd(nc, [arrays], core_ids=[0])
    return r.results[0]["out_0"]
```

```python
from contextlib import ExitStack

import concourse.bass as bass
from concourse import mybir

ALU = mybir.AluOpType
ACT = mybir.ActivationFunctionType
AX = mybir.AxisListType
F32 = mybir.dt.float32
BF16 = mybir.dt.bfloat16
I32 = mybir.dt.int32
U32 = mybir.dt.uint32

B, T, C = 16, 128, 256
P = 128
NC = C // P
NTOK = B * T
HEADS, HD = 16, 16
KC = 4
XH, XD = 16, 8
NPAIR = XD * (XD + 1) // 2
G = 2
NG = B // G
GT = G * T
E, TOPK, INNER = 32, 4, 128
NSLOT = NTOK * TOPK
NTILE = (NSLOT + E * (P - 1)) // P + 1
NTILE += -NTILE % 8
ELOW = 7
GUW = NC * 2 * INNER
LN_EPS = 1e-5
NB = 8
NR = 4
AHEAD = 2
NZ = 16
RT_SEL, RT_CUM, RT_STEPS = 10, 13, 17
PLAN_DONE = 19


class Signal:

    def __init__(self, sem, per):
        self.sem, self.per = sem, per

    def now(self, g, k=None):
        return (g + 1) * self.per + (self.per if k is None else k)

    def before(self, g, k=None):
        return g * self.per + (self.per if k is None else k)


def pair_offset(s):
    return s * XD - s * (s - 1) // 2


def program(nc, x, ctx_t, w_qk, w_v, w_ig, w_g, w_og, w_o, w_rt, cols, rows, toep, dskip,
            w_gu, w_dn, consts, iotas, out):
    with ExitStack() as stack:
        def sb(name, shape, dt=F32):
            return stack.enter_context(nc.sbuf_tensor(name, shape, dt))

        def sem(name):
            return stack.enter_context(nc.semaphore(name))

        def signal(name, per):
            return Signal(sem(name), per)

        hn_dram = nc.dram_tensor("hn_scratch", [NTOK, C], F32, kind="Internal").ap()
        rows_dram = nc.dram_tensor("rows_scratch", [E * NTOK, 1], F32, kind="Internal").ap()
        z_dram = nc.dram_tensor("z_scratch", [NTILE * P, C], F32, kind="Internal").ap()

        X2 = sb("X2", [P, B, C])
        WQK = sb("WQK", [P, NC, 2 * C])
        WV = sb("WV", [P, NC, C])
        WIG = sb("WIG", [P, NC, C])
        WG = sb("WG", [P, NC, C])
        WOG = sb("WOG", [P, NC, C])
        WO = sb("WO", [P, NC, C])
        WRT = sb("WRT", [P, NC, E])
        COLS = sb("COLS", [P, NC, 10])
        ROWS = sb("ROWS", [P, 2, C])
        TOEP = sb("TOEP", [P, XH, C])
        DSK = sb("DSK", [P, XH])
        CST = sb("CST", [P, 3, P])
        IOT = sb("IOT", [P, 4, P])
        TRI = sb("TRI", [P, 2, P], BF16)
        WDN = sb("WDN", [P, E * C])
        WGU = sb("WGU", [P, E * GUW])
        taken = [ELOW * GUW]

        def high(n):
            first = taken[0]
            taken[0] += n
            return WGU[:, first:first + n]

        PAIRS = NC * G * XH * NPAIR
        YB = sb("YB", [P, 2 * PAIRS])
        yq = YB[:, 0:PAIRS].rearrange("p (q n) -> p q n", n=NPAIR)
        y_heads = YB[:, 0:PAIRS].rearrange("p (q h n) -> p q (h n)", h=XH, n=NPAIR)
        kvp = YB[:, PAIRS:].rearrange("p (q n) -> p q n", n=NPAIR)
        kvp_h = YB[:, PAIRS:].rearrange("p (c b h n) -> p c b h n", c=NC, b=G, h=XH)
        prod_f = sb("prod", [P, NC * G * XH * XD * XD])
        prod = prod_f[:, :].rearrange("p (q n) -> p q n", n=XD * XD)
        xnT = high(NC * G * (T + KC - 1)).rearrange("p (c b t) -> p c b t", c=NC, b=G)
        ctx_f = sb("ctx_f", [P, NC * G * XH * XD])
        ctxm = ctx_f[:, :].rearrange("p (q i) -> p q i", i=XD)

        def as_tok(f):
            return f.rearrange("p (b c) -> p b c", b=G)

        def as_chan(f):
            return f.rearrange("p (c t) -> p c t", c=NC)

        xn, y, sg, v, kv, ksq_f, qsq_f, qn, ig = (high(G * C) for _ in range(9))
        bt, gam, og, qw, qb = (high(G * C) for _ in range(5))
        mem, msq, o, yo, xq = (high(G * C) for _ in range(5))
        PART3 = taken[0]
        qT, cv, hn, hT = (high(G * C) for _ in range(4))

        def per_head(f):
            return f.rearrange("p (r d) -> p r d", d=HD)

        st = sb("st", [P, 3, G, 6])
        mv = sb("mv", [P, 3, G, 2])
        rs = sb("rs", [P, 3, G])
        rstd = sb("rstd", [P, 3, G])
        nmean = sb("nmean", [P, 3, G])
        nmr = sb("nmr", [P, 3, G])
        half = sb("half", [P, G])
        eps = sb("eps", [P, 1])
        ss = sb("ss", [P, 2 * G * HEADS])
        nqk = sb("nqk", [P, 2 * G * HEADS])
        rqk = sb("rqk", [P, 2 * G * HEADS])
        s2 = sb("s2", [P, G * HEADS])
        d2 = sb("d2", [P, G * HEADS])
        d3 = sb("d3", [P, G * HEADS])
        r2 = sb("r2", [P, G * HEADS])
        mu = sb("mu", [P, G * HEADS])
        s3 = sb("s3", [P, G * HEADS])
        r3 = sb("r3", [P, G * HEADS])
        lmax = sb("lmax", [P, G])
        lg = sb("lg", [P, G, E])
        ex = sb("ex", [P, G, E])
        psm = sb("psm", [P, 2, G])
        pr = sb("pr", [P, G, E])
        m8 = sb("m8", [P, G, 8])
        ix = sb("ix", [P, G, 8], U32)
        ixf = sb("ixf", [P, G, TOPK])
        wsum = sb("wsum", [P, 2, G])
        WT = sb("WT", [P, B, TOPK])
        OH = sb("OH", [P, B, TOPK * E], BF16)
        sel = sb("sel", [P, G, E], BF16)
        selg = sb("selg", [P, E], BF16)
        cum = sb("cum", [P, E], BF16)
        posr = sb("posr", [P, B, TOPK])
        place_f = sb("place_f", [P, G, TOPK])
        place = sb("place", [P, G * TOPK], U32)
        number = sb("number", [P, G * TOPK])
        tmp_oh = sb("tmp_oh", [P, G * TOPK * E])
        big = TOEP[:, :, :].rearrange("p h l -> p (h l)")
        oh_prod = prod_f[:, 0:B * TOPK * E].rearrange("p (q e) -> p q e", e=E)
        tile_rows = big[0:NTILE, 0:P]
        starts = sb("starts", [P, B * TOPK])
        ntf = sb("ntf", [E, 1])
        nti = sb("nti", [E, 2], I32)
        ntb = sb("ntb", [E, P])
        first_f = sb("first_f", [NTILE, 2])
        first = sb("first", [NTILE, 1], U32)
        plan_f = prod_f[:, B * TOPK * E:]
        over = plan_f[0:E, 2 * NTILE:3 * NTILE]
        etile = sb("etile", [1, NTILE + NB], I32)
        start = sb("start", [P, E])
        row1 = plan_f[:, 0:NTILE]
        GIDX = plan_f[:, NTILE:2 * NTILE].bitcast(I32)
        slot_f = plan_f[:, 3 * NTILE:3 * NTILE + B * TOPK]
        SLOT = sb("SLOT", [P, B * TOPK], U32)
        gcol = sb("gcol", [P, NB], U32)

        def ybuf(k):
            return YB[:, k * C:(k + 1) * C]

        xg = [ybuf(i) for i in range(NB)]
        xgT = [ybuf(NB + i) for i in range(2)]
        res = [ybuf(NB + 2 + i) for i in range(NR)]
        act_g = [ybuf(NB + NR + 2)[:, i * P:(i + 1) * P] for i in range(2)]
        hid = [ybuf(NB + NR + 3)[:, i * P:(i + 1) * P] for i in range(2)]
        hidT = [ybuf(NB + NR + 4)[:, i * P:(i + 1) * P] for i in range(2)]

        pA, pB, pC = (stack.enter_context(nc.psum_tensor(n, [P, 1024], F32)) for n in ("pA", "pB", "pC"))
        pY = stack.enter_context(nc.psum_tensor("pY", [P, 2, 512], F32))
        pV, pK = pA[:, 0:512], pA[:, 512:]
        pQ, pX = pB[:, 0:512], pB[:, 512:]
        pM, pT = pC[:, 0:512], pC[:, 512:]
        Y2 = 2 * NC * G * NPAIR
        logits_f, ranks = pQ[:, 0:G * E], pX[:, 0:G * E]

        WDN_E = WDN[:, :].rearrange("p (e n) -> p e n", n=C)
        WGU_E = WGU[:, :].rearrange("p (q n) -> p q n", n=2 * INNER)
        z_buf = [prod_f[:, i * C:(i + 1) * C] for i in range(NZ)]

        ident = CST[:, 0, :]
        center = CST[:, 1, :]
        onesf = CST[:, 2, :]
        part = IOT[0:NTILE, 2, 2 * E:2 * E + 1]
        tri_lt = IOT[0:E, 2, 0:E]
        tri_le = IOT[0:E, 2, E:2 * E]
        CONVB, BIG, BG, BOG, GNW, GNB = range(KC, KC + 6)

        const_in = [sem(f"const_in{i}") for i in range(6)]
        half_set = sem("half_set")
        eps_set = sem("eps_set")
        toep_ready = sem("toep_ready")
        x_in = signal("x_in", 16)
        ctx_in = signal("ctx_in", 16)
        stats = [signal(f"stats{i}", G) for i in range(3)]
        aggr = [signal(f"aggr{i}", G) for i in range(3)]
        factor = [signal(f"factor{i}", 4) for i in range(3)]
        xn_ready = signal("xn_ready", 1)
        xn_tr = signal("xn_tr", 1)
        xnT_ready = signal("xnT_ready", 2)
        tap0 = signal("tap0", 2)
        conv = signal("conv", 6)
        sig_y = signal("sig_y", 1)
        xc_ready = signal("xc_ready", 1)
        v_mm = signal("v_mm", 1)
        k_mm = signal("k_mm", 1)
        q_mm = signal("q_mm", 1)
        v_out = signal("v_out", 1)
        ksq = signal("ksq", 1)
        qsq = signal("qsq", 1)
        ssum = signal("ssum", 2)
        ssmax = signal("ssmax", 1)
        nqk_ready = signal("nqk_ready", 1)
        rqk_ready = signal("rqk_ready", 1)
        kv_step = signal("kv_step", 1)
        kv_ready = signal("kv_ready", 1)
        qn_ready = signal("qn_ready", 1)
        qw_ready = signal("qw_ready", 1)
        qb_ready = signal("qb_ready", 1)
        ig_mm = signal("ig_mm", 1)
        gam_mm = signal("gam_mm", 1)
        ig_ready = signal("ig_ready", 2)
        gam_out = signal("gam_out", 2)
        gam_ready = signal("gam_ready", 1)
        kv_tr = signal("kv_tr", 1)
        bt_ready = signal("bt_ready", 1)
        mem_ready = signal("mem_ready", 2)
        og_mm = signal("og_mm", 1)
        og_ready = signal("og_ready", 2)
        mem_tr = signal("mem_tr", 1)
        memsq = signal("memsq", 1)
        memvar = signal("memvar", 1)
        d2_ready = signal("d2_ready", 1)
        r2_ready = signal("r2_ready", 1)
        o_step = signal("o_step", 7)
        osq = signal("osq", 1)
        ovar = signal("ovar", 1)
        d3_ready = signal("d3_ready", 1)
        r3_ready = signal("r3_ready", 1)
        o_tr = signal("o_tr", 1)
        oT_out = signal("oT_out", 2)
        gated = signal("gated", 1)
        wo_mm = signal("wo_mm", 1)
        x1_ready = signal("x1_ready", 1)
        q2_ready = signal("q2_ready", 1)
        q2_tr = signal("q2_tr", 1)
        q2T_ready = signal("q2T_ready", 1)
        pairs = signal("pairs", XD)
        y_mm = signal("y_mm", XH // 2)
        y_out = signal("y_out", XH // 2)
        prods = signal("prods", 2 * XD - 1)
        redd = signal("redd", 2)
        y2_tr = signal("y2_tr", 1)
        x2_ready = signal("x2_ready", 1)
        h_ready = signal("h_ready", 1)
        normed = (xn_ready, q2_ready, h_ready)
        hn_stored = signal("hn_stored", 16)
        h_tr = signal("h_tr", 1)
        hT_ready = signal("hT_ready", 1)
        lg_mm = signal("lg_mm", 1)
        rt = signal("rt", RT_STEPS)
        ex_ready = signal("ex_ready", 1)
        rank_mm = signal("rank_mm", 1)
        gu_in = sem("gu_in")
        high_in = sem("high_in")
        cnt_mm = sem("cnt_mm")
        plan = sem("plan")
        start_mm = sem("start_mm")
        etile_mm = sem("etile_mm")
        rows_zero = sem("rows_zero")
        zero_set = sem("zero_set")
        numbers_out = sem("numbers_out")
        numbered = signal("numbered", 1)
        rows_in = sem("rows_in")
        rows_tr = sem("rows_tr")
        gcol_ready = sem("gcol_ready")
        gathered = [sem(f"gathered{i}") for i in range(NB)]
        z_stored = [sem(f"z_stored{i}") for i in range(NR)]
        xg_tr = sem("xg_tr")
        xgT_ready = sem("xgT_ready")
        gu_mm = sem("gu_mm")
        silu_ready = sem("silu_ready")
        hid_ready = sem("hid_ready")
        hid_tr = sem("hid_tr")
        hidT_ready = sem("hidT_ready")
        dn_mm = sem("dn_mm")
        res_ready = sem("res_ready")
        z_in = [sem(f"z_in{i}") for i in range(NZ)]
        comb = sem("comb")
        out_stored = sem("out_stored")

        block = stack.enter_context(nc.Block())

        @block.sync
        def _(sp):
            sp.sem_inc(x_in.sem, 16)
            sp.sem_inc(ctx_in.sem, 16)
            sp.sem_inc(hn_stored.sem, 16)
            sp.dma_start(X2[:, 0:G, :], x[0:G].rearrange("b t c -> t b c")).then_inc(x_in.sem, 16)
            for n, loads in enumerate((((CST, consts), (COLS, cols)), ((WV, w_v), (WQK, w_qk)),
                                       ((WIG, w_ig), (WG, w_g), (WOG, w_og)), ((ROWS, rows), (IOT, iotas), (DSK, dskip)),
                                       ((TOEP, toep),), ((WO, w_o), (WRT, w_rt)))):
                if n == 2:
                    sp.dma_start(ctx_f[:], ctx_t[0]).then_inc(ctx_in.sem, 16)
                for dst, src in loads:
                    sp.dma_start(dst[:], src).then_inc(const_in[n], 16)

            def load_group(g):
                sp.wait_ge(x_in.sem, x_in.now(g - 1))
                sp.nop(nofuse=True)
                sp.dma_start(X2[:, bass.ds(G * g, G), :],
                             x[bass.ds(G * g, G)].rearrange("b t c -> t b c")).then_inc(x_in.sem, 16)
                sp.wait_ge(ctx_in.sem, ctx_in.now(g - 1))
                sp.wait_ge(pairs.sem, pairs.now(g - 1))
                sp.nop(nofuse=True)
                sp.dma_start(ctx_f[:], ctx_t[bass.ds(g, 1)].rearrange("g p n -> (g p) n"))\
                    .then_inc(ctx_in.sem, 16)

            def store_hn(g):
                sp.wait_ge(h_ready.sem, h_ready.now(g))
                sp.wait_ge(hn_stored.sem, hn_stored.before(g))
                sp.nop(nofuse=True)
                sp.dma_start(hn_dram[bass.ds(GT * g, GT), :].rearrange("(b t) c -> t b c", t=T), as_tok(hn))\
                    .then_inc(hn_stored.sem, 16)

            load_group(1)
            sp.wait_ge(zero_set, 1)
            sp.dma_start(rows_dram.rearrange("(p n) o -> p (n o)", p=P), prod_f[:, 0:E * NTOK // P])\
                .then_inc(rows_zero, 16)
            load_group(2)
            sp.dma_start(WGU[:, 0:ELOW * GUW], w_gu[:, 0:ELOW * GUW]).then_inc(gu_in, 16)
            sp.dma_start(WDN[:, :], w_dn).then_inc(gu_in, 16)
            with sp.Fori(3, NG) as g:
                load_group(g)
                store_hn(g - 3)
            for g in range(NG - 3, NG - 2):
                store_hn(g)
            last = NG - 1
            sp.wait_ge(q2_tr.sem, q2_tr.now(last))
            sp.dma_start(WGU[:, ELOW * GUW:PART3], w_gu[:, ELOW * GUW:PART3]).then_inc(high_in, 16)
            store_hn(NG - 2)
            sp.wait_ge(redd.sem, redd.now(last))
            sp.wait_ge(y2_tr.sem, y2_tr.now(last))
            sp.wait_ge(lg_mm.sem, lg_mm.now(last))
            store_hn(last)
            sp.wait_ge(hn_stored.sem, hn_stored.now(last))
            sp.dma_start(WGU[:, PART3:], w_gu[:, PART3:]).then_inc(high_in, 16)
            with sp.Fori(0, NTILE // NR) as i:
                for u in range(NR):
                    sp.wait_ge(res_ready, NR * i + u + 1 + AHEAD)
                    sp.nop(nofuse=True)
                    sp.dma_start(z_dram[bass.ds(P * (NR * i + u), P), :], res[u]).then_inc(z_stored[u], 16)
            for n in range(B):
                sp.wait_ge(comb, TOPK * (n + 1))
                sp.dma_start(out[n], X2[:, n, :]).then_inc(out_stored, 16)
            sp.wait_ge(out_stored, 16 * B)

        @block.gpsimd
        def _(pool):
            for s in (numbered, *factor, qw_ready, qb_ready, gam_ready, pairs):
                pool.sem_inc(s.sem, s.per)
            pool.memset(half[:], -0.5).then_inc(half_set, 1)
            pool.memset(xnT[:, :, :, 0:KC - 1], 0.0).then_inc(half_set, 1)
            pool.wait_ge(half_set, 2)

            def norm_factors(g, i):
                f = factor[i]
                pool.wait_ge(aggr[i].sem, aggr[i].now(g))
                pool.wait_ge(normed[i].sem, normed[i].before(g))
                pool.nop(nofuse=True)
                nc.gpsimd.tensor_scalar(rs[:, i, :], mv[:, i, :, 1], LN_EPS, None, ALU.add).then_inc(f.sem, 1)
                nc.gpsimd.tensor_scalar(nmean[:, i, :], mv[:, i, :, 0], -1.0, None, ALU.mult).then_inc(f.sem, 1)
                pool.wait_ge(f.sem, f.now(g, 2))
                pool.nop(nofuse=True)
                nc.gpsimd.tensor_tensor(rstd[:, i, :], rs[:, i, :], half[:, 0:G], ALU.pow).then_inc(f.sem, 1)
                pool.wait_ge(f.sem, f.now(g, 3))
                pool.nop(nofuse=True)
                nc.gpsimd.tensor_tensor(nmr[:, i, :], nmean[:, i, :], rstd[:, i, :], ALU.mult).then_inc(f.sem, 1)

            def body(i, one, two, three, five):
                g, g2, g3, g5 = i, i - 1, i - 2, i - 4
                if one:
                    norm_factors(g, 0)
                if two:
                    pool.wait_ge(ctx_in.sem, ctx_in.now(g2))
                    pool.wait_ge(y_mm.sem, y_mm.before(g2))
                    pool.nop(nofuse=True)
                    for s in range(XD):
                        n, off = XD - s, pair_offset(s)
                        nc.gpsimd.tensor_tensor(kvp[:, :, off:off + n], ctxm[:, :, 0:n], ctxm[:, :, s:XD],
                                                ALU.mult).then_inc(pairs.sem, 1)
                if five:
                    pool.wait_ge(rows_zero, 16)
                    pool.wait_ge(rt.sem, rt.now(g5))
                    pool.nop(nofuse=True)
                    for q in range(G * TOPK):
                        pool.indirect_dma_start(out=rows_dram,
                                                out_offset=bass.IndirectOffsetOnAxis(place[:, q:q + 1], 0),
                                                in_=number[:, q:q + 1], in_offset=None).then_inc(numbers_out, 16)
                    pool.wait_ge(numbers_out, 16 * G * TOPK * (g5 + 1))
                    pool.nop(nofuse=True)
                    pool.sem_inc(numbered.sem, 1)
                if one:
                    pool.wait_ge(gam_out.sem, gam_out.now(g))
                    pool.nop(nofuse=True)
                    pool.memset(gam.rearrange("p (q t) -> p q t", t=T)[:, :, 0:1], 0.0).then_inc(gam_ready.sem, 1)
                    pool.wait_ge(const_in[3], 16 * 3)
                    pool.wait_ge(qn_ready.sem, qn_ready.now(g))
                    pool.wait_ge(o_step.sem, o_step.before(g, 3))
                    pool.nop(nofuse=True)
                    nc.gpsimd.tensor_tensor(as_tok(qw), as_tok(qn), ROWS[:, 0:1, :].to_broadcast([P, G, C]),
                                            ALU.mult).then_inc(qw_ready.sem, 1)
                if three:
                    norm_factors(g3, 2)
                if two:
                    norm_factors(g2, 1)
                if one:
                    nc.gpsimd.tensor_tensor(as_tok(qb), as_tok(qn), ROWS[:, 1:2, :].to_broadcast([P, G, C]),
                                            ALU.mult).then_inc(qb_ready.sem, 1)


            body(0, True, False, False, False)
            body(1, True, True, False, False)
            body(2, True, True, True, False)
            body(3, True, True, True, False)
            with pool.Fori(4, NG) as i:
                body(i, True, True, True, True)
            body(NG, False, True, True, True)
            body(NG + 1, False, False, True, True)
            body(NG + 2, False, False, False, True)
            body(NG + 3, False, False, False, True)

            pool.wait_ge(plan, 11)
            pool.indirect_dma_start(out=tile_rows, out_offset=None,
                                    in_=rows_dram.rearrange("(t p) o -> t (p o)", p=P),
                                    in_offset=bass.IndirectOffsetOnAxis(first[:, 0:1], 0)).then_inc(rows_in, 16)

            def gather(t, u):
                pool.wait_ge(gcol_ready, t + 1)
                pool.nop(nofuse=True)
                pool.indirect_dma_start(out=xg[u], out_offset=None, in_=hn_dram,
                                        in_offset=bass.IndirectOffsetOnAxis(gcol[:, u:u + 1], 0))\
                    .then_inc(gathered[u], 16)

            pool.wait_ge(hn_stored.sem, hn_stored.now(NG - 1))
            for u in range(NB):
                gather(u, u)
            with pool.Fori(0, NTILE // NB - 1) as i:
                for u in range(NB):
                    pool.wait_ge(xg_tr, NB * i + u + 1)
                    gather(NB * i + u + NB, u)

            for i in range(NR):
                pool.wait_ge(z_stored[i], 16 * (NTILE // NR))
            for q in range(B * TOPK):
                if q >= NZ:
                    pool.wait_ge(comb, q - NZ + 1)
                pool.indirect_dma_start(out=z_buf[q % NZ], out_offset=None, in_=z_dram,
                                        in_offset=bass.IndirectOffsetOnAxis(SLOT[:, q:q + 1], 0))\
                    .then_inc(z_in[q % NZ], 16)

        @block.tensor
        def _(pe):
            for s in (xn_tr, v_mm, k_mm, q_mm, ig_mm, gam_mm, kv_tr, og_mm, mem_tr, o_tr, wo_mm, q2_tr,
                      y_mm, y2_tr, h_tr, lg_mm, rank_mm):
                pe.sem_inc(s.sem, s.per)
            for s in (gu_mm, hid_tr, dn_mm):
                pe.sem_inc(s, AHEAD)

            def transposed(src, dst, signal_):
                for c in range(NC):
                    for b in range(G):
                        last = nc.tensor.transpose(as_chan(dst)[:, c, b * T:(b + 1) * T],
                                                   as_tok(src)[:, b, c * P:(c + 1) * P], ident)
                last.then_inc(signal_.sem, 1)

            def by_channel(dst, w, rhs, signal_):
                for c in range(NC):
                    for k in range(NC):
                        last = nc.tensor.matmul(as_chan(dst)[:, c, :], w[:, k, c * P:(c + 1) * P],
                                                as_chan(rhs)[:, k, :], start=(k == 0), stop=(k == NC - 1))
                last.then_inc(signal_.sem, 1)

            def by_token(dst, lhs, w, signal_):
                for b in range(G):
                    for k in range(NC):
                        last = nc.tensor.matmul(as_tok(dst)[:, b, :], lhs(k, b), w[:, k, :],
                                                start=(k == 0), stop=(k == NC - 1))
                last.then_inc(signal_.sem, 1)

            def toeplitz(g, twos):
                for w in twos:
                    pe.wait_ge(y_out.sem, y_out.now(g, w - 1))
                    for h in (2 * w, 2 * w + 1):
                        for lc in range(NC):
                            for mc in range(lc + 1):
                                last = nc.tensor.matmul(
                                    pY[:, w % 2, 0:Y2].rearrange("p (c b h n) -> p c b h n", c=NC, b=G, h=2)
                                    [:, lc, :, h % 2, :],
                                    TOEP[:, h, (lc - mc) * P:(lc - mc + 1) * P], kvp_h[:, mc, :, h, :],
                                    start=(mc == 0), stop=(mc == lc))
                    last.then_inc(y_mm.sem, 1)

            def body(i, one, two, three, four):
                g, g2, g3, g4 = i, i - 1, i - 2, i - 3

                def feature(k, b):
                    return xnT[:, k, b, KC - 1:]

                if two:
                    pe.wait_ge(mem_ready.sem, mem_ready.now(g2))
                    pe.wait_ge(x1_ready.sem, x1_ready.before(g2))
                    for b in range(G):
                        for c in range(NC):
                            last = nc.tensor.matmul(as_tok(pM)[:, b, c * P:(c + 1) * P],
                                                    as_chan(mem)[:, c, b * T:(b + 1) * T], center,
                                                    start=True, stop=True)
                    last.then_inc(mem_tr.sem, 1)
                if one:
                    pe.wait_ge(const_in[0], 16 * 2)
                    pe.wait_ge(xn_ready.sem, xn_ready.now(g))
                    pe.wait_ge(bt_ready.sem, bt_ready.before(g))
                    transposed(xn, pX, xn_tr)
                    pe.wait_ge(const_in[1], 16 * 2)
                    pe.wait_ge(half_set, 2)
                    pe.wait_ge(xnT_ready.sem, xnT_ready.now(g))
                    pe.wait_ge(ig_ready.sem, ig_ready.before(g))
                    by_token(pV, feature, WV[:, :, :], v_mm)
                    pe.wait_ge(gam_out.sem, gam_out.before(g))
                    by_token(pK, feature, WQK[:, :, C:2 * C], k_mm)
                    pe.wait_ge(og_ready.sem, og_ready.before(g))
                    if four:
                        pe.wait_ge(rt.sem, rt.now(g4, 2))
                    by_token(pQ, feature, WQK[:, :, 0:C], q_mm)
                if four:
                    pe.wait_ge(toep_ready, 2)
                    pe.wait_ge(rt.sem, rt.now(g4, RT_SEL))
                    for b in range(G):
                        bank = ranks[:, b * E:(b + 1) * E]
                        nc.tensor.matmul(bank, TRI[:, 0, :], sel[:, b, :], start=True, stop=False)
                        for e_ in range(b):
                            nc.tensor.matmul(bank, TRI[:, 1, :], sel[:, e_, :], start=False, stop=False)
                        last = nc.tensor.matmul(bank, TRI[:, 1, :], cum[:, :], start=False, stop=True)
                    last.then_inc(rank_mm.sem, 1)
                if two:
                    pe.wait_ge(toep_ready, 1)
                    pe.wait_ge(pairs.sem, pairs.now(g2))
                    toeplitz(g2, range(4))
                    pe.wait_ge(o_step.sem, o_step.now(g2))
                    pe.wait_ge(q2T_ready.sem, q2T_ready.before(g2))
                    transposed(o, pT, o_tr)
                if one:
                    pe.wait_ge(const_in[2], 16 * 3)
                    pe.wait_ge(xc_ready.sem, xc_ready.now(g))
                    pe.wait_ge(v_out.sem, v_out.now(g))
                    by_channel(pV, WIG, y, ig_mm)
                    pe.wait_ge(kv_step.sem, kv_step.now(g))
                    pe.wait_ge(ksq.sem, ksq.now(g))
                    by_channel(pK, WG, y, gam_mm)
                if three:
                    pe.wait_ge(redd.sem, redd.now(g3))
                    if two:
                        pe.wait_ge(oT_out.sem, oT_out.now(g2))
                    for b in range(G):
                        for c in range(NC):
                            last = nc.tensor.transpose(as_tok(pT)[:, b, c * P:(c + 1) * P],
                                                       cv[:, (c * G + b) * P:(c * G + b + 1) * P], ident)
                    last.then_inc(y2_tr.sem, 1)
                if two:
                    pe.wait_ge(const_in[5], 16 * 2)
                    pe.wait_ge(gated.sem, gated.now(g2))
                    by_token(pM, lambda k, b: as_chan(yo)[:, k, b * T:(b + 1) * T], WO, wo_mm)
                if one:
                    pe.wait_ge(kv_ready.sem, kv_ready.now(g))
                    if four:
                        pe.wait_ge(rt.sem, rt.now(g4, RT_CUM + 1))
                    transposed(kv, pX, kv_tr)
                if two:
                    toeplitz(g2, (4, 5))
                if one:
                    pe.wait_ge(qn_ready.sem, qn_ready.now(g))
                    by_channel(pQ, WOG, y, og_mm)
                if three:
                    pe.wait_ge(h_ready.sem, h_ready.now(g3))
                    pe.wait_ge(x2_ready.sem, x2_ready.now(g3))
                    transposed(hn, pT, h_tr)
                if two:
                    toeplitz(g2, (6, 7))
                    pe.wait_ge(q2_ready.sem, q2_ready.now(g2))
                    pe.wait_ge(oT_out.sem, oT_out.now(g2))
                if three:
                    pe.wait_ge(hT_ready.sem, hT_ready.now(g3))
                if two:
                    transposed(xq, pT, q2_tr)
                if three:
                    if one:
                        pe.wait_ge(og_ready.sem, og_ready.now(g))
                    for b in range(G):
                        for k in range(NC):
                            last = nc.tensor.matmul(logits_f[:, b * E:(b + 1) * E],
                                                    as_chan(hT)[:, k, b * T:(b + 1) * T],
                                                    WRT[:, k, :], start=(k == 0), stop=(k == NC - 1))
                    last.then_inc(lg_mm.sem, 1)

            body(0, True, False, False, False)
            body(1, True, True, False, False)
            body(2, True, True, True, False)
            with pe.Fori(3, NG) as i:
                body(i, True, True, True, True)
            body(NG, False, True, True, True)
            body(NG + 1, False, False, True, True)
            body(NG + 2, False, False, False, True)

            pe.wait_ge(rt.sem, rt.now(NG - 1, RT_CUM))
            nc.tensor.matmul(pB[0:E, 0:1], cum[:, :], TRI[:, 1, 0:1], start=True, stop=True).then_inc(cnt_mm, 1)
            pe.wait_ge(plan, 6)
            nc.tensor.matmul(pA[:, 0:E], ntb[:, :], tri_lt, start=True, stop=True)
            nc.tensor.matmul(pA[0:E, 512:513], tri_le, ntf[:, :], start=True, stop=True).then_inc(start_mm, 1)
            pe.wait_ge(plan, 7)
            nc.tensor.matmul(pB[0:1, 512:512 + NTILE], onesf[0:E, 0:1], over, start=True, stop=True)
            nc.tensor.matmul(pB[0:NTILE, 0:1], over, onesf[0:E, 0:1], start=True, stop=True)
            nc.tensor.matmul(pB[0:NTILE, 1:2], over, ntf[:, :], start=True, stop=True).then_inc(etile_mm, 1)
            pe.wait_ge(plan, 8)
            pe.wait_ge(rows_in, 16)
            nc.tensor.transpose(pA[:, 0:NTILE], tile_rows, CST[0:NTILE, 0, 0:NTILE]).then_inc(rows_tr, 1)

            def rows_T(u):
                for k in range(NC):
                    last = nc.tensor.transpose(pA[:, (u % 2) * 512 + k * P:(u % 2) * 512 + (k + 1) * P],
                                               xg[u % NB][:, k * P:(k + 1) * P], ident)
                last.then_inc(xg_tr, 1)

            def gate_up(t, u, e):
                pe.wait_ge(xgT_ready, t + 1 + AHEAD)
                pe.wait_ge(hid_ready, t + 1)
                for k in range(NC):
                    last = nc.tensor.matmul(pB[:, (u % 2) * 512:(u % 2) * 512 + 2 * INNER],
                                            xgT[u % 2][:, k * P:(k + 1) * P], WGU_E[:, bass.ds(e * NC + k, 1), :],
                                            start=(k == 0), stop=(k == NC - 1))
                last.then_inc(gu_mm, 1)

            def hidden_T(t, u):
                pe.wait_ge(hid_ready, t + 1 + AHEAD)
                nc.tensor.transpose(pY[:, u % 2, 0:P], hid[u % 2], ident).then_inc(hid_tr, 1)

            def down(t, u, e):
                pe.wait_ge(hidT_ready, t + 1 + AHEAD)
                pe.wait_ge(res_ready, t + 1)
                nc.tensor.matmul(pC[:, (u % 2) * 512:(u % 2) * 512 + C], hidT[u % 2],
                                 WDN_E[:, bass.ds(e, 1), :], start=True, stop=True).then_inc(dn_mm, 1)

            def experts_of(t, n):
                _, e = nc.values_load_multi_w_load_instructions(
                    etile[0:1, bass.ds(t, n)], engines=(mybir.EngineType.PE,), min_val=0, max_val=E - 1,
                    skip_runtime_bounds_check_because="the plan clamps them")
                return e

            pe.wait_ge(plan, PLAN_DONE)
            pe.wait_ge(gu_in, 32)
            pe.wait_ge(high_in, 32)
            pe.wait_ge(gathered[0], 16)
            rows_T(0)
            pe.wait_ge(gathered[1], 16)
            rows_T(1)
            e = experts_of(0, 1)
            gate_up(0, 0, e[0])
            pe.wait_ge(gathered[2], 16)
            rows_T(2)

            def round_(i, t0, last, first=False):
                e = experts_of(t0 if first else t0 - 1, NB + (not last) + (not first))
                e = e if first else e[1:] + e[:1]
                for u in range(NB):
                    t = t0 + u
                    if not (last and u >= NB - 1):
                        gate_up(t + 1, u + 1, e[u + 1])
                    if not (last and u >= NB - 3):
                        pe.wait_ge(gathered[(u + 3) % NB], 16 * i + 16 * (1 + (u + 3) // NB))
                        rows_T(u + 3)
                    if not (first and u == 0):
                        down(t - 1, u + 1, e[u - 1])
                    hidden_T(t, u)

            round_(0, 0, False, first=True)
            with pe.Fori(1, NTILE // NB - 1) as i:
                round_(i, NB * i, False)
            round_(NTILE // NB - 1, NTILE - NB, True)
            e = experts_of(NTILE - 1, 1)
            down(NTILE - 1, NB - 1, e[0])

        @block.scalar
        def _(act):
            for s in (xn_ready, q2_ready, h_ready, xnT_ready, tap0, sig_y, v_out, ksq, qsq, nqk_ready, ig_ready,
                      gam_out, og_ready, memsq, d2_ready, osq, d3_ready, oT_out, q2T_ready, y_out, hT_ready,
                      ex_ready):
                act.sem_inc(s.sem, s.per)
            act.sem_inc(xgT_ready, AHEAD)
            act.wait_ge(eps_set, 1)
            act.sem_inc(silu_ready, AHEAD)

            def evict_y(g, twos):
                for w in twos:
                    act.wait_ge(y_mm.sem, y_mm.now(g, w + 1))
                    nc.scalar.activation(y_heads[:, :, 2 * w * NPAIR:2 * (w + 1) * NPAIR],
                                         pY[:, w % 2, 0:Y2].rearrange("p (q m) -> p q m", q=NC * G),
                                         ACT.Copy).then_inc(y_out.sem, 1)

            def normalize(g, dst, i):
                act.wait_ge(factor[i].sem, factor[i].now(g))
                act.nop(nofuse=True)
                for b in range(G):
                    last = nc.scalar.activation(as_tok(dst)[:, b, :], X2[:, bass.ds(G * g + b, 1), :]
                                                .rearrange("p b c -> p (b c)"), ACT.Identity,
                                                scale=rstd[:, i, b:b + 1], bias=nmr[:, i, b:b + 1])
                last.then_inc(normed[i].sem, 1)

            def gate_out(g, mm, src, dst, bias, ready):
                act.wait_ge(mm.sem, mm.now(g))
                for c in range(NC):
                    nc.scalar.activation(as_chan(dst)[:, c, :], as_chan(src)[:, c, :], ACT.Sigmoid,
                                         bias=COLS[:, c, bias:bias + 1]).then_inc(ready.sem, 1)

            def body(i, one, two, three, four):
                g, g2, g3, g4 = i, i - 1, i - 2, i - 3
                if two:
                    act.wait_ge(mem_tr.sem, mem_tr.now(g2))
                    nc.scalar.activation(msq, pM, ACT.Square).then_inc(memsq.sem, 1)
                if four:
                    act.wait_ge(rt.sem, rt.now(g4, 2))
                    nc.scalar.activation(ex[:], lg[:], ACT.Exp).then_inc(ex_ready.sem, 1)
                if one:
                    normalize(g, xn, 0)
                if two:
                    act.wait_ge(memvar.sem, memvar.now(g2))
                    nc.scalar.activation(d2[:], s2[:], ACT.Sqrt, scale=1.0 / HD, bias=eps[:, 0:1]).then_inc(d2_ready.sem, 1)
                if one:
                    act.wait_ge(const_in[0], 16 * 2)
                    act.wait_ge(xn_tr.sem, xn_tr.now(g))
                    act.wait_ge(conv.sem, conv.before(g))
                    act.wait_ge(og_mm.sem, og_mm.before(g))
                    for c in range(NC):
                        nc.scalar.activation(xnT[:, c, :, KC - 1:],
                                             as_chan(pX)[:, c, :].rearrange("p (b t) -> p b t", b=G),
                                             ACT.Copy).then_inc(xnT_ready.sem, 1)
                    for c in range(NC):
                        act.wait_ge(xnT_ready.sem, xnT_ready.now(g, c + 1))
                        nc.scalar.activation(as_chan(y)[:, c, :].rearrange("p (b t) -> p b t", b=G),
                                             xnT[:, c, :, KC - 1:],
                                             ACT.Identity, scale=COLS[:, c, KC - 1:KC],
                                             bias=COLS[:, c, CONVB:CONVB + 1]).then_inc(tap0.sem, 1)
                    act.wait_ge(v_mm.sem, v_mm.now(g))
                    nc.scalar.activation(v, pV, ACT.Copy).then_inc(v_out.sem, 1)
                if two:
                    act.wait_ge(o_step.sem, o_step.now(g2, 6))
                    nc.scalar.activation(msq, o, ACT.Square).then_inc(osq.sem, 1)
                if one:
                    act.wait_ge(k_mm.sem, k_mm.now(g))
                    nc.scalar.activation(ksq_f, pK, ACT.Square).then_inc(ksq.sem, 1)
                    act.wait_ge(q_mm.sem, q_mm.now(g))
                    nc.scalar.activation(qsq_f, pQ, ACT.Square).then_inc(qsq.sem, 1)
                if two:
                    act.wait_ge(ovar.sem, ovar.now(g2))
                    nc.scalar.activation(d3[:], s3[:], ACT.Sqrt, scale=1.0 / HD, bias=eps[:, 0:1]).then_inc(d3_ready.sem, 1)
                if two:
                    if three:
                        act.wait_ge(prods.sem, prods.now(g3))
                    evict_y(g2, (0, 1))
                if one:
                    act.wait_ge(ssmax.sem, ssmax.now(g))
                    nc.scalar.activation(nqk[:], ss[:], ACT.Sqrt).then_inc(nqk_ready.sem, 1)
                    act.wait_ge(conv.sem, conv.now(g))
                    nc.scalar.activation(sg, y, ACT.Sigmoid).then_inc(sig_y.sem, 1)
                if two:
                    evict_y(g2, (2, 3))
                    act.wait_ge(o_tr.sem, o_tr.now(g2))
                    for c in range(NC):
                        nc.scalar.activation(as_chan(yo)[:, c, :], as_chan(pT)[:, c, :], ACT.Identity,
                                             scale=COLS[:, c, GNW:GNW + 1],
                                             bias=COLS[:, c, GNB:GNB + 1]).then_inc(oT_out.sem, 1)
                if one:
                    gate_out(g, ig_mm, pV, ig, BIG, ig_ready)
                    if two:
                        act.wait_ge(mem_ready.sem, mem_ready.now(g2))
                    gate_out(g, gam_mm, pK, gam, BG, gam_out)
                if three:
                    act.wait_ge(hn_stored.sem, hn_stored.before(g3))
                    normalize(g3, hn, 2)
                if two:
                    evict_y(g2, (4, 5))
                if one:
                    if two:
                        act.wait_ge(gated.sem, gated.now(g2))
                    gate_out(g, og_mm, pQ, og, BOG, og_ready)
                if two:
                    normalize(g2, xq, 1)
                if three:
                    act.wait_ge(h_tr.sem, h_tr.now(g3))
                    nc.scalar.activation(hT, pT, ACT.Copy).then_inc(hT_ready.sem, 1)
                if two:
                    evict_y(g2, (6, 7))
                    act.wait_ge(q2_tr.sem, q2_tr.now(g2))
                    nc.scalar.activation(qT, pT, ACT.Copy).then_inc(q2T_ready.sem, 1)

            body(0, True, False, False, False)
            body(1, True, True, False, False)
            body(2, True, True, True, False)
            with act.Fori(3, NG) as i:
                body(i, True, True, True, True)
            body(NG, False, True, True, True)
            body(NG + 1, False, False, True, True)
            body(NG + 2, False, False, False, True)

            def rows_out(t, u):
                act.wait_ge(xg_tr, t + 1)
                act.wait_ge(gu_mm, t + 1)
                nc.scalar.activation(xgT[u % 2], pA[:, (u % 2) * 512:(u % 2) * 512 + C], ACT.Copy)\
                    .then_inc(xgT_ready, 1)

            def gate(t, u):
                act.wait_ge(gu_mm, t + 1 + AHEAD)
                act.wait_ge(hid_ready, t + 1)
                nc.scalar.activation(act_g[u % 2], pB[:, (u % 2) * 512:(u % 2) * 512 + INNER], ACT.Silu)\
                    .then_inc(silu_ready, 1)

            rows_out(0, 0)
            rows_out(1, 1)
            with act.Fori(0, NTILE // NB - 1) as i:
                for u in range(NB):
                    gate(NB * i + u, u)
                    rows_out(NB * i + u + 2, u)
            for u in range(NB):
                gate(NTILE - NB + u, u)
                if u < NB - 2:
                    rows_out(NTILE - NB + u + 2, u)

        @block.vector
        def _(dve):
            for s in (*stats, *aggr, conv, xc_ready, ssum, ssmax, rqk_ready, kv_step, kv_ready,
                      qn_ready, bt_ready, mem_ready, memvar, r2_ready, o_step, ovar, r3_ready, gated, x1_ready,
                      prods, redd, x2_ready, rt):
                dve.sem_inc(s.sem, s.per)
            for s in (hid_ready, hidT_ready, res_ready):
                dve.sem_inc(s, AHEAD)
            nc.vector.memset(eps[:], LN_EPS).then_inc(eps_set, 1)
            nc.vector.memset(prod_f[:, 0:E * NTOK // P], 0.0).then_inc(zero_set, 1)
            nc.vector.memset(cum[:], 0.0).then_inc(plan, 1)
            nc.vector.memset(TRI[:, 1, :], 1.0).then_inc(plan, 1)

            def x2_of(g, b=None):
                return X2[:, bass.ds(G * g, G), :] if b is None else \
                    X2[:, bass.ds(G * g + b, 1), :].rearrange("p b c -> p (b c)")

            def statistics(g, i):
                dve.wait_ge(factor[i].sem, factor[i].before(g))
                dve.nop(nofuse=True)
                for b in range(G):
                    nc.vector.bn_stats(st[:, i, b, :], x2_of(g, b)).then_inc(stats[i].sem, 1)
                dve.wait_ge(stats[i].sem, stats[i].now(g))
                dve.nop(nofuse=True)
                for b in range(G):
                    nc.vector.bn_aggr(mv[:, i, b, :], st[:, i, b, :]).then_inc(aggr[i].sem, 1)

            qTq = qT.rearrange("p (q i) -> p q i", i=XD)

            def products(g, first, last):
                for s in range(first, last):
                    n, off = XD - s, pair_offset(s)
                    nc.vector.tensor_tensor(prod[:, :, s * XD:s * XD + n * (XD + 1) - XD:XD + 1],
                                            yq[:, :, off:off + n], qTq[:, :, 0:n], ALU.mult).then_inc(prods.sem, 1)
                    if s:
                        nc.vector.tensor_tensor(prod[:, :, s:s + n * (XD + 1) - XD:XD + 1],
                                                yq[:, :, off:off + n], qTq[:, :, s:XD], ALU.mult)\
                            .then_inc(prods.sem, 1)

            def sum_products(g, lc):
                n = G * C // NC
                nc.vector.tensor_reduce(cv[:, lc * n:(lc + 1) * n],
                                        prod_f[:, lc * n * XD:(lc + 1) * n * XD].rearrange("p (r i) -> p r i", i=XD),
                                        AX.X, ALU.add).then_inc(redd.sem, 1)

            def bc(f, n):
                return f.rearrange("p (b o) -> p b o", o=1).to_broadcast([P, G, n])

            def small(f):
                return f.rearrange("p (r o) -> p r o", o=1).to_broadcast([P, G * HEADS, HD])

            def body(i, one, two, three, four):
                g, g2, g3, g4 = i, i - 1, i - 2, i - 3
                done = [0]

                def rt_step(ins):
                    done[0] += 1
                    ins.then_inc(rt.sem, 1)

                def rt_wait():
                    dve.wait_ge(rt.sem, rt.now(g4, done[0]))
                    dve.nop(nofuse=True)

                if two:
                    dve.wait_ge(gam_ready.sem, gam_ready.now(g2))
                    dve.wait_ge(bt_ready.sem, bt_ready.now(g2))
                    dve.wait_ge(mem_tr.sem, mem_tr.before(g2))
                    for c in range(NC):
                        nc.vector.tensor_tensor_scan(as_chan(mem)[:, c, :], as_chan(gam)[:, c, :],
                                                     as_chan(bt)[:, c, :], 0.0, ALU.mult, ALU.add)\
                            .then_inc(mem_ready.sem, 1)
                if one:
                    dve.wait_ge(x_in.sem, x_in.now(g))
                    statistics(g, 0)
                if four:
                    dve.wait_ge(lg_mm.sem, lg_mm.now(g4))
                    logits = logits_f.rearrange("p (b e) -> p b e", b=G)
                    dve.nop(nofuse=True)
                    rt_step(nc.vector.tensor_reduce(lmax[:], logits, AX.X, ALU.max))
                if four:
                    rt_wait()
                    rt_step(nc.vector.tensor_tensor(lg[:], logits, bc(lmax[:, :], E), ALU.subtract))
                if three:
                    if not four:
                        dve.wait_ge(rows_zero, 16)
                    dve.wait_ge(q2T_ready.sem, q2T_ready.now(g3))
                    dve.wait_ge(y_out.sem, y_out.now(g3))
                    dve.wait_ge(redd.sem, redd.before(g3))
                    products(g3, 0, 3)
                if two:
                    dve.wait_ge(memsq.sem, memsq.now(g2))
                    nc.vector.tensor_reduce(s2[:], per_head(msq), AX.X, ALU.add).then_inc(memvar.sem, 1)
                if four:
                    dve.wait_ge(ex_ready.sem, ex_ready.now(g4))
                    dve.nop(nofuse=True)
                    rt_step(nc.vector.tensor_reduce(psm[:, 0, :], ex[:], AX.X, ALU.add))
                if two and not three and one:
                    dve.wait_ge(const_in[3], 16 * 3)
                    dve.wait_ge(const_in[4], 16)
                    for h in range(XH):
                        last = nc.vector.scalar_tensor_tensor(TOEP[:, h, 0:P], ident, DSK[:, h:h + 1],
                                                              TOEP[:, h, 0:P], ALU.mult, ALU.add)
                    last.then_inc(toep_ready, 1)
                    nc.vector.tensor_copy(TRI[:, 0, :], IOT[:, 3, :]).then_inc(toep_ready, 1)
                if three:
                    products(g3, 3, 4)
                if four:
                    rt_wait()
                    rt_step(nc.vector.reciprocal(psm[:, 1, :], psm[:, 0, :]))
                if three:
                    products(g3, 4, 5)
                if four:
                    rt_wait()
                    rt_step(nc.vector.tensor_tensor(pr[:], ex[:], bc(psm[:, 1, :], E), ALU.mult))
                if two:
                    dve.wait_ge(d2_ready.sem, d2_ready.now(g2))
                    nc.vector.reciprocal(r2[:], d2[:]).then_inc(r2_ready.sem, 1)
                if four:
                    rt_wait()
                    for b in range(G - 1):
                        nc.vector.max(m8[:, b, :], pr[:, b, :])
                    rt_step(nc.vector.max(m8[:, G - 1, :], pr[:, G - 1, :]))
                if two:
                    dve.wait_ge(r2_ready.sem, r2_ready.now(g2))
                    nc.vector.tensor_tensor(per_head(o), per_head(pM), small(r2[:, :]), ALU.mult)\
                        .then_inc(o_step.sem, 1)
                if four:
                    rt_wait()
                    for b in range(G - 1):
                        nc.vector.max_index(ix[:, b, :], m8[:, b, :], pr[:, b, :])
                    rt_step(nc.vector.max_index(ix[:, G - 1, :], m8[:, G - 1, :], pr[:, G - 1, :]))
                if two:
                    dve.wait_ge(qw_ready.sem, qw_ready.now(g2))
                    dve.wait_ge(o_step.sem, o_step.now(g2, 1))
                    nc.vector.tensor_tensor(o, o, qw, ALU.mult).then_inc(o_step.sem, 1)
                if four:
                    rt_wait()
                    rt_step(nc.vector.tensor_copy(ixf[:], ix[:, :, 0:TOPK]))
                if two:
                    dve.wait_ge(qb_ready.sem, qb_ready.now(g2))
                    dve.wait_ge(o_step.sem, o_step.now(g2, 2))
                    nc.vector.tensor_tensor(o, o, qb, ALU.add).then_inc(o_step.sem, 1)
                if four:
                    oh_g = OH[:, bass.ds(G * g4, G), :]
                    rt_wait()
                    rt_step(nc.vector.tensor_tensor(
                        oh_g.rearrange("p b (k e) -> p (b k) e", k=TOPK),
                        IOT[:, 0:1, 0:E].to_broadcast([P, G * TOPK, E]),
                        ixf[:, :, :].rearrange("p b (k o) -> p (b k) o", o=1).to_broadcast([P, G * TOPK, E]),
                        ALU.is_equal))
                if two:
                    dve.wait_ge(o_step.sem, o_step.now(g2, 3))
                    nc.vector.tensor_reduce(mu[:], per_head(o), AX.X, ALU.add).then_inc(o_step.sem, 1)
                if four:
                    rt_wait()
                    with nc.allow_low_precision("zeros and ones"):
                        rt_step(nc.vector.tensor_reduce(sel[:], oh_g.rearrange("p b (k e) -> p b e k", k=TOPK),
                                                        AX.X, ALU.add))
                    assert done[0] == RT_SEL
                if two:
                    dve.wait_ge(o_step.sem, o_step.now(g2, 4))
                    nc.vector.tensor_scalar(mu[:], mu[:], 1.0 / HD, None, ALU.mult).then_inc(o_step.sem, 1)
                if three:
                    products(g3, 5, 6)
                if two:
                    dve.wait_ge(o_step.sem, o_step.now(g2, 5))
                    nc.vector.tensor_tensor(per_head(o), per_head(o), small(mu[:, :]), ALU.subtract)\
                        .then_inc(o_step.sem, 1)
                if one:
                    for j in range(1, KC):
                        for c in range(NC):
                            if j == 1:
                                dve.wait_ge(tap0.sem, tap0.now(g, c + 1))
                            else:
                                dve.wait_ge(conv.sem, conv.now(g, 2 * (j - 1) - 1 + c))
                            yc = as_chan(y)[:, c, :].rearrange("p (b t) -> p b t", b=G)
                            nc.vector.scalar_tensor_tensor(yc, xnT[:, c, :, KC - 1 - j:KC - 1 - j + T],
                                                           COLS[:, c, KC - 1 - j:KC - j], yc, ALU.mult, ALU.add)\
                                .then_inc(conv.sem, 1)
                if two:
                    dve.wait_ge(osq.sem, osq.now(g2))
                    nc.vector.tensor_reduce(s3[:], per_head(msq), AX.X, ALU.add).then_inc(ovar.sem, 1)
                if three:
                    products(g3, 6, XD)
                if four:
                    rt_wait()
                    with nc.allow_low_precision("counts up to 16"):
                        nc.vector.tensor_reduce(selg[:], sel[:, :, :].rearrange("p b e -> p e b"), AX.X, ALU.add)
                    rt_step(nc.vector.tensor_reduce(wsum[:, 0, :], m8[:, :, 0:TOPK], AX.X, ALU.add))
                if one:
                    dve.wait_ge(ksq.sem, ksq.now(g))
                    nc.vector.tensor_reduce(ss[:, G * HEADS:], per_head(ksq_f), AX.X, ALU.add)\
                        .then_inc(ssum.sem, 1)
                    dve.wait_ge(qsq.sem, qsq.now(g))
                    nc.vector.tensor_reduce(ss[:, 0:G * HEADS], per_head(qsq_f), AX.X, ALU.add)\
                        .then_inc(ssum.sem, 1)
                    dve.wait_ge(ssum.sem, ssum.now(g))
                    nc.vector.tensor_scalar(ss[:], ss[:], 1e-24, None, ALU.max).then_inc(ssmax.sem, 1)
                if four:
                    rt_wait()
                    rt_step(nc.vector.reciprocal(wsum[:, 1, :], wsum[:, 0, :]))
                if three:
                    dve.wait_ge(prods.sem, prods.now(g3))
                    sum_products(g3, 0)
                if two:
                    dve.wait_ge(d3_ready.sem, d3_ready.now(g2))
                    nc.vector.reciprocal(r3[:], d3[:]).then_inc(r3_ready.sem, 1)
                    dve.wait_ge(r3_ready.sem, r3_ready.now(g2))
                    nc.vector.tensor_tensor(per_head(o), per_head(o), small(r3[:, :]), ALU.mult)\
                        .then_inc(o_step.sem, 1)
                if four:
                    rt_wait()
                    nc.vector.tensor_tensor(WT[:, bass.ds(G * g4, G), :], m8[:, :, 0:TOPK],
                                            bc(wsum[:, 1, :], TOPK), ALU.mult)
                    dve.wait_ge(rank_mm.sem, rank_mm.now(g4))
                    rt_step(nc.vector.tensor_tensor(cum[:, :], cum[:, :], selg[:, :], ALU.add))
                    assert done[0] == RT_CUM
                if one:
                    dve.wait_ge(sig_y.sem, sig_y.now(g))
                    nc.vector.tensor_tensor(y, y, sg, ALU.mult).then_inc(xc_ready.sem, 1)
                    dve.wait_ge(v_out.sem, v_out.now(g))
                    nc.vector.tensor_tensor(kv, pK, v, ALU.mult).then_inc(kv_step.sem, 1)
                if four:
                    rt_wait()
                    rt_step(nc.vector.tensor_tensor(
                        tmp_oh[:, :].rearrange("p (b k e) -> p b k e", b=G, k=TOPK),
                        ranks.rearrange("p (b o e) -> p b o e", b=G, o=1).to_broadcast([P, G, TOPK, E]),
                        oh_g.rearrange("p b (k e) -> p b k e", k=TOPK), ALU.mult))
                if three:
                    sum_products(g3, 1)
                if two:
                    dve.wait_ge(oT_out.sem, oT_out.now(g2))
                    nc.vector.tensor_tensor(yo, yo, og, ALU.mult).then_inc(gated.sem, 1)
                if four:
                    rt_wait()
                    rt_step(nc.vector.tensor_reduce(posr[:, bass.ds(G * g4, G), :],
                                                    tmp_oh[:, :].rearrange("p (b k e) -> p b k e", b=G, k=TOPK),
                                                    AX.X, ALU.add))
                if one:
                    dve.wait_ge(nqk_ready.sem, nqk_ready.now(g))
                    nc.vector.reciprocal(rqk[:], nqk[:]).then_inc(rqk_ready.sem, 1)
                    dve.wait_ge(kv_step.sem, kv_step.now(g))
                    dve.wait_ge(rqk_ready.sem, rqk_ready.now(g))
                    nc.vector.tensor_tensor(per_head(kv), per_head(kv), small(rqk[:, G * HEADS:]), ALU.mult)\
                        .then_inc(kv_ready.sem, 1)
                    dve.wait_ge(qb_ready.sem, qb_ready.before(g))
                    nc.vector.tensor_tensor(per_head(qn), per_head(pQ), small(rqk[:, 0:G * HEADS]), ALU.mult)\
                        .then_inc(qn_ready.sem, 1)
                if four:
                    rt_wait()
                    rt_step(nc.vector.scalar_tensor_tensor(place_f[:], ixf[:], float(NTOK),
                                                           posr[:, bass.ds(G * g4, G), :], ALU.mult, ALU.add))
                if three:
                    dve.wait_ge(y2_tr.sem, y2_tr.now(g3))
                    nc.vector.tensor_tensor(x2_of(g3), as_tok(pT), x2_of(g3), ALU.add).then_inc(x2_ready.sem, 1)
                if four:
                    rt_wait()
                    dve.wait_ge(numbered.sem, numbered.before(g4))
                    dve.nop(nofuse=True)
                    nc.vector.tensor_copy(number[:], IOT[:, 1, bass.ds(G * TOPK * g4, G * TOPK)])
                    rt_step(nc.vector.tensor_copy(place[:], place_f[:, :, :].rearrange("p b k -> p (b k)")))
                    assert done[0] == RT_STEPS
                if three:
                    dve.wait_ge(x2_ready.sem, x2_ready.now(g3))
                    statistics(g3, 2)
                if two:
                    dve.wait_ge(wo_mm.sem, wo_mm.now(g2))
                    nc.vector.tensor_tensor(x2_of(g2), as_tok(pM), x2_of(g2), ALU.add).then_inc(x1_ready.sem, 1)
                    dve.wait_ge(x1_ready.sem, x1_ready.now(g2))
                    statistics(g2, 1)
                if one:
                    dve.wait_ge(kv_tr.sem, kv_tr.now(g))
                    dve.wait_ge(ig_ready.sem, ig_ready.now(g))
                    dve.wait_ge(mem_ready.sem, mem_ready.before(g))
                    nc.vector.tensor_tensor(bt, pX, ig, ALU.mult).then_inc(bt_ready.sem, 1)

            body(0, True, False, False, False)
            body(1, True, True, False, False)
            body(2, True, True, True, False)
            with dve.Fori(3, NG) as i:
                body(i, True, True, True, True)
            body(NG, False, True, True, True)
            body(NG + 1, False, False, True, True)
            body(NG + 2, False, False, False, True)

            def step(ins, value):
                ins.then_inc(plan, 1)
                dve.wait_ge(plan, value)

            dve.wait_ge(cnt_mm, 1)
            step(nc.vector.tensor_scalar(nti[:, 0:1], pB[0:E, 0:1], float(P - 1), None, ALU.add), 3)
            step(nc.vector.tensor_scalar(nti[:, 1:2], nti[:, 0:1], 7, None, ALU.arith_shift_right), 4)
            step(nc.vector.tensor_copy(ntf[:], nti[:, 1:2]), 5)
            step(nc.vector.tensor_copy(ntb[:], ntf[:, 0:1].to_broadcast([E, P])), 6)
            dve.wait_ge(start_mm, 1)
            step(nc.vector.tensor_scalar(over, IOT[0:E, 0, 0:NTILE], pA[0:E, 512:513], None, ALU.is_ge), 7)
            step(nc.vector.tensor_copy(start[:], pA[:, 0:E]), 8)
            dve.wait_ge(etile_mm, 1)
            step(nc.vector.scalar_tensor_tensor(first_f[:, 0:1], pB[0:NTILE, 0:1], float(NTOK // P), part,
                                                ALU.mult, ALU.add), 9)
            step(nc.vector.tensor_tensor(first_f[:, 1:2], first_f[:, 0:1], pB[0:NTILE, 1:2], ALU.subtract), 10)
            step(nc.vector.tensor_scalar(first[:], first_f[:, 1:2], float(E * NTOK // P - 1), None, ALU.min), 11)
            step(nc.vector.tensor_scalar(etile[:, 0:NTILE], pB[0:1, 512:512 + NTILE], float(E - 1), None,
                                         ALU.min), 12)
            step(nc.vector.tensor_tensor(oh_prod, OH[:, :, :].rearrange("p b (k e) -> p (b k) e", k=TOPK),
                                         start[:, :].rearrange("p (o e) -> p o e", o=1)
                                         .to_broadcast([P, B * TOPK, E]), ALU.mult), 13)
            step(nc.vector.tensor_reduce(starts[:], oh_prod, AX.X, ALU.add), 14)
            step(nc.vector.scalar_tensor_tensor(slot_f, starts[:], float(P),
                                                posr[:, :, :].rearrange("p b k -> p (b k)"),
                                                ALU.mult, ALU.add), 15)
            step(nc.vector.tensor_copy(SLOT[:], slot_f), 16)
            dve.wait_ge(rows_tr, 1)
            step(nc.vector.tensor_scalar(row1, pA[:, 0:NTILE], -1.0, 0.0, ALU.add, ALU.max), 17)
            step(nc.vector.tensor_copy(GIDX, row1), 18)
            step(nc.vector.tensor_scalar(GIDX, GIDX, 2, None, ALU.arith_shift_right), PLAN_DONE)

            def gather_column(t, u):
                nc.vector.tensor_copy(gcol[:, u:u + 1], GIDX[:, bass.ds(t, 1)].bitcast(U32)).then_inc(gcol_ready, 1)

            for u in range(NB):
                gather_column(u, u)

            def result_out(t, u, i):
                if i is not None:
                    dve.wait_ge(z_stored[u % NR], 16 * (NB // NR) * i + 16 * (u // NR))
                dve.wait_ge(dn_mm, t + 1 + AHEAD)
                nc.vector.tensor_copy(res[u % NR], pC[:, (u % 2) * 512:(u % 2) * 512 + C]).then_inc(res_ready, 1)

            def hidden(t, u, i, first=False):
                dve.wait_ge(silu_ready, t + 1 + AHEAD)
                dve.wait_ge(hid_tr, t + 1)
                nc.vector.tensor_tensor(hid[u % 2], act_g[u % 2],
                                        pB[:, (u % 2) * 512 + INNER:(u % 2) * 512 + 2 * INNER], ALU.mult)\
                    .then_inc(hid_ready, 1)
                if not first:
                    result_out(t - 1, (u - 1) % NB, i if u or i is None else i - 1)
                dve.wait_ge(hid_tr, t + 1 + AHEAD)
                dve.wait_ge(dn_mm, t + 1)
                nc.vector.tensor_copy(hidT[u % 2], pY[:, u % 2, 0:P]).then_inc(hidT_ready, 1)

            for u in range(NB):
                hidden(u, u, 0 if u > NR else None, first=(u == 0))
                dve.wait_ge(gathered[u], 16)
                gather_column(u + NB, u)
            with dve.Fori(1, NTILE // NB - 1) as i:
                for u in range(NB):
                    hidden(NB * i + u, u, i)
                    dve.wait_ge(gathered[u], 16 * i + 16)
                    gather_column(NB * i + u + NB, u)
            last = NTILE // NB - 1
            for u in range(NB):
                hidden(NTILE - NB + u, u, last)
            result_out(NTILE - 1, NB - 1, last)

            for n in range(B):
                for k in range(TOPK):
                    q = TOPK * n + k
                    dve.wait_ge(z_in[q % NZ], 16 * (q // NZ + 1))
                    if k:
                        dve.wait_ge(comb, q)
                    nc.vector.scalar_tensor_tensor(X2[:, n, :], z_buf[q % NZ],
                                                   WT[:, n, k:k + 1], X2[:, n, :], ALU.mult, ALU.add)\
                        .then_inc(comb, 1)


_OUTS = [((B, T, C), "float32")]


def kernel(**inputs):
    import numpy as np
    import concourse.bacc as bacc
    from concourse import mybir as mb
    from concourse.bass_utils import run_bass_kernel_spmd

    a = {k: np.asarray(v) for k, v in inputs.items()}
    f32 = np.float32

    def chunked(w):
        return np.ascontiguousarray(w.reshape(NC, P, -1).transpose(1, 0, 2))

    wq, wk, wv, wo, wig, wog = (a[f"L0_attn_{n}"].T for n in ("Wq", "Wk", "Wv", "Wo", "Wig", "Wog"))
    wg = np.repeat(a["L0_attn_Wg"], HD, axis=0).T
    cols = np.stack([*a["L0_attn_conv_w"].T, a["L0_attn_conv_b"], a["L0_attn_b_ig"],
                     np.repeat(a["L0_attn_b_g"], HD), a["L0_attn_b_og"], a["L0_attn_gn_w"],
                     a["L0_attn_gn_b"]], axis=1)
    rows = np.broadcast_to(np.stack([a["L0_attn_mn_w"], a["L0_attn_mn_b"]]), (P, 2, C))
    padded = np.zeros((XH, P + C), f32)
    padded[:, P:] = a["L0_xattn_ssm_kernel"]
    toep = padded[:, P + np.arange(C)[None, :] - np.arange(P)[:, None]].transpose(1, 0, 2)
    ctx_t = a["ctx_2048"].reshape(NG, G, T, NC, P).transpose(0, 4, 3, 1, 2).reshape(NG, P, NC * G * T)
    w_gu = np.concatenate([a["L0_ffn_w_gate"], a["L0_ffn_w_up"]], axis=1)
    w_gu = w_gu.reshape(E, 2 * INNER, NC, P).transpose(3, 0, 2, 1).reshape(P, E * GUW)
    w_dn = a["L0_ffn_w_down"].transpose(2, 0, 1).reshape(P, E * C)
    eye = np.eye(P, dtype=f32)
    head = np.kron(np.eye(P // HD), np.ones((HD, HD))).astype(f32)
    consts = np.stack([eye, eye - head / f32(HD), np.ones((P, P), f32)], axis=1)
    iotas = np.zeros((P, 4, P), f32)
    iotas[:, 0] = np.arange(P)
    n, k = np.divmod(np.arange(B * TOPK), TOPK)
    iotas[:, 1, :B * TOPK] = (n * P)[None] * TOPK + np.arange(P)[:, None] * TOPK + k[None] + 1
    before = np.arange(E)[:, None] < np.arange(E)[None, :]
    iotas[:E, 2, :E] = before
    iotas[:E, 2, E:2 * E] = before | np.eye(E, dtype=bool)
    iotas[:, 2, 2 * E] = np.arange(P)
    iotas[:, 3] = np.arange(P)[:, None] < np.arange(P)[None, :]

    data = {
        "x": a["x"], "ctx_t": ctx_t, "w_qk": chunked(np.concatenate([wq, wk], axis=1)), "w_v": chunked(wv),
        "w_ig": chunked(wig), "w_g": chunked(wg), "w_og": chunked(wog), "w_o": chunked(wo),
        "w_rt": chunked(a["L0_ffn_router_w"].T), "cols": chunked(cols), "rows": rows, "toep": toep,
        "dskip": np.broadcast_to(a["L0_xattn_D"], (P, XH)), "w_gu": w_gu, "w_dn": w_dn,
        "consts": consts, "iotas": iotas,
    }
    nc = bacc.Bacc("TRN2", target_bir_lowering=False, num_devices=1)
    arrays, args = {}, []
    for name, v in data.items():
        v = np.ascontiguousarray(v)
        arrays[f"in_{name}"] = v
        args.append(nc.dram_tensor(f"in_{name}", v.shape, mb.dt.from_np(v.dtype), kind="ExternalInput").ap())
    args.append(nc.dram_tensor("out_0", _OUTS[0][0], mb.dt.from_np(np.dtype("float32")), kind="ExternalOutput").ap())
    program(nc, *args)
    r = run_bass_kernel_spmd(nc, [arrays], core_ids=[0])
    return r.results[0]["out_0"]
```
